# Optimizing a Trainium2 kernel written in Bass

```python
import numpy as np
import jax
import jax.numpy as jnp

def _softmax(x, axis=-1):
    return jax.nn.softmax(x, axis=axis)

def _gelu(x):
    return jax.nn.gelu(x, approximate=True)

def _silu(x):
    return jax.nn.silu(x)

def _sigmoid(x):
    return jax.nn.sigmoid(x)

def _layernorm(x, axis=-1, eps=1e-05):
    m = jnp.mean(x, axis=axis, keepdims=True)
    v = jnp.var(x, axis=axis, keepdims=True)
    return (x - m) / jnp.sqrt(v + eps)

def _scatter_add(tgt, idx, src, axis=0):
    return tgt.at[idx].add(src)

def _segment_sum(src, seg, n):
    return jax.ops.segment_sum(src, seg, n)
kernel_name = 'mk_gnn_resnorm_d2_gnn_r8_10da83'

def setup_inputs(seed: int=0):
    np.random.seed(seed)
    _w = jnp.asarray

    def _rec_inputs():
        import jax
        import jax.numpy as jnp
        _gk = jax.random.key(seed)
        x = -0.0002117 + 1 * jax.random.normal(jax.random.fold_in(_gk, 1), (6250, 256), jnp.float32)
        _s = jax.random.randint(jax.random.fold_in(_gk, 2), (100000,), 0, 6250, jnp.int32)
        _d = jax.random.randint(jax.random.fold_in(_gk, 3), (100000,), 0, 6250, jnp.int32)
        _loop = jnp.arange(6250, dtype=jnp.int32)
        src = jnp.concatenate([_s, _d, _loop])
        dst = jnp.concatenate([_d, _s, _loop])
        _o = jnp.argsort(dst, stable=True)
        src = src[_o]
        dst = dst[_o]
        edge_attr_64 = 0.000279952 + 1.00013 * jax.random.normal(jax.random.fold_in(_gk, 12), (206250, 64), jnp.float32)
        edge_weight = jax.random.uniform(jax.random.fold_in(_gk, 14), (206250,), jnp.float32, 0.0, 0.999998)
        edge_weight_n2 = jax.random.uniform(jax.random.fold_in(_gk, 15), (206250,), jnp.float32, 0.0, 0.999998)
        return (x, src, dst, edge_attr_64, edge_weight, edge_weight_n2)
    x, src, dst, edge_attr_64, edge_weight, edge_weight_n2 = _rec_inputs()

    def _L0_gnn_setup():
        import jax, jax.numpy as jnp
        import numpy as np
        N = 12500
        E = 40000
        CIN = 256
        EDIM = 64
        EEMB = 256
        H = 1024
        LN_EPS = 1e-05

        def _ln(x, g, b):
            m = jnp.mean(x, axis=-1, keepdims=True)
            v = jnp.var(x, axis=-1, keepdims=True)
            return (x - m) * jax.lax.rsqrt(v + LN_EPS) * g + b
        key = jax.random.key(seed)
        ks = jax.random.split(key, 16)

        def w(k, i, o):
            return (jax.random.normal(k, (i, o), jnp.float32) / np.sqrt(i)).astype(jnp.float32)
        return {'x': jax.random.normal(ks[0], (N, CIN), jnp.float32), 'edge_index': jax.random.randint(ks[1], (2, E), 0, N, dtype=jnp.int64), 'edge_attr': jax.random.normal(ks[2], (E, EDIM), jnp.float32), 'eps': jnp.float32(0.0), 'ee_w1': w(ks[3], EDIM, EEMB), 'ee_b1': jnp.zeros((EEMB,), jnp.float32), 'ee_w2': w(ks[4], EEMB, CIN), 'ee_b2': jnp.zeros((CIN,), jnp.float32), 'w1': w(ks[5], CIN, H), 'b1': jnp.zeros((H,), jnp.float32), 'g1': jnp.ones((H,), jnp.float32), 'be1': jnp.zeros((H,), jnp.float32), 'w2': w(ks[6], H, H), 'b2': jnp.zeros((H,), jnp.float32), 'g2': jnp.ones((H,), jnp.float32), 'be2': jnp.zeros((H,), jnp.float32), 'w3': w(ks[7], H, CIN), 'b3': jnp.zeros((CIN,), jnp.float32), 'bn_g': jnp.ones((CIN,), jnp.float32), 'bn_b': jnp.zeros((CIN,), jnp.float32)}
    _L0_gnn_all = _L0_gnn_setup()
    _L0_gnn_in = {k: v for k, v in _L0_gnn_all.items() if k in ('eps', 'ee_w1', 'ee_b1', 'ee_w2', 'ee_b2', 'w1', 'b1', 'g1', 'be1', 'w2', 'b2', 'g2', 'be2', 'w3', 'b3', 'bn_g', 'bn_b')}
    del _L0_gnn_all

    def _L1_gnn_setup():
        import jax, jax.numpy as jnp
        import numpy as np
        N_NODES = 12500
        N_EDGES = 100000
        DIM = 256
        EPS = 1e-05
        key = jax.random.key(seed)
        ks = jax.random.split(key, 12)
        H = DIM
        s = 1.0 / np.sqrt(H)
        s2 = 1.0 / np.sqrt(2 * H)
        return {'feat': jax.random.normal(ks[0], (N_NODES, DIM), dtype=jnp.float32), 'src': jax.random.randint(ks[1], (N_EDGES,), 0, N_NODES, dtype=jnp.int32), 'dst': jax.random.randint(ks[2], (N_EDGES,), 0, N_NODES, dtype=jnp.int32), 'iw': jax.random.uniform(ks[3], (N_EDGES,), dtype=jnp.float32), 'ow': jax.random.uniform(ks[4], (N_EDGES,), dtype=jnp.float32), 'gamma': jnp.ones((DIM,), jnp.float32), 'beta': jnp.zeros((DIM,), jnp.float32), 'W_in': jax.random.uniform(ks[5], (H, H), jnp.float32, -s, s), 'b_in': jax.random.uniform(ks[6], (H,), jnp.float32, -s, s), 'W_out': jax.random.uniform(ks[7], (H, H), jnp.float32, -s, s), 'b_out': jax.random.uniform(ks[8], (H,), jnp.float32, -s, s), 'W_x2i': jax.random.uniform(ks[9], (2 * H, 2 * H), jnp.float32, -s2, s2), 'b_x2i': jax.random.uniform(ks[10], (2 * H,), jnp.float32, -s2, s2), 'W_h2h': jax.random.uniform(ks[11], (H, 2 * H), jnp.float32, -s, s)}
    _L1_gnn_all = _L1_gnn_setup()
    _L1_gnn_in = {k: v for k, v in _L1_gnn_all.items() if k in ('gamma', 'beta', 'W_in', 'b_in', 'W_out', 'b_out', 'W_x2i', 'b_x2i', 'W_h2h')}
    del _L1_gnn_all
    return {'x': x, 'src': src, 'dst': dst, 'edge_attr_64': edge_attr_64, 'edge_weight': edge_weight, 'edge_weight_n2': edge_weight_n2, 'L0_gnn_eps': _L0_gnn_in['eps'], 'L0_gnn_ee_w1': _L0_gnn_in['ee_w1'], 'L0_gnn_ee_b1': _L0_gnn_in['ee_b1'], 'L0_gnn_ee_w2': _L0_gnn_in['ee_w2'], 'L0_gnn_ee_b2': _L0_gnn_in['ee_b2'], 'L0_gnn_w1': _L0_gnn_in['w1'], 'L0_gnn_b1': _L0_gnn_in['b1'], 'L0_gnn_g1': _L0_gnn_in['g1'], 'L0_gnn_be1': _L0_gnn_in['be1'], 'L0_gnn_w2': _L0_gnn_in['w2'], 'L0_gnn_b2': _L0_gnn_in['b2'], 'L0_gnn_g2': _L0_gnn_in['g2'], 'L0_gnn_be2': _L0_gnn_in['be2'], 'L0_gnn_w3': _L0_gnn_in['w3'], 'L0_gnn_b3': _L0_gnn_in['b3'], 'L0_gnn_bn_g': _L0_gnn_in['bn_g'], 'L0_gnn_bn_b': _L0_gnn_in['bn_b'], 'L1_gnn_gamma': _L1_gnn_in['gamma'], 'L1_gnn_beta': _L1_gnn_in['beta'], 'L1_gnn_W_in': _L1_gnn_in['W_in'], 'L1_gnn_b_in': _L1_gnn_in['b_in'], 'L1_gnn_W_out': _L1_gnn_in['W_out'], 'L1_gnn_b_out': _L1_gnn_in['b_out'], 'L1_gnn_W_x2i': _L1_gnn_in['W_x2i'], 'L1_gnn_b_x2i': _L1_gnn_in['b_x2i'], 'L1_gnn_W_h2h': _L1_gnn_in['W_h2h']}

def reference(x, src, dst, edge_attr_64, edge_weight, edge_weight_n2, L0_gnn_eps, L0_gnn_ee_w1, L0_gnn_ee_b1, L0_gnn_ee_w2, L0_gnn_ee_b2, L0_gnn_w1, L0_gnn_b1, L0_gnn_g1, L0_gnn_be1, L0_gnn_w2, L0_gnn_b2, L0_gnn_g2, L0_gnn_be2, L0_gnn_w3, L0_gnn_b3, L0_gnn_bn_g, L0_gnn_bn_b, L1_gnn_gamma, L1_gnn_beta, L1_gnn_W_in, L1_gnn_b_in, L1_gnn_W_out, L1_gnn_b_out, L1_gnn_W_x2i, L1_gnn_b_x2i, L1_gnn_W_h2h):
    import jax
    import jax.numpy as jnp

    def _L0_gnn_ref(x, edge_index, edge_attr, eps, ee_w1, ee_b1, ee_w2, ee_b2, w1, b1, g1, be1, w2, b2, g2, be2, w3, b3, bn_g, bn_b):
        import jax, jax.numpy as jnp
        import numpy as np
        N = 12500
        E = 40000
        CIN = 256
        EDIM = 64
        EEMB = 256
        H = 1024
        LN_EPS = 1e-05

        def _ln(x, g, b):
            m = jnp.mean(x, axis=-1, keepdims=True)
            v = jnp.var(x, axis=-1, keepdims=True)
            return (x - m) * jax.lax.rsqrt(v + LN_EPS) * g + b
        n = x.shape[0]
        sl = jnp.arange(n, dtype=edge_index.dtype)
        ei = jnp.concatenate([edge_index, jnp.stack([sl, sl], axis=0)], axis=1)
        ea = jnp.concatenate([edge_attr, jnp.zeros((n, edge_attr.shape[1]), edge_attr.dtype)], axis=0)
        src, dst = (ei[0], ei[1])
        e = jax.nn.relu(ea @ ee_w1 + ee_b1) @ ee_w2 + ee_b2
        msg = x[src] + e
        agg = jax.ops.segment_sum(msg, dst, num_segments=n)
        h = (1.0 + eps) * x + agg
        h = jax.nn.relu(_ln(h @ w1 + b1, g1, be1))
        h = jax.nn.relu(_ln(h @ w2 + b2, g2, be2))
        y = h @ w3 + b3
        out = x + y
        out = _ln(out, bn_g, bn_b)
        return jax.nn.relu(out)

    def _L1_gnn_ref(feat, src, dst, iw, ow, gamma, beta, W_in, b_in, W_out, b_out, W_x2i, b_x2i, W_h2h):
        import jax, jax.numpy as jnp
        import numpy as np
        N_NODES = 12500
        N_EDGES = 100000
        DIM = 256
        EPS = 1e-05
        N = feat.shape[0]
        num_steps = 1
        mean = jnp.mean(feat, axis=0)
        var = jnp.var(feat, axis=0)
        h = (feat - mean) * jax.lax.rsqrt(var + EPS) * gamma + beta
        for _ in range(num_steps):
            feat_in = h @ W_in + b_in
            feat_out = h @ W_out + b_out
            a_in = jax.ops.segment_sum(feat_in[src] * iw[:, None], dst, num_segments=N)
            a_out = jax.ops.segment_sum(feat_out[dst] * ow[:, None], src, num_segments=N)
            a = jnp.concatenate((a_in, a_out), axis=1)
            xi = a @ W_x2i + b_x2i
            hh = h @ W_h2h
            i_i, i_n = jnp.split(xi, 2, axis=1)
            h_i, h_n = jnp.split(hh, 2, axis=1)
            input_gate = jax.nn.sigmoid(i_i + h_i)
            new_gate = jnp.tanh(i_n + h_n)
            h = new_gate + input_gate * (h - new_gate)
        return h
    edge_index = jnp.stack([src, dst])
    x = _layernorm(x + _L0_gnn_ref(x, edge_index, edge_attr_64, L0_gnn_eps, L0_gnn_ee_w1, L0_gnn_ee_b1, L0_gnn_ee_w2, L0_gnn_ee_b2, L0_gnn_w1, L0_gnn_b1, L0_gnn_g1, L0_gnn_be1, L0_gnn_w2, L0_gnn_b2, L0_gnn_g2, L0_gnn_be2, L0_gnn_w3, L0_gnn_b3, L0_gnn_bn_g, L0_gnn_bn_b), axis=-1)
    x = _layernorm(x + _L1_gnn_ref(x, src, dst, edge_weight, edge_weight_n2, L1_gnn_gamma, L1_gnn_beta, L1_gnn_W_in, L1_gnn_b_in, L1_gnn_W_out, L1_gnn_b_out, L1_gnn_W_x2i, L1_gnn_b_x2i, L1_gnn_W_h2h), axis=-1)
    return x

_drawn_inputs = setup_inputs


def setup_inputs(seed=0):
    import zlib

    import numpy as np

    out = dict(_drawn_inputs(seed))
    spreads = {'L0_gnn_ee_b1': (0.0, 0.296),
     'L0_gnn_ee_b2': (0.0, 0.1),
     'L0_gnn_b1': (0.0, 0.8),
     'L0_gnn_g1': (1.0, 0.2),
     'L0_gnn_be1': (0.0, 0.366),
     'L0_gnn_b2': (0.0, 0.274),
     'L0_gnn_g2': (1.0, 0.2),
     'L0_gnn_be2': (0.0, 0.372),
     'L0_gnn_b3': (0.0, 0.316),
     'L0_gnn_bn_g': (1.0, 0.2),
     'L0_gnn_bn_b': (0.0, 0.1),
     'L1_gnn_gamma': (1.0, 0.2),
     'L1_gnn_beta': (0.0, 0.1)}
    factors = {'L1_gnn_b_x2i': 8.0}
    for name, (base, spread) in spreads.items():
        noise = np.random.default_rng([zlib.crc32(name.encode()), seed]).standard_normal(out[name].shape)
        drawn = base * np.exp(spread * noise) if base else spread * noise
        out[name] = jnp.asarray(drawn.astype(out[name].dtype))
    for name, factor in factors.items():
        out[name] = (out[name] * factor).astype(out[name].dtype)
    return out
```

```python
from contextlib import ExitStack, contextmanager

import concourse.bass as bass
from concourse import mybir

P = 128
ALU = mybir.AluOpType
ACT = mybir.ActivationFunctionType
F32 = mybir.dt.float32
I32 = mybir.dt.int32
AX = mybir.AxisListType.X

NODES = 6250
EDGES = 206250
C = 256
EC = 64
H = 1024
CC = C // P
HC = H // P
NB = -(-NODES // P)
NP = NB * P
LAST = NODES - (NB - 1) * P
T = 4
GE = T * P
U = 4
NG = -(-EDGES // (GE * U)) * U
NT = NG * T
EP = NG * GE
SG = NG + NB - 1
SG = -(-SG // U) * U
STORE = 7
PAD_DMAS = 16
ST = 8
LN_EPS = 1e-5
BUCKET_SHIFT = 7
GROUP_SHIFT = 9
assert 1 << BUCKET_SHIFT == P and 1 << GROUP_SHIFT == GE


def gnn_kernel(nc, a, out):
    with ExitStack() as whole:
        def scratch(name, shape, dt):
            return nc.dram_tensor(name, shape, dt, kind="Internal").ap()

        dram = {
            "x_plus_b2": scratch("x_plus_b2", (NP, C), F32),
            "edge_slot": scratch("edge_slot", (P, NT), I32),
            "edge_record": scratch("edge_record", (P, NT * 4), F32),
            "sorted_record": scratch("sorted_record", (SG * GE, 4), F32),
            "dst_windows": scratch("dst_windows", (NG, 2), I32),
            "sorted_bucket": scratch("sorted_bucket", (P, U), I32),
            "feat_in": scratch("feat_in", (NP, C), F32),
            "feat_out": scratch("feat_out", (NP, C), F32),
            "x1": scratch("x1", (P, NB * C), F32),
            "hT": scratch("hT", (P, NB * C), F32),
        }
        sb = lambda name, shape, dt=F32: whole.enter_context(nc.sbuf_tensor(name, shape, dt))
        t = {
            "acc": sb("acc", [P, NB, 2 * C]),
            "ident": sb("ident", [P, P]),
            "dstf": sb("dstf", [P, NT + T]),
            "windows": sb("windows", [1, 2 * (NG + 1)], I32),
            "sorted_bucket": sb("sorted_bucket_sb", [1, SG + U], I32),
        }
        prepare(nc, a, dram, t)
        sum_over_dst(nc, a, dram, t, first=True)
        node_network(nc, a, dram, t)
        make_tables(nc, a, dram, t)
        sum_over_dst(nc, a, dram, t, first=False)
        sum_over_src(nc, a, dram, t)
        gates(nc, a, dram, t, out)


class Chain:

    def __init__(self, engine, sem):
        self.engine, self.sem, self.before, self.steps = engine, sem, 0, 0

    def then(self, ins):
        self.steps += 1
        ins.then_inc(self.sem, 1)
        self.engine.wait_ge(self.sem, self.before + self.steps)

    @contextmanager
    def loop(self, engine, start, end, per):
        began = self.steps
        with engine.Fori(start, end) as i:
            self.before = (i - start) * per
            yield i
        assert self.steps - began == per, self.steps - began
        self.before, self.steps = 0, began + per * (end - start)


class Names:

    def __init__(self, nc, stage, stack):
        self.nc, self.stage, self.stack = nc, stage, stack

    def sb(self, name, shape, dt=F32):
        return self.stack.enter_context(self.nc.sbuf_tensor(f"{self.stage}_{name}", shape, dt))

    def ps(self, name, shape, dt=F32):
        return self.stack.enter_context(self.nc.psum_tensor(f"{self.stage}_{name}", shape, dt))

    def sem(self, name):
        return self.stack.enter_context(self.nc.semaphore(f"{self.stage}_{name}"))


def row(v):
    return v.partition_broadcast(P)


def prepare(nc, a, dram, t):
    acc, dstf, ident = t["acc"], t["dstf"], t["ident"]
    with ExitStack() as s:
        n = Names(nc, "prep", s)
        srci = n.sb("srci", [P, NT], I32)
        srcblk = n.sb("srcblk", [P, NT])
        mask = n.sb("mask", [P, NT])
        scan = n.sb("scan", [P, NT])
        slot = n.sb("slot", [P, NT])
        dsti = scan[:].bitcast(I32)
        dstblk, ow = mask, slot
        rec = n.sb("rec", [P, NT, 4])
        b1 = n.sb("b1", [P, C])
        b2 = n.sb("b2", [P, C])
        eps = n.sb("eps", [P, 1])
        lohi = n.sb("lohi", [P, 2, NG])
        ones = n.sb("ones", [P, P])
        before = n.sb("before", [P, P])
        count = n.sb("count", [P, NB])
        kcol = n.sb("kcol", [P, NB])
        total_i, zero = n.sb("total_i", [P, NB], I32), n.sb("zero", [P, NB])
        groups = n.sb("groups", [P, NB])
        ends = n.sb("ends", [P, NB])
        offset = n.sb("offset", [P, NB])
        gid = n.sb("gid", [P, U])
        cmp = n.sb("cmp", [P, U, NB])
        bucket = n.sb("bucket", [P, U])
        bucket_i = n.sb("bucket_i", [P, U], I32)
        QG = NG // 4
        lohi_r = n.sb("lohi_r", [QG, 4, 2])
        lohi_i = n.sb("lohi_i", [QG, 4, 2], I32)
        tick = n.sb("tick", [1, 1])
        pad_rec = n.sb("pad_rec", [P, SG * GE // P // PAD_DMAS, 4])
        ps_count = n.ps("ps_count", [P, 2, 512])
        ps_t = n.ps("ps_t", [P, 2, 512])

        loaded, x_loaded = n.sem("loaded"), n.sem("x_loaded")
        iotas, ident0, pool_done = n.sem("iotas"), n.sem("ident0"), n.sem("pool_done")
        dve = n.sem("dve")
        counted, prefixed = n.sem("counted"), n.sem("prefixed")
        ranges, turned, turned_read = n.sem("ranges"), n.sem("turned"), n.sem("turned_read")
        slot_step = n.sem("slot_step")
        slots_ready, rec_ready = n.sem("slots_ready"), n.sem("rec_ready")
        small_ready, acc_ready, xb_ready = n.sem("small_ready"), n.sem("acc_ready"), n.sem("xb_ready")
        pad_ready = n.sem("pad_ready")
        xb_stored = n.sem("xb_stored")
        written, tables = n.sem("written"), n.sem("tables")
        block = s.enter_context(nc.Block())

        @block.sync
        def _(sp):
            sp.dma_start(srci[:], a["src"]).then_inc(loaded, 16)
            sp.dma_start(dsti, a["dst"]).then_inc(loaded, 16)
            sp.dma_start(ow[:], a["ow"]).then_inc(loaded, 16)
            sp.dma_start(b1[:], row(a["ee_b1"])).then_inc(loaded, 16)
            sp.dma_start(b2[:], row(a["ee_b2"])).then_inc(loaded, 16)
            sp.dma_start(eps[:], row(a["eps"])).then_inc(loaded, 16)
            sp.dma_start(acc[:, :, 0:C], a["x"].rearrange("(b p) c -> p b c", p=P)).then_inc(x_loaded, 16)
            sp.wait_ge(pad_ready, 1)
            for q in range(PAD_DMAS):
                sp.dma_start(dram["sorted_record"].rearrange("(q p n) w -> q p (n w)", q=PAD_DMAS, p=P)[q],
                             pad_rec[:].rearrange("p n w -> p (n w)")).then_inc(written, 16)
            sp.wait_ge(small_ready, 1)
            sp.dma_start(dram["sorted_bucket"], bucket_i[:]).then_inc(tables, 16)
            sp.wait_ge(small_ready, 2)
            sp.dma_start(dram["dst_windows"].rearrange("(q g) w -> g q w", q=4), lohi_i[:]).then_inc(tables, 16)
            sp.wait_ge(tables, 32)
            flat = dram["sorted_bucket"].rearrange("p u -> (p u)")
            sp.dma_start(t["sorted_bucket"][0:1, 0:SG], flat[0:SG].unsqueeze(0)).then_inc(written, 16)
            sp.dma_start(t["windows"][0:1, 0:2 * NG],
                         dram["dst_windows"].rearrange("g w -> (g w)").unsqueeze(0)).then_inc(written, 16)
            sp.wait_ge(rec_ready, 1)
            sp.dma_start(dram["edge_record"], rec[:].rearrange("p n w -> p (n w)")).then_inc(written, 16)
            sp.wait_ge(slots_ready, 1)
            sp.dma_start(dram["edge_slot"], srci[:]).then_inc(written, 16)
            sp.wait_ge(written, 16 * (PAD_DMAS + 4))

        @block.gpsimd
        def _(pool):
            nc.gpsimd.memset(ident[:], 0.0).then_inc(ident0, 1)
            nc.gpsimd.memset(before[:], 1.0).then_inc(ident0, 1)
            nc.gpsimd.iota(kcol[:], pattern=[[1, NB]], base=0, channel_multiplier=0,
                           allow_small_or_imprecise_dtypes=True).then_inc(iotas, 1)
            nc.gpsimd.iota(gid[:], pattern=[[1, U]], base=0, channel_multiplier=U,
                           allow_small_or_imprecise_dtypes=True).then_inc(iotas, 1)
            pool.wait_ge(ident0, 2)
            nc.gpsimd.affine_select(out=ident[:], in_=ident[:], compare_op=ALU.not_equal, fill=1.0, base=0,
                                    pattern=[[-1, P]], channel_multiplier=1).then_inc(pool_done, 1)
            nc.gpsimd.affine_select(out=before[:], in_=before[:], compare_op=ALU.is_gt, fill=0.0, base=0,
                                    pattern=[[1, P]], channel_multiplier=-1).then_inc(pool_done, 1)

        @block.tensor
        def _(pe):
            pe.wait_ge(pool_done, 2)
            pe.wait_ge(ranges, 2)
            for k in range(8):
                if k >= 2:
                    pe.wait_ge(turned_read, k - 1)
                nc.tensor.transpose(ps_t[0:QG, k % 2, 0:P], lohi[:, k % 2, (k // 2) * QG:(k // 2 + 1) * QG],
                                    ident[:]).then_inc(turned, 1)
            pe.wait_ge(counted, NB)
            nc.tensor.matmul(ps_count[:, 0, 0:NB], before[:], count[:], start=True, stop=True)
            nc.tensor.matmul(ps_count[:, 1, 0:NB], ones[:], count[:], start=True, stop=True).then_inc(prefixed, 1)

        @block.scalar
        def _(act):
            act.wait_ge(loaded, 96)
            act.wait_ge(x_loaded, 16)
            act.wait_ge(xb_ready, NB)
            act.dma_start(dram["x_plus_b2"].rearrange("(b p) c -> p b c", p=P), acc[:, :, C:2 * C]).then_inc(xb_stored, 16)
            act.wait_ge(xb_stored, 16)
            for b in range(NB):
                act.wait_ge(acc_ready, b + 1)
                nc.scalar.activation(acc[:, b, C:2 * C], b1[:], ACT.Relu)

        @block.vector
        def _(v):
            steps = [0]

            def then(ins):
                steps[0] += 1
                ins.then_inc(dve, 1)
                v.wait_ge(dve, steps[0])

            v.memset(pad_rec[:, :, 0].bitcast(I32), NODES)
            v.memset(pad_rec[:, :, 1], -1.0)
            v.memset(pad_rec[:, :, 2:4], 0.0).then_inc(pad_ready, 1)
            v.memset(ones[:], 1.0)
            v.memset(zero[:], 0.0)
            v.memset(dstf[:, NT:], -1.0)
            v.memset(rec[:, :, 3], 0.0)
            v.memset(t["sorted_bucket"][:, SG:], 0)
            then(v.memset(t["windows"][:, 2 * NG:], 0))
            v.wait_ge(loaded, 96)
            v.tensor_copy(dstf[:, 0:NT], dsti)
            v.tensor_copy(rec[:, :, 1], srci[:])
            v.tensor_copy(rec[:, :, 2], ow[:])
            then(v.tensor_copy(rec[:, :, 0].bitcast(I32), dsti))
            v.tensor_single_scalar(srci[:], srci[:], BUCKET_SHIFT, op=ALU.arith_shift_right)
            then(v.tensor_single_scalar(dsti, dsti, BUCKET_SHIFT, op=ALU.arith_shift_right))
            v.tensor_copy(srcblk[:], srci[:]).then_inc(rec_ready, 1)
            then(v.tensor_copy(dstblk[:], dsti))
            by_group = dstblk[:].rearrange("p (g j) -> p g j", j=T)
            v.tensor_reduce(lohi[:, 0, :], by_group, AX, ALU.min).then_inc(ranges, 1)
            v.tensor_reduce(lohi[:, 1, :], by_group, AX, ALU.max).then_inc(ranges, 1)
            for k in range(8):
                v.wait_ge(turned, k + 1)
                v.tensor_reduce(lohi_r[:, k // 2, k % 2:k % 2 + 1], ps_t[0:QG, k % 2, 0:P], AX,
                                ALU.max if k % 2 else ALU.min).then_inc(turned_read, 1)
            v.wait_ge(iotas, 2)
            for k in range(NB):
                if k:
                    v.wait_ge(counted, k)
                v.tensor_scalar(scan[:], srcblk[:], float(k), None, ALU.is_equal, ALU.add,
                                accum_out=count[:, k:k + 1]).then_inc(counted, 1)
            v.wait_ge(prefixed, 1)
            then(v.tensor_scalar(groups[:], ps_count[:, 1, 0:NB], float(GE - 1), None, ALU.add))
            then(v.tensor_copy(total_i[:], groups[:]))
            then(v.tensor_single_scalar(total_i[:], total_i[:], GROUP_SHIFT, op=ALU.arith_shift_right))
            then(v.tensor_copy(groups[:], total_i[:]))
            then(v.tensor_tensor_scan(ends[:], zero[:], groups[:], 0.0, ALU.add, ALU.add))
            then(v.tensor_tensor(offset[:], ends[:], groups[:], ALU.subtract))
            then(v.tensor_scalar(offset[:], offset[:], float(GE), -1.0, ALU.mult, ALU.add))
            then(v.tensor_tensor(offset[:], offset[:], ps_count[:, 0, 0:NB], ALU.add))
            then(v.tensor_tensor(cmp[:, :, 0:NB - 1], gid[:].unsqueeze(2).to_broadcast([P, U, NB - 1]),
                                 ends[:, 0:NB - 1].unsqueeze(1).to_broadcast([P, U, NB - 1]), ALU.is_ge))
            then(v.tensor_reduce(bucket[:], cmp[:, :, 0:NB - 1], AX, ALU.add))
            v.tensor_copy(bucket_i[:], bucket[:]).then_inc(small_ready, 1)
            v.wait_ge(turned_read, 8)
            v.tensor_copy(lohi_i[:], lohi_r[:]).then_inc(small_ready, 1)
            with v.Fori(0, NB) as k:
                v.tensor_scalar(mask[:], srcblk[:], kcol[:, bass.ds(k, 1)], None, ALU.is_equal).then_inc(slot_step, 1)
                v.wait_ge(slot_step, k * 3 + 1)
                v.tensor_tensor_scan(scan[:], mask[:], mask[:], offset[:, bass.ds(k, 1)], ALU.add,
                                     ALU.bypass).then_inc(slot_step, 1)
                v.wait_ge(slot_step, k * 3 + 2)
                v.memset(tick[:], 0.0)
                v.copy_predicated(slot[:], mask[:].bitcast(I32), scan[:]).then_inc(slot_step, 1)
                v.wait_ge(slot_step, k * 3 + 3)
            v.tensor_copy(srci[:], slot[:]).then_inc(slots_ready, 1)
            v.wait_ge(x_loaded, 16)
            for b in range(NB):
                v.tensor_tensor(acc[:, b, C:2 * C], acc[:, b, 0:C], b2[:], ALU.add).then_inc(xb_ready, 1)
            then(v.tensor_scalar(eps[:], eps[:], 1.0, None, ALU.add))
            v.wait_ge(xb_ready, NB)
            for b in range(NB):
                v.scalar_tensor_tensor(out=acc[:, b, 0:C], in0=acc[:, b, 0:C], scalar=eps[:, 0:1],
                                       in1=acc[:, b, C:2 * C], op0=ALU.mult, op1=ALU.add).then_inc(acc_ready, 1)


def sum_over_dst(nc, a, dram, t, first):
    acc, dstf, windows = t["acc"], t["dstf"], t["windows"]
    parts = 2 if first else 1
    table = dram["x_plus_b2"] if first else dram["feat_in"]
    with ExitStack() as s:
        n = Names(nc, "sum1" if first else "sum2", s)
        iota = n.sb("iota", [P, NP])
        index = n.sb("index", [P, U, T], I32)
        rows = n.sb("rows", [P, U, T, C])
        onehot = n.sb("onehot", [P, 2, T, P])
        onehot_x = n.sb("onehot_x", [P, T, P])
        if first:
            attr = n.sb("attr", [EC + 1, U, T, P])
            w1 = n.sb("w1", [EC + 1, C])
            hidden = n.sb("hidden", [P, 2, T, C])
            ps_h = n.ps("ps_h", [P, 2, 2, C])
        else:
            iw = n.sb("iw", [P, NT + T])
        ps = n.ps("ps", [P, 2, 2, 512])
        ps_x = n.ps("ps_x", [P, 2, 512])

        consts, iota_set = n.sem("consts"), n.sem("iota_set")
        index_loaded = [n.sem(f"index_loaded{u}") for u in range(U)]
        attr_loaded = [n.sem(f"attr_loaded{u}") for u in range(U)]
        gathered = [n.sem(f"gathered{u}") for u in range(U)]
        ones_set = n.sem("ones_set")
        turns, turns_v = n.sem("turns"), n.sem("turns_v")
        onehot_ready, summed, ps_free = n.sem("onehot_ready"), n.sem("summed"), n.sem("ps_free")
        onehot_x_ready, summed_x, added_x = n.sem("onehot_x_ready"), n.sem("summed_x"), n.sem("added_x")
        group_done = n.sem("group_done")
        hidden_ps = n.sem("hidden_ps")
        hidden_ready = n.sem("hidden_ready")
        block = s.enter_context(nc.Block())

        @block.sync
        def _(sp):
            if first:
                sp.dma_start(w1[0:EC, :], a["ee_w1"]).then_inc(consts, 16)
                sp.dma_start(w1[EC:EC + 1, :], a["ee_b1"].unsqueeze(0)).then_inc(consts, 16)
            else:
                sp.dma_start(iw[:, 0:NT], a["iw"]).then_inc(consts, 16)

            def load_attr(g, u):
                sp.wait_ge(hidden_ps, g * 2 + 2)
                sp.dma_start(attr[0:EC, u, :, :], a["edge_attr"].rearrange("e (g j p) -> e g j p", j=T, p=P)
                             [:, bass.ds(g, 1), :, :].rearrange("e g j p -> e (g j p)")
                             ).then_inc(attr_loaded[u], 16)

            with sp.Fori(0, NG // U) as i:
                for u in range(U):
                    g = i * U + u
                    sp.wait_ge(group_done, g + 1)
                    sp.dma_start(index[:, u, :], a["src"][:, bass.ds(g * T, T)]).then_inc(index_loaded[u], 16)
                    if first:
                        load_attr(g, u)
            if first:
                load_attr(NG, 0)

        @block.gpsimd
        def _(pool):
            nc.gpsimd.iota(iota[:], pattern=[[1, NP]], base=0, channel_multiplier=0,
                           allow_small_or_imprecise_dtypes=True).then_inc(iota_set, 1)
            with pool.Fori(0, NG // U) as i:
                for u in range(U):
                    pool.wait_ge(index_loaded[u], i * 16 + 16)
                    pool.sem_inc(turns, 1)
                    for j in range(T):
                        pool.indirect_dma_start(
                            out=rows[:, u, j, :], out_offset=None, in_=table,
                            in_offset=bass.IndirectOffsetOnAxis(ap=index[:, u, j:j + 1], axis=0),
                        ).then_inc(gathered[u], 16)

        @block.tensor
        def _(pe):
            def edge_network(g, u, count):
                pe.wait_ge(attr_loaded[u], count * 16)
                for m in range(2):
                    pe.wait_ge(hidden_ready, g * 2 + m + 1)
                    for j in range(2):
                        mm = nc.tensor.matmul(ps_h[:, m, j, :], attr[:, u, 2 * m + j, :], w1[:],
                                              start=j == 0, stop=j == 1, skip_group_check=True)
                    mm.then_inc(hidden_ps, 1)

            def window(target, hot, u, hu):
                for part in range(parts):
                    for j in range(T):
                        data = rows[:, u, j, :] if part == 0 else hidden[:, hu, j, :]
                        mm = nc.tensor.matmul(target[:, part, 0:C], hot[:, j, :], data,
                                              start=j == 0, stop=j == T - 1)
                return mm

            if first:
                pe.sem_inc(hidden_ps, 2 * U)
                pe.wait_ge(consts, 32)
                pe.wait_ge(ones_set, 1)
                edge_network(0, 0, 1)
            further = pe.alloc_register(f"further_windows_{parts}")
            pe.reg_mov(further, 0)
            with pe.Fori(0, NG // U) as i:
                for u in range(U):
                    g = i * U + u
                    low = pe.value_load(windows[0:1, bass.ds(g * 2, 1)], min_val=0, max_val=NB - 1)
                    high = pe.value_load(windows[0:1, bass.ds(g * 2 + 1, 1)], min_val=0, max_val=NB - 1)
                    if first:
                        edge_network(g + 1, (u + 1) % U, i + 1 + (u + 1) // U)
                        pe.wait_ge(hidden_ready, g * 2 + 4)
                    pe.wait_ge(gathered[u], i * 16 * T + 16 * T)
                    pe.wait_ge(onehot_ready, g + 1)
                    pe.wait_ge(ps_free, g + 1)
                    window(ps[:, u % 2], onehot[:, u % 2], u, u % 2).then_inc(summed, 1)
                    with pe.If(low < high):
                        with pe.Fori(low, high) as b:
                            pe.reg_add(further, further, 1)
                            pe.wait_ge(onehot_x_ready, pe.snap(further, min_val=1, max_val=NG * NB))
                            window(ps_x, onehot_x, u, u % 2).then_inc(summed_x, 1)

        @block.scalar
        def _(act):
            if first:
                act.preload_act_table(ACT.Relu)
                act.sem_inc(hidden_ready, 2)

                def relu(g, hu):
                    act.wait_ge(group_done, g + 3)
                    for m in range(2):
                        act.wait_ge(hidden_ps, g * 2 + m + 1 + 2 * U)
                        nc.scalar.activation(hidden[:, hu, 2 * m:2 * m + 2, :], ps_h[:, m, :, :],
                                             ACT.Relu).then_inc(hidden_ready, 1)

                with act.Fori(0, NG // U) as i:
                    for u in range(U):
                        relu(i * U + u, u % 2)
                relu(NG, 0)

        @block.vector
        def _(v):
            v.sem_inc(group_done, U)
            v.sem_inc(ps_free, 2)
            if first:
                v.memset(attr[EC:EC + 1, :, :, :], 1.0).then_inc(ones_set, 1)
            else:
                v.wait_ge(consts, 16)
                v.memset(iw[:, NT:], 0.0).then_inc(ones_set, 1)
                v.wait_ge(ones_set, 1)
            further = v.alloc_register(f"further_windows_{parts}")
            v.reg_mov(further, 0)

            def one_hots(target, g, b):
                for j in range(T):
                    column = bass.ds(g * T + j, 1)
                    block_nodes = iota[:, bass.ds(b * P, P)]
                    if first:
                        ins = v.tensor_scalar(target[:, j, :], block_nodes, dstf[:, column], None, ALU.is_equal)
                    else:
                        ins = v.tensor_scalar(target[:, j, :], block_nodes, dstf[:, column], iw[:, column],
                                              ALU.is_equal, ALU.mult)
                return ins

            def add(source, b):
                sums = acc[:, bass.ds(b, 1), :].rearrange("p b (k c) -> p (b k) c", k=2)[:, 0:parts, :]
                return v.tensor_tensor(sums, sums, source[:, 0:parts, 0:C], ALU.add)

            v.wait_ge(iota_set, 1)
            low = v.value_load(windows[0:1, 0:1], min_val=0, max_val=NB - 1)
            one_hots(onehot[:, 0], 0, low).then_inc(onehot_ready, 1)
            with v.Fori(0, NG // U) as i:
                for u in range(U):
                    g = i * U + u
                    low = v.value_load(windows[0:1, bass.ds(g * 2, 1)], min_val=0, max_val=NB - 1)
                    high = v.value_load(windows[0:1, bass.ds(g * 2 + 1, 1)], min_val=0, max_val=NB - 1)
                    low_next = v.value_load(windows[0:1, bass.ds(g * 2 + 2, 1)], min_val=0, max_val=NB - 1)
                    one_hots(onehot[:, (u + 1) % 2], g + 1, low_next).then_inc(onehot_ready, 1)
                    v.wait_ge(summed, g + 1)
                    v.wait_ge(ps_free, g + 2)
                    add(ps[:, u % 2], low).then_inc(ps_free, 1)
                    with v.If(low < high):
                        with v.Fori(low + 1, high + 1) as b:
                            one_hots(onehot_x, g, b).then_inc(onehot_x_ready, 1)
                            v.reg_add(further, further, 1)
                            done = v.snap(further, min_val=1, max_val=NG * NB)
                            v.wait_ge(summed_x, done)
                            add(ps_x, b).then_inc(added_x, 1)
                            v.wait_ge(added_x, done)
                    v.sem_inc(group_done, 1)


def node_network(nc, a, dram, t):
    acc, ident = t["acc"], t["ident"]
    with ExitStack() as s:
        n = Names(nc, "net", s)
        w_ee = n.sb("w_ee", [P, CC, C])
        w1 = n.sb("w1", [P, CC, H])
        w2 = n.sb("w2", [P, HC, H])
        w3 = n.sb("w3", [P, HC, C])
        bias = n.sb("bias", [P, 2, H])
        bias3 = n.sb("bias3", [P, C])
        bn_g, bn_b = n.sb("bn_g", [P, C]), n.sb("bn_b", [P, C])
        gain = n.sb("gain", [P, 2, HC])
        shift = n.sb("shift", [P, 2, HC])
        sums = n.sb("sums", [P, 2 * C])
        hid_t = n.sb("hid_t", [P, CC, P])
        in_t = n.sb("in_t", [P, CC, P])
        z = n.sb("z", [P, H])
        act_t = n.sb("act_t", [P, 2, HC, P])
        stats = n.sb("stats", [P, 2, 6])
        mv = n.sb("mv", [P, 2])
        std, rstd, eps = n.sb("std", [P, 1]), n.sb("rstd", [P, 1]), n.sb("eps", [P, 1])
        x_in = n.sb("x_in", [P, C])
        y = n.sb("y", [P, C])
        x1 = n.sb("x1", [P, C])
        index = n.sb("index", [P, 2, ST], I32)
        record = n.sb("record", [P, 2, ST, 4])
        ps_t = n.ps("ps_t", [P, 1, 512])
        ps_z = n.ps("ps_z", [P, 2, 512])
        ps_a = n.ps("ps_a", [P, 2, 512])
        ps_in = n.ps("ps_in", [P, 512])
        ps_y = n.ps("ps_y", [P, 512])
        ps_x = n.ps("ps_x", [P, 512])

        loaded = n.sem("loaded")
        x_loaded = n.sem("x_loaded")
        sums_ready, hid_turned, hid_copied = n.sem("sums_ready"), n.sem("hid_turned"), n.sem("hid_copied")
        in_summed, in_copied = n.sem("in_summed"), n.sem("in_copied")
        eps_set = n.sem("eps_set")
        z_summed, z_read = n.sem("z_summed"), n.sem("z_read")
        z_ready, z_turned, act_ready = n.sem("z_ready"), n.sem("z_turned"), n.sem("act_ready")
        var_ready, std_ready = n.sem("var_ready"), n.sem("std_ready")
        y_summed, y_read = n.sem("y_summed"), n.sem("y_read")
        x1_ready, x1_turned, x1_stored = n.sem("x1_ready"), n.sem("x1_turned"), n.sem("x1_stored")
        dve = n.sem("dve")
        slots_loaded = [n.sem("slots_loaded0"), n.sem("slots_loaded1")]
        scattered = [n.sem("scattered0"), n.sem("scattered1")]
        turns, turns_v = n.sem("turns"), n.sem("turns_v")
        block = s.enter_context(nc.Block())
        LOADS = 13
        steps = NT // ST
        assert NT % ST == 0 and steps % 2 == 0

        @block.sync
        def _(sp):
            sp.dma_start(w_ee[:], a["ee_w2"].rearrange("(c p) n -> p c n", p=P)).then_inc(loaded, 16)
            sp.dma_start(w1[:], a["w1"].rearrange("(c p) n -> p c n", p=P)).then_inc(loaded, 16)
            sp.dma_start(bias[:, 0, :], row(a["b1"])).then_inc(loaded, 16)
            sp.dma_start(bias[:, 1, :], row(a["b2"])).then_inc(loaded, 16)
            for k, (g, be) in enumerate((("g1", "be1"), ("g2", "be2"))):
                sp.dma_start(gain[:, k, :], a[g]).then_inc(loaded, 16)
                sp.dma_start(shift[:, k, :], a[be]).then_inc(loaded, 16)
            sp.dma_start(w2[:], a["w2"].rearrange("(c p) n -> p c n", p=P)).then_inc(loaded, 16)
            sp.dma_start(w3[:], a["w3"].rearrange("(c p) n -> p c n", p=P)).then_inc(loaded, 16)
            sp.dma_start(bias3[:], row(a["b3"])).then_inc(loaded, 16)
            sp.dma_start(bn_g[:], row(a["bn_g"])).then_inc(loaded, 16)
            sp.dma_start(bn_b[:], row(a["bn_b"])).then_inc(loaded, 16)
            def load(q, k):
                sp.dma_start(index[:, k, :], dram["edge_slot"][:, bass.ds(q * ST, ST)]
                             ).then_inc(slots_loaded[k], 16)
                sp.dma_start(record[:, k, :, :].rearrange("p t w -> p (t w)"),
                             dram["edge_record"][:, bass.ds(q * (4 * ST), 4 * ST)]
                             ).then_inc(slots_loaded[k], 16)

            for k in range(2):
                load(k, k)
            with sp.Fori(1, steps // 2) as i:
                for k in range(2):
                    sp.wait_ge(scattered[k], i * (16 * ST))
                    load(i * 2 + k, k)

        @block.gpsimd
        def _(pool):
            with pool.Fori(0, steps // 2) as i:
                for k in range(2):
                    pool.wait_ge(slots_loaded[k], i * 32 + 32)
                    pool.sem_inc(turns, 1)
                    for j in range(ST):
                        pool.indirect_dma_start(
                            out=dram["sorted_record"],
                            out_offset=bass.IndirectOffsetOnAxis(ap=index[:, k, j:j + 1], axis=0),
                            in_=record[:, k, j, :], in_offset=None,
                        ).then_inc(scattered[k], 16)
            for k in range(2):
                pool.wait_ge(scattered[k], steps // 2 * 16 * ST)

        @block.tensor
        def _(pe):
            def network_input(b):
                pe.wait_ge(sums_ready, b + 1)
                for c in range(CC):
                    mm = nc.tensor.transpose(ps_t[:, 0, c * P:(c + 1) * P], sums[:, C + c * P:C + (c + 1) * P], ident[:])
                mm.then_inc(hid_turned, 1)
                pe.wait_ge(hid_copied, b + 1)
                for c in range(CC):
                    target = ps_in[:, c * P:(c + 1) * P]
                    nc.tensor.matmul(target, sums[:, c * P:(c + 1) * P], ident[:], start=c == 0, stop=False,
                                     skip_group_check=True)
                    for k in range(CC):
                        mm = nc.tensor.matmul(target, w_ee[:, k, c * P:(c + 1) * P], hid_t[:, k, :], start=False,
                                              stop=k == CC - 1, skip_group_check=True)
                mm.then_inc(in_summed, 1)

            def hidden_layer(b, layer):
                pe.wait_ge(z_read, b * 2 + layer + 1)
                if layer == 0:
                    pe.wait_ge(in_copied, b + 1)
                    chunks, w = [in_t[:, c, :] for c in range(CC)], w1
                else:
                    chunks, w = [act_t[:, 0, c, :] for c in range(HC)], w2
                for m in range(2):
                    for c, x in enumerate(chunks):
                        if layer == 1 and m == 0:
                            pe.wait_ge(act_ready, b * 2 * HC + HC // 2 + c + 2)
                        mm = nc.tensor.matmul(ps_z[:, m, :], x, w[:, c, m * 512:(m + 1) * 512], start=c == 0,
                                              stop=c == len(chunks) - 1)
                    mm.then_inc(z_summed, 1)

            def turn_hidden(b, layer):
                pe.wait_ge(z_ready, b * 2 + layer + 1)
                for m in range(2):
                    pe.wait_ge(act_ready, (b * 2 + layer) * HC + m * (HC // 2) + 1)
                    for c in range(HC // 2):
                        k = m * (HC // 2) + c
                        mm = nc.tensor.transpose(ps_a[:, m, c * P:(c + 1) * P], z[:, k * P:(k + 1) * P], ident[:])
                    mm.then_inc(z_turned, 1)

            def output_layer(b):
                pe.wait_ge(y_read, b + 1)
                for c in range(HC):
                    pe.wait_ge(act_ready, b * 2 * HC + HC + HC // 2 + c + 2)
                    mm = nc.tensor.matmul(ps_y[:, 0:C], act_t[:, 1, c, :], w3[:, c, :], start=c == 0, stop=c == HC - 1)
                mm.then_inc(y_summed, 1)

            def turn_x1(b):
                pe.wait_ge(x1_ready, b + 1)
                pe.wait_ge(x1_stored, b + 1)
                for c in range(CC):
                    mm = nc.tensor.transpose(ps_x[:, c * P:(c + 1) * P], x1[:, c * P:(c + 1) * P], ident[:])
                mm.then_inc(x1_turned, 1)

            def body(b, first=False, last=False):
                turn_hidden(b, 0)
                hidden_layer(b, 1)
                if not first:
                    turn_x1(b - 1)
                if not last:
                    network_input(b + 1)
                turn_hidden(b, 1)
                if not last:
                    hidden_layer(b + 1, 0)
                output_layer(b)

            pe.wait_ge(loaded, 16 * LOADS)
            network_input(0)
            hidden_layer(0, 0)
            body(0, first=True)
            with pe.Fori(1, NB - 1) as b:
                body(b)
            body(NB - 1, last=True)
            turn_x1(NB - 1)

        @block.scalar
        def _(act):
            act.preload_act_table(ACT.Sqrt)
            act.sem_inc(act_ready, HC // 2 + 1)
            act.sem_inc(x1_stored, 1)
            act.wait_ge(loaded, 16 * LOADS)

            def copy_sums(b):
                nc.scalar.activation(sums[:], acc[:, bass.ds(b, 1), :].rearrange("p b c -> p (b c)"),
                                     ACT.Copy).then_inc(sums_ready, 1)

            def copy_input(b):
                act.wait_ge(hid_turned, b + 1)
                nc.scalar.activation(hid_t[:].rearrange("p c n -> p (c n)"), ps_t[:, 0, 0:C], ACT.Copy
                                     ).then_inc(hid_copied, 1)
                act.wait_ge(in_summed, b + 1)
                nc.scalar.activation(in_t[:].rearrange("p c n -> p (c n)"), ps_in[:, 0:C], ACT.Copy
                                     ).then_inc(in_copied, 1)

            def activate(b, layer):
                for c in range(HC):
                    if c % (HC // 2) == 0:
                        act.wait_ge(z_turned, (b * 2 + layer) * 2 + c // (HC // 2) + 1)
                    nc.scalar.activation(act_t[:, layer, c, :],
                                         ps_a[:, c // (HC // 2), (c % (HC // 2)) * P:(c % (HC // 2) + 1) * P], ACT.Relu,
                                         bias=shift[:, layer, c:c + 1], scale=gain[:, layer, c:c + 1]
                                         ).then_inc(act_ready, 1)

            def load_x(b):
                act.dma_start(x_in[:], a["x"].rearrange("(b p) c -> p b c", p=P)[:, bass.ds(b, 1), :]
                              .rearrange("p b c -> p (b c)")).then_inc(x_loaded, 16)

            def root(number):
                act.wait_ge(var_ready, number + 1)
                nc.scalar.activation(std[:], mv[:, 1:2], ACT.Sqrt, bias=eps[:, 0:1]).then_inc(std_ready, 1)

            def store_x1(b):
                act.wait_ge(x1_turned, b + 1)
                nc.scalar.activation(acc[:, bass.ds(b, 1), C:2 * C].rearrange("p b c -> p (b c)"), ps_x[:, 0:C],
                                     ACT.Copy).then_inc(x1_stored, 1)

            def body(b, first=False, last=False):
                activate(b, 0)
                if not last:
                    act.wait_ge(in_summed, b + 1)
                    copy_sums(b + 1)
                if not first:
                    root(b * 4 - 1)
                    root(b * 4)
                    store_x1(b - 1)
                    load_x(b)
                if not last:
                    copy_input(b + 1)
                root(b * 4 + 1)
                activate(b, 1)
                if not last:
                    root(b * 4 + 2)

            load_x(0)
            copy_sums(0)
            copy_input(0)
            act.wait_ge(eps_set, 1)
            root(0)
            body(0, first=True)
            with act.Fori(1, NB - 1) as b:
                body(b)
            body(NB - 1, last=True)
            root(NB * 4 - 2)
            root(NB * 4 - 1)
            store_x1(NB - 1)

        @block.vector
        def _(v):
            chain = Chain(v, dve)
            v.sem_inc(z_read, 1)
            v.sem_inc(y_read, 1)
            v.memset(eps[:], LN_EPS).then_inc(eps_set, 1)
            v.wait_ge(loaded, 16 * LOADS)

            def normed(out_, in_, number):
                halves = -(-in_.shape[1] // 512)
                w = in_.shape[1] // halves
                for m in range(halves):
                    ins = v.bn_stats(stats[:, m, :], in_[:, m * w:(m + 1) * w])
                chain.then(ins)
                v.sem_inc(turns_v, 1)
                chain.then(v.bn_aggr(mv[:], stats[:, 0:halves, :].rearrange("p m s -> p (m s)")))
                v.sem_inc(var_ready, 1)
                v.wait_ge(std_ready, number + 1)
                chain.then(v.reciprocal(rstd[:], std[:]))
                return v.tensor_scalar(out_, in_, mv[:, 0:1], rstd[:, 0:1], ALU.subtract, ALU.mult)

            def hidden(b, layer):
                number = b * 2 + layer
                for m in range(2):
                    v.wait_ge(z_summed, number * 2 + m + 1)
                    ins = v.tensor_tensor(z[:, m * 512:(m + 1) * 512], ps_z[:, m, :],
                                          bias[:, layer, m * 512:(m + 1) * 512], ALU.add)
                ins.then_inc(z_read, 1)
                v.wait_ge(z_read, number + 2)
                normed(z[:], z[:], b * 4 + 1 if layer else b * 4 - 2 if not isinstance(b, int) or b else 0
                       ).then_inc(z_ready, 1)

            def output(b, last):
                v.wait_ge(y_summed, b + 1)
                v.tensor_tensor(y[:], ps_y[:, 0:C], bias3[:], ALU.add).then_inc(y_read, 1)
                v.wait_ge(y_read, b + 2)
                v.wait_ge(x_loaded, b * 16 + 16)
                chain.then(v.tensor_tensor(y[:], y[:], x_in[:], ALU.add))
                at = b * 4 + 3 - last
                chain.then(normed(y[:], y[:], at))
                chain.then(v.tensor_tensor(y[:], y[:], bn_g[:], ALU.mult))
                chain.then(v.tensor_tensor(y[:], y[:], bn_b[:], ALU.add))
                chain.then(v.scalar_tensor_tensor(out=y[:], in0=y[:], scalar=0.0, in1=x_in[:], op0=ALU.max, op1=ALU.add))
                normed(x1[:], y[:], at + 1).then_inc(x1_ready, 1)
                v.wait_ge(x1_ready, b + 1)
                v.tensor_copy(acc[:, bass.ds(b, 1), 0:C].rearrange("p b c -> p (b c)"), x1[:])

            def body(b, last=False):
                hidden(b, 1)
                if not last:
                    hidden(b + 1, 0)
                output(b, last)

            hidden(0, 0)
            body(0)
            with chain.loop(v, 1, NB - 1, 17) as b:
                body(b)
            body(NB - 1, last=True)


def make_tables(nc, a, dram, t):
    acc = t["acc"]
    with ExitStack() as s:
        n = Names(nc, "tab", s)
        w_io = n.sb("w_io", [P, CC, 2 * C])
        bias = n.sb("bias", [P, 2 * C])
        gamma, beta = n.sb("gamma", [P, CC]), n.sb("beta", [P, CC])
        stats = n.sb("stats", [P, CC, NB, 6])
        mv = n.sb("mv", [P, CC, 2])
        scale, shift = n.sb("scale", [P, CC]), n.sb("shift", [P, CC])
        h_t = n.sb("h_t", [P, 2, CC, P])
        feat = n.sb("feat", [P, 2, 2 * C])
        ps = n.ps("ps", [P, 2, 2 * C])
        loaded, x1_saved, dve, stats_done = n.sem("loaded"), n.sem("x1_saved"), n.sem("dve"), n.sem("stats_done")
        h_ready, summed, feat_ready = n.sem("h_ready"), n.sem("summed"), n.sem("feat_ready")
        var_ready, std_ready = n.sem("var_ready"), n.sem("std_ready")
        stored = [n.sem("stored0"), n.sem("stored1")]
        block = s.enter_context(nc.Block())
        LD = 6

        def blocks(eng, body):
            body(0, 0, 0)
            body(1, 1, 0)
            with eng.Fori(1, NB // 2) as i:
                for k in range(2):
                    body(i * 2 + k, k, i)
            body(NB - 1, 0, NB // 2)

        @block.sync
        def _(sp):
            sp.dma_start(w_io[:, :, 0:C], a["W_in"].rearrange("(c p) n -> p c n", p=P)).then_inc(loaded, 16)
            sp.dma_start(w_io[:, :, C:2 * C], a["W_out"].rearrange("(c p) n -> p c n", p=P)).then_inc(loaded, 16)
            sp.dma_start(bias[:, 0:C], row(a["b_in"])).then_inc(loaded, 16)
            sp.dma_start(bias[:, C:2 * C], row(a["b_out"])).then_inc(loaded, 16)
            sp.dma_start(gamma[:], a["gamma"]).then_inc(loaded, 16)
            sp.dma_start(beta[:], a["beta"]).then_inc(loaded, 16)
            sp.dma_start(dram["x1"].rearrange("p (b c) -> p b c", c=C), acc[:, :, 0:C]).then_inc(x1_saved, 16)

            def store(b, k, i):
                sp.wait_ge(h_ready, b + 1)
                sp.dma_start(dram["hT"][:, bass.ds(b * C, C)], h_t[:, k].rearrange("p c n -> p (c n)")
                             ).then_inc(stored[k], 16)
                sp.wait_ge(feat_ready, b + 1)
                for part, name in enumerate(("feat_in", "feat_out")):
                    sp.dma_start(dram[name].rearrange("(b p) c -> p b c", p=P)[:, bass.ds(b, 1), :]
                                 .rearrange("p b c -> p (b c)"), feat[:, k, part * C:(part + 1) * C]
                                 ).then_inc(stored[k], 16)

            blocks(sp, store)
            sp.wait_ge(stored[0], (NB // 2 + 1) * 48)
            sp.wait_ge(stored[1], NB // 2 * 48)
            sp.wait_ge(x1_saved, 16)

        @block.tensor
        def _(pe):
            pe.wait_ge(loaded, 16 * LD)

            def multiply(b, k, i):
                pe.wait_ge(h_ready, b + 1)
                for c in range(CC):
                    mm = nc.tensor.matmul(ps[:, k, :], h_t[:, k, c, :], w_io[:, c, :], start=c == 0, stop=c == CC - 1)
                mm.then_inc(summed, 1)

            blocks(pe, multiply)

        @block.scalar
        def _(act):
            act.wait_ge(var_ready, 1)
            nc.scalar.activation(shift[:], scale[:], ACT.Sqrt).then_inc(std_ready, 1)

        @block.vector
        def _(v):
            chain = Chain(v, dve)
            with v.Fori(0, NB - 1) as b:
                for c in range(CC):
                    v.bn_stats(stats[:, c, bass.ds(b, 1), :].rearrange("p b s -> p (b s)"),
                               acc[:, bass.ds(b, 1), C + c * P:C + (c + 1) * P].rearrange("p b c -> p (b c)")
                               ).then_inc(stats_done, 1)
            for c in range(CC):
                v.bn_stats(stats[:, c, NB - 1, :], acc[:, NB - 1, C + c * P:C + c * P + LAST]).then_inc(stats_done, 1)
            v.wait_ge(stats_done, CC * NB)
            v.wait_ge(loaded, 16 * LD)
            for c in range(CC):
                ins = v.bn_aggr(mv[:, c, :], stats[:, c, :, :].rearrange("p b s -> p (b s)"))
            chain.then(ins)
            chain.then(v.tensor_scalar(scale[:], mv[:, :, 1], LN_EPS, None, ALU.add))
            v.sem_inc(var_ready, 1)
            v.wait_ge(std_ready, 1)
            chain.then(v.reciprocal(scale[:], shift[:]))
            chain.then(v.tensor_tensor(scale[:], scale[:], gamma[:], ALU.mult))
            chain.then(v.tensor_tensor(shift[:], scale[:], mv[:, :, 0], ALU.mult))
            chain.then(v.tensor_tensor(shift[:], beta[:], shift[:], ALU.subtract))

            def table(b, k, i):
                if not isinstance(i, int) or i:
                    v.wait_ge(stored[k], i * 48)
                for c in range(CC):
                    ins = v.tensor_scalar(h_t[:, k, c, :],
                                          acc[:, bass.ds(b, 1), C + c * P:C + (c + 1) * P].rearrange("p b c -> p (b c)"),
                                          scale[:, c:c + 1], shift[:, c:c + 1], ALU.mult, ALU.add)
                ins.then_inc(h_ready, 1)
                v.wait_ge(summed, b + 1)
                v.tensor_tensor(feat[:, k, :], ps[:, k, :], bias[:], ALU.add).then_inc(feat_ready, 1)

            blocks(v, table)
            v.wait_ge(x1_saved, 16)
            v.wait_ge(feat_ready, NB)
            v.memset(acc[:].rearrange("p b c -> p (b c)"), 0.0)


def sum_over_src(nc, a, dram, t):
    acc, bucket = t["acc"], t["sorted_bucket"]
    with ExitStack() as s:
        n = Names(nc, "sum3", s)
        iota = n.sb("iota", [P, NP])
        record = n.sb("record", [P, U, T, 4])
        rows = n.sb("rows", [P, U, T, C])
        onehot = n.sb("onehot", [P, 2, T, P])
        ps = n.ps("ps", [P, 2, 512])
        loaded = [n.sem(f"loaded{u}") for u in range(U)]
        gathered = [n.sem(f"gathered{u}") for u in range(U)]
        turns, onehot_ready, summed, ps_free = n.sem("turns"), n.sem("onehot_ready"), n.sem("summed"), n.sem("ps_free")
        group_done = n.sem("group_done")
        iota_set = n.sem("iota_set")
        block = s.enter_context(nc.Block())
        records = dram["sorted_record"].rearrange("(g p j) w -> p g (j w)", p=P, j=T)

        @block.sync
        def _(sp):
            def load(g, u, source):
                sp.wait_ge(group_done, g + 1)
                sp.dma_start(record[:, u].rearrange("p j w -> p (j w)"),
                             records[:, bass.ds(source, 1), :].rearrange("p g w -> p (g w)")).then_inc(loaded[u], 16)

            with sp.Fori(0, SG // U) as i:
                for u in range(U):
                    load(i * U + u, u, i * U + u)
            load(SG, 0, 0)
            sp.wait_ge(loaded[0], (SG // U + 1) * 16)

        @block.gpsimd
        def _(pool):
            nc.gpsimd.iota(iota[:], pattern=[[1, NP]], base=0, channel_multiplier=0,
                           allow_small_or_imprecise_dtypes=True).then_inc(iota_set, 1)
            with pool.Fori(0, SG // U) as i:
                for u in range(U):
                    pool.wait_ge(loaded[u], i * 16 + 16)
                    pool.sem_inc(turns, 1)
                    for j in range(T):
                        pool.indirect_dma_start(
                            out=rows[:, u, j, :], out_offset=None, in_=dram["feat_out"],
                            in_offset=bass.IndirectOffsetOnAxis(ap=record[:, u, j, 0:1].bitcast(I32), axis=0),
                        ).then_inc(gathered[u], 16)

        @block.tensor
        def _(pe):
            with pe.Fori(0, SG // U) as i:
                for u in range(U):
                    g = i * U + u
                    pe.wait_ge(gathered[u], i * 16 * T + 16 * T)
                    pe.wait_ge(onehot_ready, g + 1)
                    pe.wait_ge(ps_free, g + 1)
                    for j in range(T):
                        mm = nc.tensor.matmul(ps[:, u % 2, 0:C], onehot[:, u % 2, j, :], rows[:, u, j, :],
                                              start=j == 0, stop=j == T - 1)
                    mm.then_inc(summed, 1)

        @block.vector
        def _(v):
            v.sem_inc(group_done, U)
            v.sem_inc(ps_free, 2)

            def one_hots(g, u, count):
                v.wait_ge(loaded[u], count * 16)
                b = v.value_load(bucket[0:1, bass.ds(g, 1)], min_val=0, max_val=NB - 1)
                for j in range(T):
                    ins = v.tensor_scalar(onehot[:, u % 2, j, :], iota[:, bass.ds(b * P, P)], record[:, u, j, 1:2],
                                          record[:, u, j, 2:3], ALU.is_equal, ALU.mult)
                ins.then_inc(onehot_ready, 1)

            v.wait_ge(iota_set, 1)
            one_hots(0, 0, 1)
            with v.Fori(0, SG // U) as i:
                for u in range(U):
                    g = i * U + u
                    one_hots(g + 1, (u + 1) % U, i + 1 + (u + 1) // U)
                    b = v.value_load(bucket[0:1, bass.ds(g, 1)], min_val=0, max_val=NB - 1)
                    v.wait_ge(summed, g + 1)
                    v.wait_ge(ps_free, g + 2)
                    sums = acc[:, bass.ds(b, 1), C:2 * C].rearrange("p b c -> p (b c)")
                    v.tensor_tensor(sums, sums, ps[:, u % 2, 0:C], ALU.add).then_inc(ps_free, 1)
                    v.sem_inc(group_done, 1)


def gates(nc, a, dram, t, out):
    acc, ident = t["acc"], t["ident"]
    KC = 2 * CC
    with ExitStack() as s:
        n = Names(nc, "gate", s)
        w_x = n.sb("w_x", [P, KC, 2 * C])
        w_h = n.sb("w_h", [P, CC, 2 * C])
        bias = n.sb("bias", [P, 2 * C])
        x1 = n.sb("x1", [P, 2, C])
        h_t = n.sb("h_t", [P, 2, CC, P])
        sums = n.sb("sums", [P, 2, 2 * C])
        sums_t = n.sb("sums_t", [P, 2, KC, P])
        pre = n.sb("pre", [P, 2, 2 * C])
        gate = n.sb("gate", [P, 2, 2 * C])
        y = n.sb("y", [P, C])
        stats, mv_b, mv = n.sb("stats", [P, 6]), n.sb("mv_b", [P, 2]), n.sb("mv", [P, NB, 2])
        var, std, rstd = n.sb("var", [P, NB]), n.sb("std", [P, NB]), n.sb("rstd", [P, NB])
        ps_t = n.ps("ps_t", [P, 2, 512])
        ps_h = n.ps("ps_h", [P, 2, 512])
        ps_g = n.ps("ps_g", [P, 2, 512])
        loaded = n.sem("loaded")
        in_loaded = [n.sem("in_loaded0"), n.sem("in_loaded1")]
        stored = n.sem("stored")
        var_ready, std_ready = n.sem("var_ready"), n.sem("std_ready")
        sums_ready, turned, sums_t_ready = n.sem("sums_ready"), n.sem("turned"), n.sem("sums_t_ready")
        summed, pre_ready, gates_ready = n.sem("summed"), n.sem("pre_ready"), n.sem("gates_ready")
        turns, turns_v = n.sem("turns"), n.sem("turns_v")
        mixed, done, dve = n.sem("mixed"), n.sem("done"), n.sem("dve")
        block = s.enter_context(nc.Block())

        def blocks(eng, body, chain=None):
            body(0, 0, 0)
            body(1, 1, 0)
            with chain.loop(eng, 1, NB // 2, 12) if chain else eng.Fori(1, NB // 2) as i:
                for k in range(2):
                    body(i * 2 + k, k, i)
            body(NB - 1, 0, NB // 2)

        @block.sync
        def _(sp):
            sp.dma_start(w_x[:], a["W_x2i"].rearrange("(c p) n -> p c n", p=P)).then_inc(loaded, 16)
            sp.dma_start(w_h[:], a["W_h2h"].rearrange("(c p) n -> p c n", p=P)).then_inc(loaded, 16)
            sp.dma_start(bias[:], row(a["b_x2i"])).then_inc(loaded, 16)

            def load(b, k, i):
                sp.wait_ge(mixed, b + 1)
                sp.dma_start(x1[:, k, :], dram["x1"][:, bass.ds(b * C, C)]).then_inc(in_loaded[k], 16)
                sp.dma_start(h_t[:, k].rearrange("p c n -> p (c n)"), dram["hT"][:, bass.ds(b * C, C)]
                             ).then_inc(in_loaded[k], 16)

            blocks(sp, load)
            rows = out.rearrange("(b p) c -> p b c", p=P)
            for b in range(0, NB, STORE):
                m = min(STORE, NB - b)
                sp.wait_ge(done, b + m)
                sp.dma_start(rows[:, b:b + m, :], acc[:, b:b + m, C:2 * C]).then_inc(stored, 16)
            sp.wait_ge(stored, -(-NB // STORE) * 16)

        @block.tensor
        def _(pe):
            pe.wait_ge(loaded, 48)

            def multiply(b, k, i):
                pe.wait_ge(sums_ready, b + 1)
                pe.wait_ge(mixed, b + 1)
                for c in range(KC):
                    mm = nc.tensor.transpose(ps_t[:, k, c * P:(c + 1) * P], sums[:, k, c * P:(c + 1) * P], ident[:])
                mm.then_inc(turned, 1)
                pe.wait_ge(in_loaded[k], i * 32 + 32)
                for c in range(CC):
                    nc.tensor.transpose(ps_h[:, k, c * P:(c + 1) * P], h_t[:, k, c, :], ident[:])
                for c in range(CC):
                    nc.tensor.matmul(ps_g[:, k, :], h_t[:, k, c, :], w_h[:, c, :], start=c == 0, stop=False)
                pe.wait_ge(sums_t_ready, b + 1)
                for c in range(KC):
                    mm = nc.tensor.matmul(ps_g[:, k, :], sums_t[:, k, c, :], w_x[:, c, :], start=False, stop=c == KC - 1)
                mm.then_inc(summed, 1)

            blocks(pe, multiply)

        @block.scalar
        def _(act):
            act.preload_act_table(ACT.Sigmoid)

            def copy_sums(b, k):
                act.wait_ge(mixed, b + 1)
                nc.scalar.activation(sums[:, k, :], acc[:, bass.ds(b, 1), :].rearrange("p b c -> p (b c)"), ACT.Copy
                                     ).then_inc(sums_ready, 1)
                act.wait_ge(turned, b + 1)
                nc.scalar.activation(sums_t[:, k].rearrange("p c n -> p (c n)"), ps_t[:, k, :], ACT.Copy
                                     ).then_inc(sums_t_ready, 1)

            def work(b, k, i):
                copy_sums(b, k)
                act.wait_ge(pre_ready, b + 1)
                nc.scalar.activation(gate[:, k, 0:C], pre[:, k, 0:C], ACT.Sigmoid)
                nc.scalar.activation(gate[:, k, C:2 * C], pre[:, k, C:2 * C], ACT.Tanh).then_inc(gates_ready, 1)

            blocks(act, work)
            act.wait_ge(var_ready, 1)
            nc.scalar.activation(std[:], var[:], ACT.Sqrt).then_inc(std_ready, 1)

        @block.vector
        def _(v):
            chain = Chain(v, dve)
            v.sem_inc(mixed, 2)

            v.wait_ge(loaded, 48)

            def mix(b, k, i):
                v.wait_ge(summed, b + 1)
                v.tensor_tensor(pre[:, k, :], ps_g[:, k, :], bias[:], ALU.add).then_inc(pre_ready, 1)
                v.wait_ge(gates_ready, b + 1)
                new = gate[:, k, C:2 * C]
                chain.then(v.tensor_tensor(y[:], ps_h[:, k, 0:C], new, ALU.subtract))
                chain.then(v.tensor_tensor(y[:], y[:], gate[:, k, 0:C], ALU.mult))
                chain.then(v.tensor_tensor(y[:], y[:], new, ALU.add))
                v.wait_ge(in_loaded[k], i * 32 + 32)
                v.tensor_tensor(y[:], y[:], x1[:, k, :], ALU.add).then_inc(mixed, 1)
                v.wait_ge(mixed, b + 3)
                chain.then(v.bn_stats(stats[:], y[:]))
                v.sem_inc(turns_v, 1)
                chain.then(v.bn_aggr(mv_b[:], stats[:]))
                v.tensor_copy(mv[:, bass.ds(b, 1), :].rearrange("p b s -> p (b s)"), mv_b[:])
                chain.then(v.tensor_copy(acc[:, bass.ds(b, 1), 0:C].rearrange("p b c -> p (b c)"), y[:]))

            blocks(v, mix, chain)
            chain.then(v.tensor_scalar(var[:], mv[:, :, 1], LN_EPS, None, ALU.add))
            v.sem_inc(var_ready, 1)
            v.wait_ge(std_ready, 1)
            chain.then(v.reciprocal(rstd[:], std[:]))
            for b in range(NB):
                v.tensor_scalar(acc[:, b, C:2 * C], acc[:, b, 0:C], mv[:, b, 0:1], rstd[:, b:b + 1], ALU.subtract,
                                ALU.mult).then_inc(done, 1)


def kernel(**inputs):
    import numpy as np
    import concourse.bacc as bacc
    from concourse.bass_utils import run_bass_kernel_spmd as run

    arrays = layout(np, inputs)
    nc = bacc.Bacc("TRN2", target_bir_lowering=False, num_devices=1)
    a = {k: nc.dram_tensor(f"in_{k}", v.shape, mybir.dt.from_np(v.dtype), kind="ExternalInput").ap()
         for k, v in arrays.items()}
    out = nc.dram_tensor("out_0", (NP, C), F32, kind="ExternalOutput").ap()
    gnn_kernel(nc, a, out)
    r = run(nc, [{f"in_{k}": v for k, v in arrays.items()}], core_ids=[0])
    return r.results[0]["out_0"][:NODES]


def layout(np, inputs):
    def pad(v, n, fill):
        return np.concatenate([v, np.full((n - v.shape[0],) + v.shape[1:], fill, v.dtype)])

    def by_partition(v):
        return np.ascontiguousarray(v.reshape(NG, P, T).transpose(1, 0, 2).reshape(P, NT))

    given = {k: np.asarray(v) for k, v in inputs.items()}
    arrays = {
        "x": pad(given["x"], NP, 0),
        "src": by_partition(pad(given["src"], EP, NODES)),
        "dst": by_partition(pad(given["dst"], EP, NODES)),
        "iw": by_partition(pad(given["edge_weight"], EP, 0)),
        "ow": by_partition(pad(given["edge_weight_n2"], EP, 0)),
        "edge_attr": np.ascontiguousarray(
            pad(given["edge_attr_64"], (NG + 1) * GE, 0).reshape(NG + 1, P, T, EC).transpose(3, 0, 2, 1)
            .reshape(EC, (NG + 1) * GE)),
        "eps": given["L0_gnn_eps"].reshape(1),
    }
    for k in ("ee_w1", "ee_b1", "ee_w2", "ee_b2", "w1", "b1", "g1", "be1", "w2", "b2", "g2", "be2", "w3", "b3",
              "bn_g", "bn_b"):
        arrays[k] = given["L0_gnn_" + k]
    for k in ("gamma", "beta", "W_in", "b_in", "W_out", "b_out", "W_x2i", "b_x2i", "W_h2h"):
        arrays[k] = given["L1_gnn_" + k]
    for k in ("g1", "be1", "g2", "be2", "gamma", "beta"):
        arrays[k] = np.ascontiguousarray(arrays[k].reshape(-1, P).T)
    return arrays
```

```python
from contextlib import ExitStack, contextmanager

import concourse.bass as bass
from concourse import mybir

P = 128
ALU = mybir.AluOpType
ACT = mybir.ActivationFunctionType
F32 = mybir.dt.float32
I32 = mybir.dt.int32
AX = mybir.AxisListType.X

NODES = 6250
EDGES = 206250
C = 256
EC = 64
H = 1024
CC = C // P
HC = H // P
NB = -(-NODES // P)
NP = NB * P
LAST = NODES - (NB - 1) * P
T = 4
GE = T * P
U = 4
NG = -(-EDGES // (GE * U)) * U
NT = NG * T
EP = NG * GE
SG = NG + NB - 1
SG = -(-SG // U) * U
PAD_DMAS = 16
STEP_1 = (1, 1, 1, 2)
SCATTERED_1 = NG // U * sum(STEP_1)
ST = 11
assert len(STEP_1) == U and (NT - SCATTERED_1) % ST == 0
LN_EPS = 1e-5
BUCKET_SHIFT = 7
GROUP_SHIFT = 9
assert 1 << BUCKET_SHIFT == P and 1 << GROUP_SHIFT == GE


def gnn_kernel(nc, a, out):
    with ExitStack() as whole:
        def scratch(name, shape, dt):
            return nc.dram_tensor(name, shape, dt, kind="Internal").ap()

        dram = {
            "x_plus_b2": scratch("x_plus_b2", (NP, C), F32),
            "edge_slot": scratch("edge_slot", (P, NT), I32),
            "edge_record": scratch("edge_record", (P, NT * 4), F32),
            "sorted_record": scratch("sorted_record", (SG * GE, 4), F32),
            "dst_windows": scratch("dst_windows", (NG, 2), I32),
            "sorted_bucket": scratch("sorted_bucket", (P, U), I32),
            "feat_in": scratch("feat_in", (NP, C), F32),
            "feat_out": scratch("feat_out", (NP, C), F32),
            "x1": scratch("x1", (P, NB * C), F32),
            "hT": scratch("hT", (P, NB * C), F32),
        }
        sb = lambda name, shape, dt=F32: whole.enter_context(nc.sbuf_tensor(name, shape, dt))
        t = {
            "acc": sb("acc", [P, NB, 2 * C]),
            "ident": sb("ident", [P, P]),
            "dstf": sb("dstf", [P, NT + T]),
            "windows": sb("windows", [1, 2 * (NG + 1)], I32),
            "sorted_bucket": sb("sorted_bucket_sb", [1, SG + U], I32),
        }
        prepare(nc, a, dram, t)
        sum_over_dst(nc, a, dram, t, first=True)
        node_network(nc, a, dram, t)
        make_tables(nc, a, dram, t)
        sum_over_dst(nc, a, dram, t, first=False)
        sum_over_src_and_gates(nc, a, dram, t, out)


class Chain:

    def __init__(self, engine, sem):
        self.engine, self.sem, self.before, self.steps = engine, sem, 0, 0

    def then(self, ins):
        self.steps += 1
        ins.then_inc(self.sem, 1)
        self.engine.wait_ge(self.sem, self.before + self.steps)

    def at(self, before):
        self.before, self.steps = before, 0

    @contextmanager
    def loop(self, engine, start, end, per):
        began = self.steps
        with engine.Fori(start, end) as i:
            self.before = (i - start) * per
            yield i
        assert self.steps - began == per, self.steps - began
        self.before, self.steps = 0, began + per * (end - start)


class Names:

    def __init__(self, nc, stage, stack):
        self.nc, self.stage, self.stack = nc, stage, stack

    def sb(self, name, shape, dt=F32):
        return self.stack.enter_context(self.nc.sbuf_tensor(f"{self.stage}_{name}", shape, dt))

    def ps(self, name, shape, dt=F32):
        return self.stack.enter_context(self.nc.psum_tensor(f"{self.stage}_{name}", shape, dt))

    def sem(self, name):
        return self.stack.enter_context(self.nc.semaphore(f"{self.stage}_{name}"))


def row(v):
    return v.partition_broadcast(P)


def prepare(nc, a, dram, t):
    acc, dstf, ident = t["acc"], t["dstf"], t["ident"]
    with ExitStack() as s:
        n = Names(nc, "prep", s)
        srci = n.sb("srci", [P, NT], I32)
        srcblk = n.sb("srcblk", [P, NT])
        mask = n.sb("mask", [P, NT])
        scan = n.sb("scan", [P, NT])
        slot = n.sb("slot", [P, NT])
        dsti = scan[:].bitcast(I32)
        dstblk, ow = mask, slot
        rec = n.sb("rec", [P, NT, 4])
        b1 = n.sb("b1", [P, C])
        b2 = n.sb("b2", [P, C])
        eps = n.sb("eps", [P, 1])
        lohi = n.sb("lohi", [P, 2, NG])
        ones = n.sb("ones", [P, P])
        before = n.sb("before", [P, P])
        count = n.sb("count", [P, NB])
        kcol = n.sb("kcol", [P, NB])
        total_i, zero = n.sb("total_i", [P, NB], I32), n.sb("zero", [P, NB])
        groups = n.sb("groups", [P, NB])
        ends = n.sb("ends", [P, NB])
        offset = n.sb("offset", [P, NB])
        gid = n.sb("gid", [P, U])
        cmp = n.sb("cmp", [P, U, NB])
        bucket = n.sb("bucket", [P, U])
        bucket_i = n.sb("bucket_i", [P, U], I32)
        QG = NG // 4
        lohi_r = n.sb("lohi_r", [QG, 4, 2])
        lohi_i = n.sb("lohi_i", [QG, 4, 2], I32)
        tick = n.sb("tick", [1, 1])
        pad_rec = n.sb("pad_rec", [P, SG * GE // P // PAD_DMAS, 4])
        ps_count = n.ps("ps_count", [P, 2, 512])
        ps_t = n.ps("ps_t", [P, 2, 512])

        loaded, x_loaded = n.sem("loaded"), n.sem("x_loaded")
        iotas, ident0, pool_done = n.sem("iotas"), n.sem("ident0"), n.sem("pool_done")
        dve = n.sem("dve")
        counted, prefixed = n.sem("counted"), n.sem("prefixed")
        ranges, turned, turned_read = n.sem("ranges"), n.sem("turned"), n.sem("turned_read")
        slot_step = n.sem("slot_step")
        slots_ready, rec_ready = n.sem("slots_ready"), n.sem("rec_ready")
        small_ready, acc_ready, xb_ready = n.sem("small_ready"), n.sem("acc_ready"), n.sem("xb_ready")
        pad_ready = n.sem("pad_ready")
        xb_stored = n.sem("xb_stored")
        written, tables = n.sem("written"), n.sem("tables")
        block = s.enter_context(nc.Block())

        @block.sync
        def _(sp):
            sp.dma_start(srci[:], a["src"]).then_inc(loaded, 16)
            sp.dma_start(dsti, a["dst"]).then_inc(loaded, 16)
            sp.dma_start(ow[:], a["ow"]).then_inc(loaded, 16)
            sp.dma_start(b1[:], row(a["ee_b1"])).then_inc(loaded, 16)
            sp.dma_start(b2[:], row(a["ee_b2"])).then_inc(loaded, 16)
            sp.dma_start(eps[:], row(a["eps"])).then_inc(loaded, 16)
            sp.dma_start(acc[:, :, 0:C], a["x"].rearrange("(b p) c -> p b c", p=P)).then_inc(x_loaded, 16)
            sp.wait_ge(pad_ready, 1)
            for q in range(PAD_DMAS):
                sp.dma_start(dram["sorted_record"].rearrange("(q p n) w -> q p (n w)", q=PAD_DMAS, p=P)[q],
                             pad_rec[:].rearrange("p n w -> p (n w)")).then_inc(written, 16)
            sp.wait_ge(small_ready, 1)
            sp.dma_start(dram["sorted_bucket"], bucket_i[:]).then_inc(tables, 16)
            sp.wait_ge(small_ready, 2)
            sp.dma_start(dram["dst_windows"].rearrange("(q g) w -> g q w", q=4), lohi_i[:]).then_inc(tables, 16)
            sp.wait_ge(tables, 32)
            flat = dram["sorted_bucket"].rearrange("p u -> (p u)")
            sp.dma_start(t["sorted_bucket"][0:1, 0:SG], flat[0:SG].unsqueeze(0)).then_inc(written, 16)
            sp.dma_start(t["windows"][0:1, 0:2 * NG],
                         dram["dst_windows"].rearrange("g w -> (g w)").unsqueeze(0)).then_inc(written, 16)
            sp.wait_ge(rec_ready, 1)
            sp.dma_start(dram["edge_record"], rec[:].rearrange("p n w -> p (n w)")).then_inc(written, 16)
            sp.wait_ge(slots_ready, 1)
            sp.dma_start(dram["edge_slot"], srci[:]).then_inc(written, 16)
            sp.wait_ge(written, 16 * (PAD_DMAS + 4))

        @block.gpsimd
        def _(pool):
            nc.gpsimd.memset(ident[:], 0.0).then_inc(ident0, 1)
            nc.gpsimd.memset(before[:], 1.0).then_inc(ident0, 1)
            nc.gpsimd.iota(kcol[:], pattern=[[1, NB]], base=0, channel_multiplier=0,
                           allow_small_or_imprecise_dtypes=True).then_inc(iotas, 1)
            nc.gpsimd.iota(gid[:], pattern=[[1, U]], base=0, channel_multiplier=U,
                           allow_small_or_imprecise_dtypes=True).then_inc(iotas, 1)
            pool.wait_ge(ident0, 2)
            nc.gpsimd.affine_select(out=ident[:], in_=ident[:], compare_op=ALU.not_equal, fill=1.0, base=0,
                                    pattern=[[-1, P]], channel_multiplier=1).then_inc(pool_done, 1)
            nc.gpsimd.affine_select(out=before[:], in_=before[:], compare_op=ALU.is_gt, fill=0.0, base=0,
                                    pattern=[[1, P]], channel_multiplier=-1).then_inc(pool_done, 1)

        @block.tensor
        def _(pe):
            pe.wait_ge(pool_done, 2)
            pe.wait_ge(ranges, 2)
            for k in range(8):
                if k >= 2:
                    pe.wait_ge(turned_read, k - 1)
                nc.tensor.transpose(ps_t[0:QG, k % 2, 0:P], lohi[:, k % 2, (k // 2) * QG:(k // 2 + 1) * QG],
                                    ident[:]).then_inc(turned, 1)
            pe.wait_ge(counted, NB)
            nc.tensor.matmul(ps_count[:, 0, 0:NB], before[:], count[:], start=True, stop=True)
            nc.tensor.matmul(ps_count[:, 1, 0:NB], ones[:], count[:], start=True, stop=True).then_inc(prefixed, 1)

        @block.scalar
        def _(act):
            act.wait_ge(loaded, 96)
            act.wait_ge(x_loaded, 16)
            act.wait_ge(xb_ready, NB)
            act.dma_start(dram["x_plus_b2"].rearrange("(b p) c -> p b c", p=P), acc[:, :, C:2 * C]).then_inc(xb_stored, 16)
            act.wait_ge(xb_stored, 16)
            for b in range(NB):
                act.wait_ge(acc_ready, b + 1)
                nc.scalar.activation(acc[:, b, C:2 * C], b1[:], ACT.Relu)

        @block.vector
        def _(v):
            steps = [0]

            def then(ins):
                steps[0] += 1
                ins.then_inc(dve, 1)
                v.wait_ge(dve, steps[0])

            v.memset(pad_rec[:, :, 0].bitcast(I32), NODES)
            v.memset(pad_rec[:, :, 1], -1.0)
            v.memset(pad_rec[:, :, 2:4], 0.0).then_inc(pad_ready, 1)
            v.memset(ones[:], 1.0)
            v.memset(zero[:], 0.0)
            v.memset(dstf[:, NT:], -1.0)
            v.memset(rec[:, :, 3], 0.0)
            v.memset(t["sorted_bucket"][:, SG:], 0)
            then(v.memset(t["windows"][:, 2 * NG:], 0))
            v.wait_ge(loaded, 96)
            v.tensor_copy(dstf[:, 0:NT], dsti)
            v.tensor_copy(rec[:, :, 1], srci[:])
            v.tensor_copy(rec[:, :, 2], ow[:])
            then(v.tensor_copy(rec[:, :, 0].bitcast(I32), dsti))
            v.tensor_single_scalar(srci[:], srci[:], BUCKET_SHIFT, op=ALU.arith_shift_right)
            then(v.tensor_single_scalar(dsti, dsti, BUCKET_SHIFT, op=ALU.arith_shift_right))
            v.tensor_copy(srcblk[:], srci[:]).then_inc(rec_ready, 1)
            then(v.tensor_copy(dstblk[:], dsti))
            by_group = dstblk[:].rearrange("p (g j) -> p g j", j=T)
            v.tensor_reduce(lohi[:, 0, :], by_group, AX, ALU.min).then_inc(ranges, 1)
            v.tensor_reduce(lohi[:, 1, :], by_group, AX, ALU.max).then_inc(ranges, 1)
            for k in range(8):
                v.wait_ge(turned, k + 1)
                v.tensor_reduce(lohi_r[:, k // 2, k % 2:k % 2 + 1], ps_t[0:QG, k % 2, 0:P], AX,
                                ALU.max if k % 2 else ALU.min).then_inc(turned_read, 1)
            v.wait_ge(iotas, 2)
            for k in range(NB):
                if k:
                    v.wait_ge(counted, k)
                v.tensor_scalar(scan[:], srcblk[:], float(k), None, ALU.is_equal, ALU.add,
                                accum_out=count[:, k:k + 1]).then_inc(counted, 1)
            v.wait_ge(prefixed, 1)
            then(v.tensor_scalar(groups[:], ps_count[:, 1, 0:NB], float(GE - 1), None, ALU.add))
            then(v.tensor_copy(total_i[:], groups[:]))
            then(v.tensor_single_scalar(total_i[:], total_i[:], GROUP_SHIFT, op=ALU.arith_shift_right))
            then(v.tensor_copy(groups[:], total_i[:]))
            then(v.tensor_tensor_scan(ends[:], zero[:], groups[:], 0.0, ALU.add, ALU.add))
            then(v.tensor_tensor(offset[:], ends[:], groups[:], ALU.subtract))
            then(v.tensor_scalar(offset[:], offset[:], float(GE), -1.0, ALU.mult, ALU.add))
            then(v.tensor_tensor(offset[:], offset[:], ps_count[:, 0, 0:NB], ALU.add))
            then(v.tensor_tensor(cmp[:, :, 0:NB - 1], gid[:].unsqueeze(2).to_broadcast([P, U, NB - 1]),
                                 ends[:, 0:NB - 1].unsqueeze(1).to_broadcast([P, U, NB - 1]), ALU.is_ge))
            then(v.tensor_reduce(bucket[:], cmp[:, :, 0:NB - 1], AX, ALU.add))
            v.tensor_copy(bucket_i[:], bucket[:]).then_inc(small_ready, 1)
            v.wait_ge(turned_read, 8)
            v.tensor_copy(lohi_i[:], lohi_r[:]).then_inc(small_ready, 1)
            with v.Fori(0, NB) as k:
                v.tensor_scalar(mask[:], srcblk[:], kcol[:, bass.ds(k, 1)], None, ALU.is_equal).then_inc(slot_step, 1)
                v.wait_ge(slot_step, k * 3 + 1)
                v.tensor_tensor_scan(scan[:], mask[:], mask[:], offset[:, bass.ds(k, 1)], ALU.add,
                                     ALU.bypass).then_inc(slot_step, 1)
                v.wait_ge(slot_step, k * 3 + 2)
                v.memset(tick[:], 0.0)
                v.copy_predicated(slot[:], mask[:].bitcast(I32), scan[:]).then_inc(slot_step, 1)
                v.wait_ge(slot_step, k * 3 + 3)
            v.tensor_copy(srci[:], slot[:]).then_inc(slots_ready, 1)
            v.wait_ge(x_loaded, 16)
            for b in range(NB):
                v.tensor_tensor(acc[:, b, C:2 * C], acc[:, b, 0:C], b2[:], ALU.add).then_inc(xb_ready, 1)
            then(v.tensor_scalar(eps[:], eps[:], 1.0, None, ALU.add))
            v.wait_ge(xb_ready, NB)
            for b in range(NB):
                v.scalar_tensor_tensor(out=acc[:, b, 0:C], in0=acc[:, b, 0:C], scalar=eps[:, 0:1],
                                       in1=acc[:, b, C:2 * C], op0=ALU.mult, op1=ALU.add).then_inc(acc_ready, 1)


def sum_over_dst(nc, a, dram, t, first):
    acc, dstf, windows = t["acc"], t["dstf"], t["windows"]
    parts = 2 if first else 1
    table = dram["x_plus_b2"] if first else dram["feat_in"]
    with ExitStack() as s:
        n = Names(nc, "sum1" if first else "sum2", s)
        iota = n.sb("iota", [P, NP])
        index = n.sb("index", [P, U, T], I32)
        rows = n.sb("rows", [P, U, T, C])
        onehot = n.sb("onehot", [P, 2, T, P])
        onehot_x = n.sb("onehot_x", [P, T, P])
        if first:
            attr = n.sb("attr", [EC + 1, U, T, P])
            w1 = n.sb("w1", [EC + 1, C])
            hidden = n.sb("hidden", [P, 2, T, C])
            ps_h = n.ps("ps_h", [P, 2, 2, C])
            ST_1 = [STEP_1[0] + STEP_1[1], STEP_1[2] + STEP_1[3]]
            slot = [n.sb(f"slot{k}", [P, ST_1[k]], I32) for k in range(2)]
            record = [n.sb(f"record{k}", [P, ST_1[k], 4]) for k in range(2)]
            slots_loaded = [n.sem(f"slots_loaded{k}") for k in range(2)]
            scattered = [n.sem(f"scattered{k}") for k in range(2)]
        else:
            iw = n.sb("iw", [P, NT + T])
        ps = n.ps("ps", [P, 2, 2, 512])
        ps_x = n.ps("ps_x", [P, 2, 512])

        consts, iota_set = n.sem("consts"), n.sem("iota_set")
        index_loaded = [n.sem(f"index_loaded{u}") for u in range(U)]
        attr_loaded = [n.sem(f"attr_loaded{u}") for u in range(U)]
        gathered = [n.sem(f"gathered{u}") for u in range(U)]
        ones_set = n.sem("ones_set")
        turns, turns_v = n.sem("turns"), n.sem("turns_v")
        onehot_ready, summed, ps_free = n.sem("onehot_ready"), n.sem("summed"), n.sem("ps_free")
        onehot_x_ready, summed_x, added_x = n.sem("onehot_x_ready"), n.sem("summed_x"), n.sem("added_x")
        group_done = n.sem("group_done")
        hidden_ps = n.sem("hidden_ps")
        hidden_ready = n.sem("hidden_ready")
        block = s.enter_context(nc.Block())

        @block.sync
        def _(sp):
            if first:
                sp.dma_start(w1[0:EC, :], a["ee_w1"]).then_inc(consts, 16)
                sp.dma_start(w1[EC:EC + 1, :], a["ee_b1"].unsqueeze(0)).then_inc(consts, 16)
            else:
                sp.dma_start(iw[:, 0:NT], a["iw"]).then_inc(consts, 16)

            def load_attr(g, u):
                sp.wait_ge(hidden_ps, g * 2 + 2)
                sp.dma_start(attr[0:EC, u, :, :], a["edge_attr"].rearrange("e (g j p) -> e g j p", j=T, p=P)
                             [:, bass.ds(g, 1), :, :].rearrange("e g j p -> e (g j p)")
                             ).then_inc(attr_loaded[u], 16)

            def load_records(i, k):
                tile = i * (ST_1[0] + ST_1[1]) + k * ST_1[0]
                sp.dma_start(slot[k][:], dram["edge_slot"][:, bass.ds(tile, ST_1[k])]).then_inc(slots_loaded[k], 16)
                sp.dma_start(record[k][:].rearrange("p t w -> p (t w)"),
                             dram["edge_record"][:, bass.ds(tile * 4, 4 * ST_1[k])]).then_inc(slots_loaded[k], 16)

            if first:
                load_records(0, 0)
            with sp.Fori(0, NG // U) as i:
                for u in range(U):
                    g = i * U + u
                    sp.wait_ge(group_done, g + 1)
                    sp.dma_start(index[:, u, :], a["src"][:, bass.ds(g * T, T)]).then_inc(index_loaded[u], 16)
                    if first:
                        load_attr(g, u)
                        if u == 1:
                            sp.wait_ge(scattered[1], i * (16 * ST_1[1]))
                            load_records(i, 1)
                        if u == 3:
                            sp.wait_ge(scattered[0], i * (16 * ST_1[0]) + 16 * ST_1[0])
                            load_records(i + 1, 0)
            if first:
                load_attr(NG, 0)
                sp.wait_ge(slots_loaded[0], 32 * (NG // U + 1))

        @block.gpsimd
        def _(pool):
            nc.gpsimd.iota(iota[:], pattern=[[1, NP]], base=0, channel_multiplier=0,
                           allow_small_or_imprecise_dtypes=True).then_inc(iota_set, 1)
            with pool.Fori(0, NG // U) as i:
                for u in range(U):
                    pool.wait_ge(index_loaded[u], i * 16 + 16)
                    pool.sem_inc(turns, 1)
                    for j in range(T):
                        pool.indirect_dma_start(
                            out=rows[:, u, j, :], out_offset=None, in_=table,
                            in_offset=bass.IndirectOffsetOnAxis(ap=index[:, u, j:j + 1], axis=0),
                        ).then_inc(gathered[u], 16)
                    if first:
                        k = u // 2
                        if u % 2 == 0:
                            pool.wait_ge(slots_loaded[k], i * 32 + 32)
                            pool.sem_inc(turns, 1)
                        for q in range(STEP_1[u]):
                            q += STEP_1[u - 1] if u % 2 else 0
                            pool.indirect_dma_start(
                                out=dram["sorted_record"],
                                out_offset=bass.IndirectOffsetOnAxis(ap=slot[k][:, q:q + 1], axis=0),
                                in_=record[k][:, q, :], in_offset=None,
                            ).then_inc(scattered[k], 16)
            if first:
                for k in range(2):
                    pool.wait_ge(scattered[k], NG // U * 16 * ST_1[k])

        @block.tensor
        def _(pe):
            def edge_network(g, u, count):
                pe.wait_ge(attr_loaded[u], count * 16)
                for m in range(2):
                    pe.wait_ge(hidden_ready, g * 2 + m + 1)
                    for j in range(2):
                        mm = nc.tensor.matmul(ps_h[:, m, j, :], attr[:, u, 2 * m + j, :], w1[:],
                                              start=j == 0, stop=j == 1, skip_group_check=True)
                    mm.then_inc(hidden_ps, 1)

            def window(target, hot, u, hu):
                for part in range(parts):
                    for j in range(T):
                        data = rows[:, u, j, :] if part == 0 else hidden[:, hu, j, :]
                        mm = nc.tensor.matmul(target[:, part, 0:C], hot[:, j, :], data,
                                              start=j == 0, stop=j == T - 1)
                return mm

            if first:
                pe.sem_inc(hidden_ps, 2 * U)
                pe.wait_ge(consts, 32)
                pe.wait_ge(ones_set, 1)
                edge_network(0, 0, 1)
            further = pe.alloc_register(f"further_windows_{parts}")
            pe.reg_mov(further, 0)
            with pe.Fori(0, NG // U) as i:
                for u in range(U):
                    g = i * U + u
                    low = pe.value_load(windows[0:1, bass.ds(g * 2, 1)], min_val=0, max_val=NB - 1)
                    high = pe.value_load(windows[0:1, bass.ds(g * 2 + 1, 1)], min_val=0, max_val=NB - 1)
                    if first:
                        edge_network(g + 1, (u + 1) % U, i + 1 + (u + 1) // U)
                        pe.wait_ge(hidden_ready, g * 2 + 4)
                    pe.wait_ge(gathered[u], i * 16 * T + 16 * T)
                    pe.wait_ge(onehot_ready, g + 1)
                    pe.wait_ge(ps_free, g + 1)
                    window(ps[:, u % 2], onehot[:, u % 2], u, u % 2).then_inc(summed, 1)
                    with pe.If(low < high):
                        with pe.Fori(low, high) as b:
                            pe.reg_add(further, further, 1)
                            pe.wait_ge(onehot_x_ready, pe.snap(further, min_val=1, max_val=NG * NB))
                            window(ps_x, onehot_x, u, u % 2).then_inc(summed_x, 1)

        @block.scalar
        def _(act):
            if first:
                act.preload_act_table(ACT.Relu)
                act.sem_inc(hidden_ready, 2)

                def relu(g, hu):
                    act.wait_ge(group_done, g + 3)
                    for m in range(2):
                        act.wait_ge(hidden_ps, g * 2 + m + 1 + 2 * U)
                        nc.scalar.activation(hidden[:, hu, 2 * m:2 * m + 2, :], ps_h[:, m, :, :],
                                             ACT.Relu).then_inc(hidden_ready, 1)

                with act.Fori(0, NG // U) as i:
                    for u in range(U):
                        relu(i * U + u, u % 2)
                relu(NG, 0)

        @block.vector
        def _(v):
            v.sem_inc(group_done, U)
            v.sem_inc(ps_free, 2)
            if first:
                v.memset(attr[EC:EC + 1, :, :, :], 1.0).then_inc(ones_set, 1)
            else:
                v.wait_ge(consts, 16)
                v.memset(iw[:, NT:], 0.0).then_inc(ones_set, 1)
                v.wait_ge(ones_set, 1)
            further = v.alloc_register(f"further_windows_{parts}")
            v.reg_mov(further, 0)

            def one_hots(target, g, b):
                for j in range(T):
                    column = bass.ds(g * T + j, 1)
                    block_nodes = iota[:, bass.ds(b * P, P)]
                    if first:
                        ins = v.tensor_scalar(target[:, j, :], block_nodes, dstf[:, column], None, ALU.is_equal)
                    else:
                        ins = v.tensor_scalar(target[:, j, :], block_nodes, dstf[:, column], iw[:, column],
                                              ALU.is_equal, ALU.mult)
                return ins

            def add(source, b):
                sums = acc[:, bass.ds(b, 1), :].rearrange("p b (k c) -> p (b k) c", k=2)[:, 0:parts, :]
                return v.tensor_tensor(sums, sums, source[:, 0:parts, 0:C], ALU.add)

            v.wait_ge(iota_set, 1)
            low = v.value_load(windows[0:1, 0:1], min_val=0, max_val=NB - 1)
            one_hots(onehot[:, 0], 0, low).then_inc(onehot_ready, 1)
            with v.Fori(0, NG // U) as i:
                for u in range(U):
                    g = i * U + u
                    low = v.value_load(windows[0:1, bass.ds(g * 2, 1)], min_val=0, max_val=NB - 1)
                    high = v.value_load(windows[0:1, bass.ds(g * 2 + 1, 1)], min_val=0, max_val=NB - 1)
                    low_next = v.value_load(windows[0:1, bass.ds(g * 2 + 2, 1)], min_val=0, max_val=NB - 1)
                    one_hots(onehot[:, (u + 1) % 2], g + 1, low_next).then_inc(onehot_ready, 1)
                    v.wait_ge(summed, g + 1)
                    v.wait_ge(ps_free, g + 2)
                    add(ps[:, u % 2], low).then_inc(ps_free, 1)
                    with v.If(low < high):
                        with v.Fori(low + 1, high + 1) as b:
                            one_hots(onehot_x, g, b).then_inc(onehot_x_ready, 1)
                            v.reg_add(further, further, 1)
                            done = v.snap(further, min_val=1, max_val=NG * NB)
                            v.wait_ge(summed_x, done)
                            add(ps_x, b).then_inc(added_x, 1)
                            v.wait_ge(added_x, done)
                    v.sem_inc(group_done, 1)


def node_network(nc, a, dram, t):
    acc, ident = t["acc"], t["ident"]
    with ExitStack() as s:
        n = Names(nc, "net", s)
        w_ee = n.sb("w_ee", [P, CC, C])
        w1 = n.sb("w1", [P, CC, H])
        w2 = n.sb("w2", [P, HC, H])
        w3 = n.sb("w3", [P, HC, C])
        bias = n.sb("bias", [P, 2, H])
        bias3 = n.sb("bias3", [P, C])
        bn_g, bn_b = n.sb("bn_g", [P, C]), n.sb("bn_b", [P, C])
        gain = n.sb("gain", [P, 2, HC])
        shift = n.sb("shift", [P, 2, HC])
        sums = n.sb("sums", [P, 2 * C])
        hid_t = n.sb("hid_t", [P, CC, P])
        in_t = n.sb("in_t", [P, CC, P])
        z = n.sb("z", [P, H])
        act_t = n.sb("act_t", [P, 2, HC, P])
        stats = n.sb("stats", [P, 2, 6])
        mv = n.sb("mv", [P, 2])
        std, rstd, eps = n.sb("std", [P, 1]), n.sb("rstd", [P, 1]), n.sb("eps", [P, 1])
        x_in = n.sb("x_in", [P, C])
        y = n.sb("y", [P, C])
        x1 = n.sb("x1", [P, C])
        index = n.sb("index", [P, 2, ST], I32)
        record = n.sb("record", [P, 2, ST, 4])
        ps_t = n.ps("ps_t", [P, 1, 512])
        ps_z = n.ps("ps_z", [P, 2, 512])
        ps_a = n.ps("ps_a", [P, 2, 512])
        ps_in = n.ps("ps_in", [P, 512])
        ps_y = n.ps("ps_y", [P, 512])
        ps_x = n.ps("ps_x", [P, 512])

        loaded = n.sem("loaded")
        x_loaded = n.sem("x_loaded")
        sums_ready, hid_turned, hid_copied = n.sem("sums_ready"), n.sem("hid_turned"), n.sem("hid_copied")
        in_summed, in_copied = n.sem("in_summed"), n.sem("in_copied")
        eps_set = n.sem("eps_set")
        z_summed, z_read = n.sem("z_summed"), n.sem("z_read")
        z_ready, z_turned, act_ready = n.sem("z_ready"), n.sem("z_turned"), n.sem("act_ready")
        var_ready, std_ready = n.sem("var_ready"), n.sem("std_ready")
        y_summed, y_read = n.sem("y_summed"), n.sem("y_read")
        x1_ready, x1_turned, x1_stored = n.sem("x1_ready"), n.sem("x1_turned"), n.sem("x1_stored")
        dve = n.sem("dve")
        slots_loaded = [n.sem("slots_loaded0"), n.sem("slots_loaded1")]
        scattered = [n.sem("scattered0"), n.sem("scattered1")]
        turns, turns_v = n.sem("turns"), n.sem("turns_v")
        block = s.enter_context(nc.Block())
        LOADS = 13
        steps = (NT - SCATTERED_1) // ST

        @block.sync
        def _(sp):
            sp.dma_start(w_ee[:], a["ee_w2"].rearrange("(c p) n -> p c n", p=P)).then_inc(loaded, 16)
            sp.dma_start(w1[:], a["w1"].rearrange("(c p) n -> p c n", p=P)).then_inc(loaded, 16)
            sp.dma_start(bias[:, 0, :], row(a["b1"])).then_inc(loaded, 16)
            sp.dma_start(bias[:, 1, :], row(a["b2"])).then_inc(loaded, 16)
            for k, (g, be) in enumerate((("g1", "be1"), ("g2", "be2"))):
                sp.dma_start(gain[:, k, :], a[g]).then_inc(loaded, 16)
                sp.dma_start(shift[:, k, :], a[be]).then_inc(loaded, 16)
            sp.dma_start(w2[:], a["w2"].rearrange("(c p) n -> p c n", p=P)).then_inc(loaded, 16)
            sp.dma_start(w3[:], a["w3"].rearrange("(c p) n -> p c n", p=P)).then_inc(loaded, 16)
            sp.dma_start(bias3[:], row(a["b3"])).then_inc(loaded, 16)
            sp.dma_start(bn_g[:], row(a["bn_g"])).then_inc(loaded, 16)
            sp.dma_start(bn_b[:], row(a["bn_b"])).then_inc(loaded, 16)
            def load(q, k):
                tile = q * ST + SCATTERED_1
                sp.dma_start(index[:, k, :], dram["edge_slot"][:, bass.ds(tile, ST)]
                             ).then_inc(slots_loaded[k], 16)
                sp.dma_start(record[:, k, :, :].rearrange("p t w -> p (t w)"),
                             dram["edge_record"][:, bass.ds(tile * 4, 4 * ST)]
                             ).then_inc(slots_loaded[k], 16)

            for k in range(2):
                load(k, k)
            with sp.Fori(1, steps // 2) as i:
                for k in range(2):
                    sp.wait_ge(scattered[k], i * (16 * ST))
                    load(i * 2 + k, k)
            if steps % 2:
                sp.wait_ge(scattered[0], steps // 2 * 16 * ST)
                load(steps - 1, 0)

        @block.gpsimd
        def _(pool):
            def scatter(i, k):
                pool.wait_ge(slots_loaded[k], i * 32 + 32)
                pool.sem_inc(turns, 1)
                for j in range(ST):
                    pool.indirect_dma_start(
                        out=dram["sorted_record"],
                        out_offset=bass.IndirectOffsetOnAxis(ap=index[:, k, j:j + 1], axis=0),
                        in_=record[:, k, j, :], in_offset=None,
                    ).then_inc(scattered[k], 16)

            with pool.Fori(0, steps // 2) as i:
                for k in range(2):
                    scatter(i, k)
            if steps % 2:
                scatter(steps // 2, 0)
            for k in range(2):
                pool.wait_ge(scattered[k], (steps + 1 - k) // 2 * 16 * ST)

        @block.tensor
        def _(pe):
            def network_input(b):
                pe.wait_ge(sums_ready, b + 1)
                for c in range(CC):
                    mm = nc.tensor.transpose(ps_t[:, 0, c * P:(c + 1) * P], sums[:, C + c * P:C + (c + 1) * P], ident[:])
                mm.then_inc(hid_turned, 1)
                pe.wait_ge(hid_copied, b + 1)
                for c in range(CC):
                    target = ps_in[:, c * P:(c + 1) * P]
                    nc.tensor.matmul(target, sums[:, c * P:(c + 1) * P], ident[:], start=c == 0, stop=False,
                                     skip_group_check=True)
                    for k in range(CC):
                        mm = nc.tensor.matmul(target, w_ee[:, k, c * P:(c + 1) * P], hid_t[:, k, :], start=False,
                                              stop=k == CC - 1, skip_group_check=True)
                mm.then_inc(in_summed, 1)

            def hidden_layer(b, layer):
                pe.wait_ge(z_read, b * 2 + layer + 1)
                if layer == 0:
                    pe.wait_ge(in_copied, b + 1)
                    chunks, w = [in_t[:, c, :] for c in range(CC)], w1
                else:
                    chunks, w = [act_t[:, 0, c, :] for c in range(HC)], w2
                for m in range(2):
                    for c, x in enumerate(chunks):
                        if layer == 1 and m == 0:
                            pe.wait_ge(act_ready, b * 2 * HC + HC // 2 + c + 2)
                        mm = nc.tensor.matmul(ps_z[:, m, :], x, w[:, c, m * 512:(m + 1) * 512], start=c == 0,
                                              stop=c == len(chunks) - 1)
                    mm.then_inc(z_summed, 1)

            def turn_hidden(b, layer):
                pe.wait_ge(z_ready, b * 2 + layer + 1)
                for m in range(2):
                    pe.wait_ge(act_ready, (b * 2 + layer) * HC + m * (HC // 2) + 1)
                    for c in range(HC // 2):
                        k = m * (HC // 2) + c
                        mm = nc.tensor.transpose(ps_a[:, m, c * P:(c + 1) * P], z[:, k * P:(k + 1) * P], ident[:])
                    mm.then_inc(z_turned, 1)

            def output_layer(b):
                pe.wait_ge(y_read, b + 1)
                for c in range(HC):
                    pe.wait_ge(act_ready, b * 2 * HC + HC + HC // 2 + c + 2)
                    mm = nc.tensor.matmul(ps_y[:, 0:C], act_t[:, 1, c, :], w3[:, c, :], start=c == 0, stop=c == HC - 1)
                mm.then_inc(y_summed, 1)

            def turn_x1(b):
                pe.wait_ge(x1_ready, b + 1)
                pe.wait_ge(x1_stored, b + 1)
                for c in range(CC):
                    mm = nc.tensor.transpose(ps_x[:, c * P:(c + 1) * P], x1[:, c * P:(c + 1) * P], ident[:])
                mm.then_inc(x1_turned, 1)

            def body(b, first=False, last=False):
                turn_hidden(b, 0)
                hidden_layer(b, 1)
                if not first:
                    turn_x1(b - 1)
                if not last:
                    network_input(b + 1)
                turn_hidden(b, 1)
                if not last:
                    hidden_layer(b + 1, 0)
                output_layer(b)

            pe.wait_ge(loaded, 16 * LOADS)
            network_input(0)
            hidden_layer(0, 0)
            body(0, first=True)
            with pe.Fori(1, NB - 1) as b:
                body(b)
            body(NB - 1, last=True)
            turn_x1(NB - 1)

        @block.scalar
        def _(act):
            act.preload_act_table(ACT.Sqrt)
            act.sem_inc(act_ready, HC // 2 + 1)
            act.sem_inc(x1_stored, 1)
            act.wait_ge(loaded, 16 * LOADS)

            def copy_sums(b):
                nc.scalar.activation(sums[:], acc[:, bass.ds(b, 1), :].rearrange("p b c -> p (b c)"),
                                     ACT.Copy).then_inc(sums_ready, 1)

            def copy_input(b):
                act.wait_ge(hid_turned, b + 1)
                nc.scalar.activation(hid_t[:].rearrange("p c n -> p (c n)"), ps_t[:, 0, 0:C], ACT.Copy
                                     ).then_inc(hid_copied, 1)
                act.wait_ge(in_summed, b + 1)
                nc.scalar.activation(in_t[:].rearrange("p c n -> p (c n)"), ps_in[:, 0:C], ACT.Copy
                                     ).then_inc(in_copied, 1)

            def activate(b, layer):
                for c in range(HC):
                    if c % (HC // 2) == 0:
                        act.wait_ge(z_turned, (b * 2 + layer) * 2 + c // (HC // 2) + 1)
                    nc.scalar.activation(act_t[:, layer, c, :],
                                         ps_a[:, c // (HC // 2), (c % (HC // 2)) * P:(c % (HC // 2) + 1) * P], ACT.Relu,
                                         bias=shift[:, layer, c:c + 1], scale=gain[:, layer, c:c + 1]
                                         ).then_inc(act_ready, 1)

            def load_x(b):
                act.dma_start(x_in[:], a["x"].rearrange("(b p) c -> p b c", p=P)[:, bass.ds(b, 1), :]
                              .rearrange("p b c -> p (b c)")).then_inc(x_loaded, 16)

            def root(number):
                act.wait_ge(var_ready, number + 1)
                nc.scalar.activation(std[:], mv[:, 1:2], ACT.Sqrt, bias=eps[:, 0:1]).then_inc(std_ready, 1)

            def store_x1(b):
                act.wait_ge(x1_turned, b + 1)
                nc.scalar.activation(acc[:, bass.ds(b, 1), C:2 * C].rearrange("p b c -> p (b c)"), ps_x[:, 0:C],
                                     ACT.Copy).then_inc(x1_stored, 1)

            def body(b, first=False, last=False):
                activate(b, 0)
                if not last:
                    act.wait_ge(in_summed, b + 1)
                    copy_sums(b + 1)
                if not first:
                    root(b * 4 - 1)
                    root(b * 4)
                    store_x1(b - 1)
                    load_x(b)
                if not last:
                    copy_input(b + 1)
                root(b * 4 + 1)
                activate(b, 1)
                if not last:
                    root(b * 4 + 2)

            load_x(0)
            copy_sums(0)
            copy_input(0)
            act.wait_ge(eps_set, 1)
            root(0)
            body(0, first=True)
            with act.Fori(1, NB - 1) as b:
                body(b)
            body(NB - 1, last=True)
            root(NB * 4 - 2)
            root(NB * 4 - 1)
            store_x1(NB - 1)

        @block.vector
        def _(v):
            chain = Chain(v, dve)
            v.sem_inc(z_read, 1)
            v.sem_inc(y_read, 1)
            v.memset(eps[:], LN_EPS).then_inc(eps_set, 1)
            v.wait_ge(loaded, 16 * LOADS)

            def normed(out_, in_, number):
                halves = -(-in_.shape[1] // 512)
                w = in_.shape[1] // halves
                for m in range(halves):
                    ins = v.bn_stats(stats[:, m, :], in_[:, m * w:(m + 1) * w])
                chain.then(ins)
                v.sem_inc(turns_v, 1)
                chain.then(v.bn_aggr(mv[:], stats[:, 0:halves, :].rearrange("p m s -> p (m s)")))
                v.sem_inc(var_ready, 1)
                v.wait_ge(std_ready, number + 1)
                chain.then(v.reciprocal(rstd[:], std[:]))
                return v.tensor_scalar(out_, in_, mv[:, 0:1], rstd[:, 0:1], ALU.subtract, ALU.mult)

            def hidden(b, layer):
                number = b * 2 + layer
                for m in range(2):
                    v.wait_ge(z_summed, number * 2 + m + 1)
                    ins = v.tensor_tensor(z[:, m * 512:(m + 1) * 512], ps_z[:, m, :],
                                          bias[:, layer, m * 512:(m + 1) * 512], ALU.add)
                ins.then_inc(z_read, 1)
                v.wait_ge(z_read, number + 2)
                normed(z[:], z[:], b * 4 + 1 if layer else b * 4 - 2 if not isinstance(b, int) or b else 0
                       ).then_inc(z_ready, 1)

            def output(b, last):
                v.wait_ge(y_summed, b + 1)
                v.tensor_tensor(y[:], ps_y[:, 0:C], bias3[:], ALU.add).then_inc(y_read, 1)
                v.wait_ge(y_read, b + 2)
                v.wait_ge(x_loaded, b * 16 + 16)
                chain.then(v.tensor_tensor(y[:], y[:], x_in[:], ALU.add))
                at = b * 4 + 3 - last
                chain.then(normed(y[:], y[:], at))
                chain.then(v.tensor_tensor(y[:], y[:], bn_g[:], ALU.mult))
                chain.then(v.tensor_tensor(y[:], y[:], bn_b[:], ALU.add))
                chain.then(v.scalar_tensor_tensor(out=y[:], in0=y[:], scalar=0.0, in1=x_in[:], op0=ALU.max, op1=ALU.add))
                normed(x1[:], y[:], at + 1).then_inc(x1_ready, 1)
                v.wait_ge(x1_ready, b + 1)
                v.tensor_copy(acc[:, bass.ds(b, 1), 0:C].rearrange("p b c -> p (b c)"), x1[:])

            def body(b, last=False):
                hidden(b, 1)
                if not last:
                    hidden(b + 1, 0)
                output(b, last)

            hidden(0, 0)
            body(0)
            with chain.loop(v, 1, NB - 1, 17) as b:
                body(b)
            body(NB - 1, last=True)


def make_tables(nc, a, dram, t):
    acc = t["acc"]
    with ExitStack() as s:
        n = Names(nc, "tab", s)
        w_io = n.sb("w_io", [P, CC, 2 * C])
        bias = n.sb("bias", [P, 2 * C])
        gamma, beta = n.sb("gamma", [P, CC]), n.sb("beta", [P, CC])
        stats = n.sb("stats", [P, CC, NB, 6])
        mv = n.sb("mv", [P, CC, 2])
        scale, shift = n.sb("scale", [P, CC]), n.sb("shift", [P, CC])
        B = 4
        assert NB % B == 1
        h_t = n.sb("h_t", [P, B, CC, P])
        feat = n.sb("feat", [P, B, 2 * C])
        ps = n.ps("ps", [P, B, 2 * C])
        loaded, x1_saved, dve, stats_done = n.sem("loaded"), n.sem("x1_saved"), n.sem("dve"), n.sem("stats_done")
        h_ready, summed, feat_ready = n.sem("h_ready"), n.sem("summed"), n.sem("feat_ready")
        var_ready, std_ready = n.sem("var_ready"), n.sem("std_ready")
        stored = [n.sem(f"stored{k}") for k in range(B)]
        block = s.enter_context(nc.Block())
        LD = 6

        def blocks(eng, body):
            for k in range(B):
                body(k, k, 0)
            with eng.Fori(1, NB // B) as i:
                for k in range(B):
                    body(i * B + k, k, i)
            body(NB - 1, 0, NB // B)

        @block.sync
        def _(sp):
            sp.dma_start(w_io[:, :, 0:C], a["W_in"].rearrange("(c p) n -> p c n", p=P)).then_inc(loaded, 16)
            sp.dma_start(w_io[:, :, C:2 * C], a["W_out"].rearrange("(c p) n -> p c n", p=P)).then_inc(loaded, 16)
            sp.dma_start(bias[:, 0:C], row(a["b_in"])).then_inc(loaded, 16)
            sp.dma_start(bias[:, C:2 * C], row(a["b_out"])).then_inc(loaded, 16)
            sp.dma_start(gamma[:], a["gamma"]).then_inc(loaded, 16)
            sp.dma_start(beta[:], a["beta"]).then_inc(loaded, 16)
            sp.dma_start(dram["x1"].rearrange("p (b c) -> p b c", c=C), acc[:, :, 0:C]).then_inc(x1_saved, 16)

            def store(b, k, i):
                sp.wait_ge(h_ready, b + 1)
                sp.dma_start(dram["hT"][:, bass.ds(b * C, C)], h_t[:, k].rearrange("p c n -> p (c n)")
                             ).then_inc(stored[k], 16)
                sp.wait_ge(feat_ready, b + 1)
                for part, name in enumerate(("feat_in", "feat_out")):
                    sp.dma_start(dram[name].rearrange("(b p) c -> p b c", p=P)[:, bass.ds(b, 1), :]
                                 .rearrange("p b c -> p (b c)"), feat[:, k, part * C:(part + 1) * C]
                                 ).then_inc(stored[k], 16)

            blocks(sp, store)
            for k in range(B):
                sp.wait_ge(stored[k], (NB // B + (k == 0)) * 48)
            sp.wait_ge(x1_saved, 16)

        @block.tensor
        def _(pe):
            pe.wait_ge(loaded, 16 * LD)

            def multiply(b, k, i):
                pe.wait_ge(h_ready, b + 1)
                for c in range(CC):
                    mm = nc.tensor.matmul(ps[:, k, :], h_t[:, k, c, :], w_io[:, c, :], start=c == 0, stop=c == CC - 1)
                mm.then_inc(summed, 1)

            blocks(pe, multiply)

        @block.scalar
        def _(act):
            act.wait_ge(var_ready, 1)
            nc.scalar.activation(shift[:], scale[:], ACT.Sqrt).then_inc(std_ready, 1)

        @block.vector
        def _(v):
            chain = Chain(v, dve)
            with v.Fori(0, NB - 1) as b:
                for c in range(CC):
                    v.bn_stats(stats[:, c, bass.ds(b, 1), :].rearrange("p b s -> p (b s)"),
                               acc[:, bass.ds(b, 1), C + c * P:C + (c + 1) * P].rearrange("p b c -> p (b c)")
                               ).then_inc(stats_done, 1)
            for c in range(CC):
                v.bn_stats(stats[:, c, NB - 1, :], acc[:, NB - 1, C + c * P:C + c * P + LAST]).then_inc(stats_done, 1)
            v.wait_ge(stats_done, CC * NB)
            v.wait_ge(loaded, 16 * LD)
            for c in range(CC):
                ins = v.bn_aggr(mv[:, c, :], stats[:, c, :, :].rearrange("p b s -> p (b s)"))
            chain.then(ins)
            chain.then(v.tensor_scalar(scale[:], mv[:, :, 1], LN_EPS, None, ALU.add))
            v.sem_inc(var_ready, 1)
            v.wait_ge(std_ready, 1)
            chain.then(v.reciprocal(scale[:], shift[:]))
            chain.then(v.tensor_tensor(scale[:], scale[:], gamma[:], ALU.mult))
            chain.then(v.tensor_tensor(shift[:], scale[:], mv[:, :, 0], ALU.mult))
            chain.then(v.tensor_tensor(shift[:], beta[:], shift[:], ALU.subtract))

            def make_h(b, k, i):
                if not isinstance(i, int) or i:
                    v.wait_ge(stored[k], i * 48)
                for c in range(CC):
                    ins = v.tensor_scalar(h_t[:, k, c, :],
                                          acc[:, bass.ds(b, 1), C + c * P:C + (c + 1) * P].rearrange("p b c -> p (b c)"),
                                          scale[:, c:c + 1], shift[:, c:c + 1], ALU.mult, ALU.add)
                ins.then_inc(h_ready, 1)

            def table(b, k, i):
                if not isinstance(b, int) or b < NB - 1:
                    make_h(b + 1, (k + 1) % B, i + (k + 1) // B)
                v.wait_ge(summed, b + 1)
                v.tensor_tensor(feat[:, k, :], ps[:, k, :], bias[:], ALU.add).then_inc(feat_ready, 1)

            make_h(0, 0, 0)
            blocks(v, table)
            v.wait_ge(x1_saved, 16)
            v.wait_ge(feat_ready, NB)
            v.memset(acc[:].rearrange("p b c -> p (b c)"), 0.0)


def sum_over_src_and_gates(nc, a, dram, t, out):
    acc, bucket, ident = t["acc"], t["sorted_bucket"], t["ident"]
    KC = 2 * CC
    with ExitStack() as s:
        n = Names(nc, "sum3", s)
        iota = n.sb("iota", [P, NP])
        record = n.sb("record", [P, U, T, 4])
        rows = n.sb("rows", [P, U, T, C])
        onehot = n.sb("onehot", [P, 2, T, P])
        w_x = n.sb("w_x", [P, KC, 2 * C])
        w_h = n.sb("w_h", [P, CC, 2 * C])
        bias = n.sb("bias", [P, 2 * C])
        x1 = n.sb("x1", [P, C])
        h_t = n.sb("h_t", [P, CC, P])
        sums = n.sb("sums", [P, 2 * C])
        sums_t = n.sb("sums_t", [P, KC, P])
        pre = n.sb("pre", [P, 2 * C])
        gate = n.sb("gate", [P, 2 * C])
        y = n.sb("y", [P, C])
        stats, mv, eps = n.sb("stats", [P, 6]), n.sb("mv", [P, 2]), n.sb("eps", [P, 1])
        std, rstd = n.sb("std", [P, 1]), n.sb("rstd", [P, 1])
        result = n.sb("result", [P, C])
        ps = n.ps("ps", [P, 2, 512])
        ps_t = n.ps("ps_t", [P, 512])
        ps_h = n.ps("ps_h", [P, 512])
        ps_g = n.ps("ps_g", [P, 512])
        loaded = [n.sem(f"loaded{u}") for u in range(U)]
        gathered = [n.sem(f"gathered{u}") for u in range(U)]
        turns, turns_v = n.sem("turns"), n.sem("turns_v")
        onehot_ready, summed, added = n.sem("onehot_ready"), n.sem("summed"), n.sem("added")
        group_done = n.sem("group_done")
        iota_set, eps_set, weights = n.sem("iota_set"), n.sem("eps_set"), n.sem("weights")
        in_loaded, stored = n.sem("in_loaded"), n.sem("stored")
        sums_ready, turned, sums_t_ready = n.sem("sums_ready"), n.sem("turned"), n.sem("sums_t_ready")
        multiplied, pre_ready, gates_ready = n.sem("multiplied"), n.sem("pre_ready"), n.sem("gates_ready")
        mixed, var_ready, std_ready = n.sem("mixed"), n.sem("var_ready"), n.sem("std_ready")
        done, dve = n.sem("done"), n.sem("dve")
        block = s.enter_context(nc.Block())
        records = dram["sorted_record"].rearrange("(g p j) w -> p g (j w)", p=P, j=T)

        def due_blocks(eng, gates):
            next_block = eng.alloc_register("next_block")
            eng.reg_mov(next_block, 0)

            def before(g, limit=None):
                if limit is None:
                    limit = eng.value_load(bucket[0:1, bass.ds(g, 1)], min_val=0, max_val=NB - 1)
                with eng.If(eng.snap(next_block, min_val=0, max_val=NB - 1) < limit):
                    gates(eng.snap(next_block, min_val=0, max_val=NB - 2), g)
                    eng.reg_add(next_block, next_block, 1)

            def rest():
                with eng.Fori(eng.snap(next_block, min_val=0, max_val=NB - 1), NB) as b:
                    gates(b, SG)

            return before, rest

        @block.sync
        def _(sp):
            sp.dma_start(w_x[:], a["W_x2i"].rearrange("(c p) n -> p c n", p=P)).then_inc(weights, 16)
            sp.dma_start(w_h[:], a["W_h2h"].rearrange("(c p) n -> p c n", p=P)).then_inc(weights, 16)
            sp.dma_start(bias[:], row(a["b_x2i"])).then_inc(weights, 16)

            def load(g, u, source):
                sp.wait_ge(group_done, g + 1)
                sp.dma_start(record[:, u].rearrange("p j w -> p (j w)"),
                             records[:, bass.ds(source, 1), :].rearrange("p g w -> p (g w)")).then_inc(loaded[u], 16)

            with sp.Fori(0, SG // U) as i:
                for u in range(U):
                    load(i * U + u, u, i * U + u)
            load(SG, 0, 0)
            sp.wait_ge(loaded[0], (SG // U + 1) * 16)

        @block.gpsimd
        def _(pool):
            nc.gpsimd.iota(iota[:], pattern=[[1, NP]], base=0, channel_multiplier=0,
                           allow_small_or_imprecise_dtypes=True).then_inc(iota_set, 1)
            with pool.Fori(0, SG // U) as i:
                for u in range(U):
                    pool.wait_ge(loaded[u], i * 16 + 16)
                    pool.sem_inc(turns, 1)
                    for j in range(T):
                        pool.indirect_dma_start(
                            out=rows[:, u, j, :], out_offset=None, in_=dram["feat_out"],
                            in_offset=bass.IndirectOffsetOnAxis(ap=record[:, u, j, 0:1].bitcast(I32), axis=0),
                        ).then_inc(gathered[u], 16)

        @block.tensor
        def _(pe):
            pe.wait_ge(weights, 48)

            def multiply(b, groups):
                pe.wait_ge(in_loaded, b * 32 + 32)
                pe.wait_ge(mixed, b + 1)
                for c in range(CC):
                    nc.tensor.transpose(ps_h[:, c * P:(c + 1) * P], h_t[:, c, :], ident[:])
                for c in range(CC):
                    nc.tensor.matmul(ps_g[:], h_t[:, c, :], w_h[:, c, :], start=c == 0, stop=False)
                pe.wait_ge(sums_ready, b + 1)
                for c in range(KC):
                    mm = nc.tensor.transpose(ps_t[:, c * P:(c + 1) * P], sums[:, c * P:(c + 1) * P], ident[:])
                mm.then_inc(turned, 1)
                pe.wait_ge(sums_t_ready, b + 1)
                for c in range(KC):
                    mm = nc.tensor.matmul(ps_g[:], sums_t[:, c, :], w_x[:, c, :], start=False, stop=c == KC - 1)
                mm.then_inc(multiplied, 1)

            before, rest = due_blocks(pe, multiply)
            with pe.Fori(0, SG // U) as i:
                for u in range(U):
                    g = i * U + u
                    before(g)
                    pe.wait_ge(gathered[u], i * 16 * T + 16 * T)
                    pe.wait_ge(onehot_ready, g + 1)
                    pe.wait_ge(added, g + 1)
                    for j in range(T):
                        mm = nc.tensor.matmul(ps[:, u % 2, 0:C], onehot[:, u % 2, j, :], rows[:, u, j, :],
                                              start=j == 0, stop=j == T - 1)
                    mm.then_inc(summed, 1)
            rest()

        @block.scalar
        def _(act):
            act.wait_ge(eps_set, 1)

            def activate(b, groups):
                act.wait_ge(mixed, b + 1)
                act.dma_start(x1[:], dram["x1"][:, bass.ds(b * C, C)]).then_inc(in_loaded, 16)
                act.dma_start(h_t[:].rearrange("p c n -> p (c n)"), dram["hT"][:, bass.ds(b * C, C)]
                              ).then_inc(in_loaded, 16)
                act.wait_ge(added, groups + 2)
                nc.scalar.activation(sums[:], acc[:, bass.ds(b, 1), :].rearrange("p b c -> p (b c)"), ACT.Copy
                                     ).then_inc(sums_ready, 1)
                act.wait_ge(turned, b + 1)
                nc.scalar.activation(sums_t[:].rearrange("p c n -> p (c n)"), ps_t[:], ACT.Copy
                                     ).then_inc(sums_t_ready, 1)
                act.wait_ge(pre_ready, b + 1)
                nc.scalar.activation(gate[:, 0:C], pre[:, 0:C], ACT.Sigmoid)
                nc.scalar.activation(gate[:, C:2 * C], pre[:, C:2 * C], ACT.Tanh).then_inc(gates_ready, 1)
                act.wait_ge(var_ready, b + 1)
                nc.scalar.activation(std[:], mv[:, 1:2], ACT.Sqrt, bias=eps[:, 0:1]).then_inc(std_ready, 1)
                act.wait_ge(done, b + 1)
                act.dma_start(out.rearrange("(b p) c -> p b c", p=P)[:, bass.ds(b, 1), :]
                              .rearrange("p b c -> p (b c)"), result[:]).then_inc(stored, 16)
                act.wait_ge(stored, b * 16 + 16)

            before, rest = due_blocks(act, activate)
            with act.Fori(0, SG) as g:
                before(g)
            rest()

        @block.vector
        def _(v):
            v.sem_inc(group_done, U)
            v.sem_inc(added, 2)
            v.sem_inc(mixed, 1)
            v.memset(eps[:], LN_EPS).then_inc(eps_set, 1)
            chain = Chain(v, dve)
            MIX_STEPS = 7

            def one_hots(g, u, count):
                v.wait_ge(loaded[u], count * 16)
                b = v.value_load(bucket[0:1, bass.ds(g, 1)], min_val=0, max_val=NB - 1)
                for j in range(T):
                    ins = v.tensor_scalar(onehot[:, u % 2, j, :], iota[:, bass.ds(b * P, P)], record[:, u, j, 1:2],
                                          record[:, u, j, 2:3], ALU.is_equal, ALU.mult)
                ins.then_inc(onehot_ready, 1)

            def mix(b, groups):
                chain.at(b * MIX_STEPS)
                v.wait_ge(multiplied, b + 1)
                v.tensor_tensor(pre[:], ps_g[:], bias[:], ALU.add).then_inc(pre_ready, 1)
                v.wait_ge(gates_ready, b + 1)
                new = gate[:, C:2 * C]
                chain.then(v.tensor_tensor(y[:], ps_h[:, 0:C], new, ALU.subtract))
                chain.then(v.tensor_tensor(y[:], y[:], gate[:, 0:C], ALU.mult))
                chain.then(v.tensor_tensor(y[:], y[:], new, ALU.add))
                chain.then(v.tensor_tensor(y[:], y[:], x1[:], ALU.add))
                v.sem_inc(mixed, 1)
                chain.then(v.bn_stats(stats[:], y[:]))
                v.sem_inc(turns_v, 1)
                chain.then(v.bn_aggr(mv[:], stats[:]))
                v.sem_inc(var_ready, 1)
                v.wait_ge(std_ready, b + 1)
                chain.then(v.reciprocal(rstd[:], std[:]))
                v.tensor_scalar(result[:], y[:], mv[:, 0:1], rstd[:, 0:1], ALU.subtract, ALU.mult).then_inc(done, 1)
                assert chain.steps == MIX_STEPS

            v.wait_ge(iota_set, 1)
            v.wait_ge(weights, 48)
            one_hots(0, 0, 1)
            before, rest = due_blocks(v, mix)
            with v.Fori(0, SG // U) as i:
                for u in range(U):
                    g = i * U + u
                    one_hots(g + 1, (u + 1) % U, i + 1 + (u + 1) // U)
                    b = v.value_load(bucket[0:1, bass.ds(g, 1)], min_val=0, max_val=NB - 1)
                    v.wait_ge(summed, g + 1)
                    v.wait_ge(added, g + 2)
                    sums_b = acc[:, bass.ds(b, 1), C:2 * C].rearrange("p b c -> p (b c)")
                    v.tensor_tensor(sums_b, sums_b, ps[:, u % 2, 0:C], ALU.add).then_inc(added, 1)
                    v.sem_inc(group_done, 1)
                    before(g, b)
            rest()


def kernel(**inputs):
    import numpy as np
    import concourse.bacc as bacc
    from concourse.bass_utils import run_bass_kernel_spmd as run

    arrays = layout(np, inputs)
    nc = bacc.Bacc("TRN2", target_bir_lowering=False, num_devices=1)
    a = {k: nc.dram_tensor(f"in_{k}", v.shape, mybir.dt.from_np(v.dtype), kind="ExternalInput").ap()
         for k, v in arrays.items()}
    out = nc.dram_tensor("out_0", (NP, C), F32, kind="ExternalOutput").ap()
    gnn_kernel(nc, a, out)
    r = run(nc, [{f"in_{k}": v for k, v in arrays.items()}], core_ids=[0])
    return r.results[0]["out_0"][:NODES]


def layout(np, inputs):
    def pad(v, n, fill):
        return np.concatenate([v, np.full((n - v.shape[0],) + v.shape[1:], fill, v.dtype)])

    def by_partition(v):
        return np.ascontiguousarray(v.reshape(NG, P, T).transpose(1, 0, 2).reshape(P, NT))

    given = {k: np.asarray(v) for k, v in inputs.items()}
    arrays = {
        "x": pad(given["x"], NP, 0),
        "src": by_partition(pad(given["src"], EP, NODES)),
        "dst": by_partition(pad(given["dst"], EP, NODES)),
        "iw": by_partition(pad(given["edge_weight"], EP, 0)),
        "ow": by_partition(pad(given["edge_weight_n2"], EP, 0)),
        "edge_attr": np.ascontiguousarray(
            pad(given["edge_attr_64"], (NG + 1) * GE, 0).reshape(NG + 1, P, T, EC).transpose(3, 0, 2, 1)
            .reshape(EC, (NG + 1) * GE)),
        "eps": given["L0_gnn_eps"].reshape(1),
    }
    for k in ("ee_w1", "ee_b1", "ee_w2", "ee_b2", "w1", "b1", "g1", "be1", "w2", "b2", "g2", "be2", "w3", "b3",
              "bn_g", "bn_b"):
        arrays[k] = given["L0_gnn_" + k]
    for k in ("gamma", "beta", "W_in", "b_in", "W_out", "b_out", "W_x2i", "b_x2i", "W_h2h"):
        arrays[k] = given["L1_gnn_" + k]
    for k in ("g1", "be1", "g2", "be2", "gamma", "beta"):
        arrays[k] = np.ascontiguousarray(arrays[k].reshape(-1, P).T)
    return arrays
```

```python
from contextlib import ExitStack, contextmanager

import concourse.bass as bass
from concourse import mybir

P = 128
ALU = mybir.AluOpType
ACT = mybir.ActivationFunctionType
F32 = mybir.dt.float32
I32 = mybir.dt.int32
F32R = mybir.dt.float32r
AX = mybir.AxisListType.X

NODES = 6250
EDGES = 206250
C = 256
EC = 64
H = 1024
CC = C // P
HC = H // P
NB = -(-NODES // P)
NP = NB * P
LAST = NODES - (NB - 1) * P
T = 4
GE = T * P
U = 4
NG = -(-EDGES // (GE * U)) * U
NT = NG * T
EP = NG * GE
GH = GE // 2
SG = -(-(2 * NG + NB - 1) // 2)
SG = -(-SG // U) * U
BT = -(-2 * SG // P)
SEED = 7
assert NB % SEED == 0
PAD_DMAS = 16
PLAIN_BODIES = NB + 2
TILES_SUM = (NG // U - PLAIN_BODIES) * 2
NET_STEP, NET_STEPS = 11, 124
TAB_STEP = 19
TILES_NET = NET_STEP * NET_STEPS
TAB_STEPS = (NT - TILES_SUM - TILES_NET) // TAB_STEP
assert TILES_SUM + TILES_NET + TAB_STEP * TAB_STEPS == NT
COUNTED_V = 21
LN_EPS = 1e-5
BUCKET_SHIFT = 7
HALF_SHIFT = 8
assert 1 << BUCKET_SHIFT == P and 1 << HALF_SHIFT == GH


def gnn_kernel(nc, a, out):
    with ExitStack() as whole:
        def scratch(name, shape, dt):
            return nc.dram_tensor(name, shape, dt, kind="Internal").ap()

        dram = {
            "x_plus_b2": scratch("x_plus_b2", (NP, C), F32),
            "edge_slot": scratch("edge_slot", (P, NT), I32),
            "edge_record": scratch("edge_record", (P, NT * 4), F32),
            "sorted_record": scratch("sorted_record", (SG * GE, 4), F32),
            "dst_windows": scratch("dst_windows", (NG, 2), I32),
            "sorted_bucket": scratch("sorted_bucket", (P, BT), I32),
            "feat_in": scratch("feat_in", (NP, C), F32),
            "feat_out": scratch("feat_out", (NP, C), F32),
            "x1": scratch("x1", (P, NB * C), F32),
            "hT": scratch("hT", (P, NB * C), F32),
        }
        sb = lambda name, shape, dt=F32: whole.enter_context(nc.sbuf_tensor(name, shape, dt))
        t = {
            "acc": sb("acc", [P, NB, 2 * C]),
            "ident": sb("ident", [P, P]),
            "dstf": sb("dstf", [P, NT + T]),
            "windows": sb("windows", [1, 2 * (NG + 1)], I32),
            "sorted_bucket": sb("sorted_bucket_sb", [1, 2 * SG + 2], I32),
            "kcol": sb("kcol", [P, NB]),
            "offset": sb("offset", [P, NB]),
        }
        with nc.sbuf_tensor("iota_first", [P, NP], F32) as t["iota"]:
            prepare(nc, a, dram, t)
            sum_over_dst(nc, a, dram, t, first=True)
        node_network(nc, a, dram, t)
        with nc.sbuf_tensor("iota_second", [P, NP], F32) as t["iota"]:
            make_tables(nc, a, dram, t)
            sum_over_dst(nc, a, dram, t, first=False)
            sum_over_src_and_gates(nc, a, dram, t, out)


class Chain:

    def __init__(self, engine, sem):
        self.engine, self.sem, self.before, self.steps = engine, sem, 0, 0

    def then(self, ins):
        self.steps += 1
        ins.then_inc(self.sem, 1)
        self.engine.wait_ge(self.sem, self.before + self.steps)

    def at(self, before):
        self.before, self.steps = before, 0

    @contextmanager
    def loop(self, engine, start, end, per):
        began = self.steps
        with engine.Fori(start, end) as i:
            self.before = (i - start) * per
            yield i
        assert self.steps - began == per, self.steps - began
        self.before, self.steps = 0, began + per * (end - start)


class Names:

    def __init__(self, nc, stage, stack):
        self.nc, self.stage, self.stack = nc, stage, stack

    def sb(self, name, shape, dt=F32):
        return self.stack.enter_context(self.nc.sbuf_tensor(f"{self.stage}_{name}", shape, dt))

    def ps(self, name, shape, dt=F32):
        return self.stack.enter_context(self.nc.psum_tensor(f"{self.stage}_{name}", shape, dt))

    def sem(self, name):
        return self.stack.enter_context(self.nc.semaphore(f"{self.stage}_{name}"))


def row(v):
    return v.partition_broadcast(P)


def prepare(nc, a, dram, t):
    acc, dstf, ident, kcol, offset = t["acc"], t["dstf"], t["ident"], t["kcol"], t["offset"]
    with ExitStack() as s:
        n = Names(nc, "prep", s)
        srci = n.sb("srci", [P, NT], I32)
        srcblk = n.sb("srcblk", [P, NT])
        dsti = n.sb("dsti", [P, NT], I32)
        dstblk = n.sb("dstblk", [P, NT])
        ow = n.sb("ow", [P, NT])
        equal, signs = srci, dsti
        rec = n.sb("rec", [P, NT, 4])
        b1 = n.sb("b1", [P, C])
        b2 = n.sb("b2", [P, C])
        eps = n.sb("eps", [P, 1])
        lohi = n.sb("lohi", [P, 2, NG])
        ones = n.sb("ones", [P, P])
        before = n.sb("before", [P, P])
        count = n.sb("count", [P, NB])
        above = n.sb("above", [P, NB])
        up_to = n.sb("up_to", [P, NB])
        total_i, zero = n.sb("total_i", [P, NB], I32), n.sb("zero", [P, NB])
        halves = n.sb("halves", [P, NB])
        ends = n.sb("ends", [P, NB])
        gid = n.sb("gid", [P, BT])
        cmp = n.sb("cmp", [P, BT, NB])
        bucket = n.sb("bucket", [P, BT])
        bucket_i = n.sb("bucket_i", [P, BT], I32)
        QG = NG // 4
        lohi_r = n.sb("lohi_r", [QG, 4, 2])
        lohi_i = n.sb("lohi_i", [QG, 4, 2], I32)
        pad_rec = n.sb("pad_rec", [P, SG * GE // P // PAD_DMAS, 4])
        ps_count = n.ps("ps_count", [P, 2, 512])
        ps_t = n.ps("ps_t", [P, 2, 512])

        loaded, x_loaded = n.sem("loaded"), n.sem("x_loaded")
        iotas, ident0, pool_done = n.sem("iotas"), n.sem("ident0"), n.sem("pool_done")
        dve = n.sem("dve")
        counted, prefixed = n.sem("counted"), n.sem("prefixed")
        ranges, turned, turned_read = n.sem("ranges"), n.sem("turned"), n.sem("turned_read")
        rec_ready, above_ready, signs_summed = n.sem("rec_ready"), n.sem("above_ready"), n.sem("signs_summed")
        small_ready, acc_ready, xb_ready = n.sem("small_ready"), n.sem("acc_ready"), n.sem("xb_ready")
        pad_ready = n.sem("pad_ready")
        xb_stored = n.sem("xb_stored")
        written, tables = n.sem("written"), n.sem("tables")
        block = s.enter_context(nc.Block())

        @block.sync
        def _(sp):
            sp.dma_start(srci[:], a["src"]).then_inc(loaded, 16)
            sp.dma_start(dsti[:], a["dst"]).then_inc(loaded, 16)
            sp.dma_start(ow[:], a["ow"]).then_inc(loaded, 16)
            sp.dma_start(b1[:], row(a["ee_b1"])).then_inc(loaded, 16)
            sp.dma_start(b2[:], row(a["ee_b2"])).then_inc(loaded, 16)
            sp.dma_start(eps[:], row(a["eps"])).then_inc(loaded, 16)
            sp.dma_start(acc[:, :, 0:C], a["x"].rearrange("(b p) c -> p b c", p=P)).then_inc(x_loaded, 16)
            sp.wait_ge(pad_ready, 1)
            for q in range(PAD_DMAS):
                sp.dma_start(dram["sorted_record"].rearrange("(q p n) w -> q p (n w)", q=PAD_DMAS, p=P)[q],
                             pad_rec[:].rearrange("p n w -> p (n w)")).then_inc(written, 16)
            for q in range(NB // SEED):
                sp.wait_ge(xb_ready, q + 1)
                sp.dma_start(dram["x_plus_b2"].rearrange("(b p) c -> p b c", p=P)[:, q * SEED:(q + 1) * SEED, :],
                             acc[:, q * SEED:(q + 1) * SEED, C:2 * C]).then_inc(xb_stored, 16)
            sp.wait_ge(small_ready, 1)
            sp.dma_start(dram["sorted_bucket"], bucket_i[:]).then_inc(tables, 16)
            sp.wait_ge(small_ready, 2)
            sp.dma_start(dram["dst_windows"].rearrange("(q g) w -> g q w", q=4), lohi_i[:]).then_inc(tables, 16)
            sp.wait_ge(tables, 32)
            flat = dram["sorted_bucket"].rearrange("p u -> (p u)")
            sp.dma_start(t["sorted_bucket"][0:1, 0:2 * SG], flat[0:2 * SG].unsqueeze(0)).then_inc(written, 16)
            sp.dma_start(t["windows"][0:1, 0:2 * NG],
                         dram["dst_windows"].rearrange("g w -> (g w)").unsqueeze(0)).then_inc(written, 16)
            sp.wait_ge(rec_ready, 1)
            sp.dma_start(dram["edge_record"], rec[:].rearrange("p n w -> p (n w)")).then_inc(written, 16)
            sp.wait_ge(written, 16 * (PAD_DMAS + 3))

        @block.gpsimd
        def _(pool):
            nc.gpsimd.memset(ident[:], 0.0).then_inc(ident0, 1)
            nc.gpsimd.memset(before[:], 1.0).then_inc(ident0, 1)
            nc.gpsimd.iota(kcol[:], pattern=[[1, NB]], base=0, channel_multiplier=0,
                           allow_small_or_imprecise_dtypes=True).then_inc(iotas, 1)
            nc.gpsimd.iota(gid[:], pattern=[[1, BT]], base=0, channel_multiplier=BT,
                           allow_small_or_imprecise_dtypes=True).then_inc(iotas, 1)
            pool.wait_ge(ident0, 2)
            nc.gpsimd.affine_select(out=ident[:], in_=ident[:], compare_op=ALU.not_equal, fill=1.0, base=0,
                                    pattern=[[-1, P]], channel_multiplier=1).then_inc(pool_done, 1)
            nc.gpsimd.affine_select(out=before[:], in_=before[:], compare_op=ALU.is_gt, fill=0.0, base=0,
                                    pattern=[[1, P]], channel_multiplier=-1).then_inc(pool_done, 1)
            nc.gpsimd.iota(t["iota"][:], pattern=[[1, NP]], base=0, channel_multiplier=0,
                           allow_small_or_imprecise_dtypes=True)
            pool.wait_ge(loaded, 96)
            pool.wait_ge(x_loaded, 16)
            for q in range(NB // SEED):
                blocks = slice(q * SEED, (q + 1) * SEED)
                nc.gpsimd.tensor_tensor(acc[:, blocks, C:2 * C], acc[:, blocks, 0:C],
                                        b2[:].unsqueeze(1).to_broadcast([P, SEED, C]), ALU.add).then_inc(xb_ready, 1)

        @block.tensor
        def _(pe):
            pe.wait_ge(pool_done, 2)
            pe.wait_ge(ranges, 2)
            for k in range(8):
                if k >= 2:
                    pe.wait_ge(turned_read, k - 1)
                nc.tensor.transpose(ps_t[0:QG, k % 2, 0:P], lohi[:, k % 2, (k // 2) * QG:(k // 2 + 1) * QG],
                                    ident[:]).then_inc(turned, 1)
            pe.wait_ge(counted, COUNTED_V + 1)
            nc.tensor.matmul(ps_count[:, 0, 0:NB], before[:], count[:], start=True, stop=True)
            nc.tensor.matmul(ps_count[:, 1, 0:NB], ones[:], count[:], start=True, stop=True).then_inc(prefixed, 1)

        @block.scalar
        def _(act):
            act.preload_act_table(ACT.Sign)
            act.wait_ge(above_ready, 1)
            for k in range(COUNTED_V - 1, NB - 1):
                nc.scalar.activation(signs[:].bitcast(F32), srcblk[:], ACT.Sign, bias=above[:, k:k + 1],
                                     accum_out=up_to[:, k:k + 1]).then_inc(signs_summed, 1)
                if k < NB - 2:
                    act.wait_ge(signs_summed, k - COUNTED_V + 2)
            act.wait_ge(loaded, 96)
            act.wait_ge(x_loaded, 16)
            act.wait_ge(xb_stored, NB // SEED * 16)
            for q in range(NB // SEED):
                act.wait_ge(acc_ready, q + 1)
                nc.scalar.activation(acc[:, q * SEED:(q + 1) * SEED, C:2 * C],
                                     b1[:].unsqueeze(1).to_broadcast([P, SEED, C]), ACT.Relu)

        @block.vector
        def _(v):
            steps = [0]

            def then(ins):
                steps[0] += 1
                ins.then_inc(dve, 1)
                v.wait_ge(dve, steps[0])

            v.memset(pad_rec[:, :, 0].bitcast(I32), NODES)
            v.memset(pad_rec[:, :, 1], -1.0)
            v.memset(pad_rec[:, :, 2:4], 0.0).then_inc(pad_ready, 1)
            v.memset(ones[:], 1.0)
            v.memset(zero[:], 0.0)
            v.memset(dstf[:, NT:], -1.0)
            v.memset(rec[:, :, 3], 0.0)
            v.memset(t["sorted_bucket"][:, 2 * SG:], 0)
            then(v.memset(t["windows"][:, 2 * NG:], 0))
            v.wait_ge(loaded, 96)
            v.tensor_copy(dstf[:, 0:NT], dsti[:])
            v.tensor_copy(rec[:, :, 1], srci[:])
            v.tensor_copy(rec[:, :, 2], ow[:])
            then(v.tensor_copy(rec[:, :, 0].bitcast(I32), dsti[:]))
            v.tensor_single_scalar(srci[:], srci[:], BUCKET_SHIFT, op=ALU.arith_shift_right)
            then(v.tensor_single_scalar(dsti[:], dsti[:], BUCKET_SHIFT, op=ALU.arith_shift_right))
            v.wait_ge(iotas, 2)
            v.tensor_scalar(above[:], kcol[:], -1.0, -0.5, ALU.mult, ALU.add)
            v.tensor_copy(srcblk[:], srci[:]).then_inc(rec_ready, 1)
            then(v.tensor_copy(dstblk[:], dsti[:]))
            v.sem_inc(above_ready, 1)
            by_group = dstblk[:].rearrange("p (g j) -> p g j", j=T)
            v.tensor_reduce(lohi[:, 0, :], by_group, AX, ALU.min).then_inc(ranges, 1)
            v.tensor_reduce(lohi[:, 1, :], by_group, AX, ALU.max).then_inc(ranges, 1)
            for k in range(8):
                v.wait_ge(turned, k + 1)
                v.tensor_reduce(lohi_r[:, k // 2, k % 2:k % 2 + 1], ps_t[0:QG, k % 2, 0:P], AX,
                                ALU.max if k % 2 else ALU.min).then_inc(turned_read, 1)
            for k in range(COUNTED_V):
                if k:
                    v.wait_ge(counted, k)
                v.tensor_scalar(equal[:].bitcast(F32), srcblk[:], float(k), None, ALU.is_equal, ALU.add,
                                accum_out=count[:, k:k + 1]).then_inc(counted, 1)
            later = slice(COUNTED_V - 1, NB - 1)
            v.memset(up_to[:, NB - 1:NB], float(NT))
            v.wait_ge(signs_summed, NB - COUNTED_V)
            then(v.tensor_scalar(up_to[:, later], up_to[:, later], -0.5, 0.5 * NT, ALU.mult, ALU.add))
            v.tensor_tensor(count[:, COUNTED_V:NB], up_to[:, COUNTED_V:NB], up_to[:, later], ALU.subtract
                            ).then_inc(counted, 1)
            v.wait_ge(prefixed, 1)
            then(v.tensor_scalar(halves[:], ps_count[:, 1, 0:NB], float(GH - 1), None, ALU.add))
            then(v.tensor_copy(total_i[:], halves[:]))
            then(v.tensor_single_scalar(total_i[:], total_i[:], HALF_SHIFT, op=ALU.arith_shift_right))
            then(v.tensor_copy(halves[:], total_i[:]))
            then(v.tensor_tensor_scan(ends[:], zero[:], halves[:], 0.0, ALU.add, ALU.add))
            then(v.tensor_tensor(offset[:], ends[:], halves[:], ALU.subtract))
            then(v.tensor_scalar(offset[:], offset[:], float(GH), NB - 1.0, ALU.mult, ALU.add))
            then(v.tensor_tensor(offset[:], offset[:], ps_count[:, 0, 0:NB], ALU.add))
            then(v.tensor_tensor(cmp[:, :, 0:NB - 1], gid[:].unsqueeze(2).to_broadcast([P, BT, NB - 1]),
                                 ends[:, 0:NB - 1].unsqueeze(1).to_broadcast([P, BT, NB - 1]), ALU.is_ge))
            then(v.tensor_reduce(bucket[:], cmp[:, :, 0:NB - 1], AX, ALU.add))
            v.tensor_copy(bucket_i[:], bucket[:]).then_inc(small_ready, 1)
            v.wait_ge(turned_read, 8)
            v.tensor_copy(lohi_i[:], lohi_r[:]).then_inc(small_ready, 1)
            v.wait_ge(x_loaded, 16)
            then(v.tensor_scalar(eps[:], eps[:], 1.0, None, ALU.add))
            v.wait_ge(xb_ready, NB // SEED)
            for q in range(NB // SEED):
                blocks = slice(q * SEED, (q + 1) * SEED)
                v.scalar_tensor_tensor(out=acc[:, blocks, 0:C], in0=acc[:, blocks, 0:C], scalar=eps[:, 0:1],
                                       in1=acc[:, blocks, C:2 * C], op0=ALU.mult, op1=ALU.add).then_inc(acc_ready, 1)


def sum_over_dst(nc, a, dram, t, first):
    acc, dstf, windows, iota = t["acc"], t["dstf"], t["windows"], t["iota"]
    parts = 2 if first else 1
    table = dram["x_plus_b2"] if first else dram["feat_in"]
    with ExitStack() as s:
        n = Names(nc, "sum1" if first else "sum2", s)
        index = n.sb("index", [P, U, T], I32)
        rows = n.sb("rows", [P, U, T, C])
        hot = F32R if first else F32
        onehot = n.sb("onehot", [P, 2, T, P], hot)
        onehot_x = n.sb("onehot_x", [P, T, P], hot)
        if first:
            attr = n.sb("attr", [EC + 1, U, T, P])
            w1 = n.sb("w1", [EC + 1, C])
            hidden = n.sb("hidden", [P, 2, 2, T, C], F32R)
            ps_h = n.ps("ps_h", [P, 2, 2, C])
            place = n.sb("place", [P, NT])
            mask, scan = n.sb("mask", [P, NT]), n.sb("scan", [P, NT])
            tick = n.sb("tick", [1, 1])
            slot = n.sb("slot", [P, 2], I32)
            record = n.sb("record", [P, 2, 4])
            slots_loaded, scattered = n.sem("slots_loaded"), n.sem("scattered")
            src_loaded, place_step = n.sem("src_loaded"), n.sem("place_step")
            places_ready, places_stored = n.sem("places_ready"), n.sem("places_stored")
        else:
            iw = n.sb("iw", [P, NT + T])
        ps = n.ps("ps", [P, 2, 2, 512])
        ps_x = n.ps("ps_x", [P, 2, 512])

        consts = n.sem("consts")
        index_loaded = [n.sem(f"index_loaded{u}") for u in range(U)]
        attr_loaded = [n.sem(f"attr_loaded{u}") for u in range(U)]
        gathered = [n.sem(f"gathered{u}") for u in range(U)]
        ones_set = n.sem("ones_set")
        turns, turns_v = n.sem("turns"), n.sem("turns_v")
        onehot_ready, summed, ps_free = n.sem("onehot_ready"), n.sem("summed"), n.sem("ps_free")
        onehot_x_ready, summed_x, added_x = n.sem("onehot_x_ready"), n.sem("summed_x"), n.sem("added_x")
        group_done = n.sem("group_done")
        hidden_ps = n.sem("hidden_ps")
        high_ready = n.sem("high_ready")
        hidden_ready = n.sem("hidden_ready")
        block = s.enter_context(nc.Block())

        @block.sync
        def _(sp):
            if first:
                sp.dma_start(w1[0:EC, :], a["ee_w1"]).then_inc(consts, 16)
                sp.dma_start(w1[EC:EC + 1, :], a["ee_b1"].unsqueeze(0)).then_inc(consts, 16)
            else:
                sp.dma_start(iw[:, 0:NT], a["iw"]).then_inc(consts, 16)

            def load_attr(g, u):
                sp.wait_ge(hidden_ps, g * 2 + 2)
                sp.dma_start(attr[0:EC, u, :, :], a["edge_attr"].rearrange("e (g j p) -> e g j p", j=T, p=P)
                             [:, bass.ds(g, 1), :, :].rearrange("e g j p -> e (g j p)")
                             ).then_inc(attr_loaded[u], 16)

            def load_records(i):
                sp.dma_start(slot[:], dram["edge_slot"][:, bass.ds(i * 2, 2)]).then_inc(slots_loaded, 16)
                sp.dma_start(record[:].rearrange("p k w -> p (k w)"), dram["edge_record"][:, bass.ds(i * 8, 8)]
                             ).then_inc(slots_loaded, 16)

            def body(i, scatters):
                for u in range(U):
                    g = i * U + u
                    if not isinstance(i, int) or i:
                        sp.wait_ge(gathered[u], i * (16 * T))
                    sp.dma_start(index[:, u, :], a["src"][:, bass.ds(g * T, T)]).then_inc(index_loaded[u], 16)
                    if first:
                        load_attr(g, u)
                    if scatters and u == 3:
                        after = i - PLAIN_BODIES + 1
                        sp.wait_ge(scattered, after * 32)
                        load_records(after)

            if first:
                sp.dma_start(mask[:].bitcast(I32), a["src"]).then_inc(src_loaded, 16)
                body(0, False)
                with sp.Fori(1, PLAIN_BODIES - 1) as i:
                    body(i, False)
                sp.wait_ge(places_ready, 1)
                sp.dma_start(dram["edge_slot"], scan[:].bitcast(I32)).then_inc(places_stored, 16)
                body(PLAIN_BODIES - 1, False)
                sp.wait_ge(places_stored, 16)
                load_records(0)
                with sp.Fori(PLAIN_BODIES, NG // U) as i:
                    body(i, True)
                load_attr(NG, 0)
                sp.wait_ge(slots_loaded, 32 * (NG // U - PLAIN_BODIES + 1))
            else:
                body(0, False)
                with sp.Fori(1, NG // U) as i:
                    body(i, False)

        @block.gpsimd
        def _(pool):
            def body(i, scatters):
                for u in range(U):
                    pool.wait_ge(index_loaded[u], i * 16 + 16)
                    pool.wait_ge(group_done, i * U + u + 1)
                    pool.sem_inc(turns, 1)
                    for j in range(T):
                        pool.indirect_dma_start(
                            out=rows[:, u, j, :], out_offset=None, in_=table,
                            in_offset=bass.IndirectOffsetOnAxis(ap=index[:, u, j:j + 1], axis=0),
                        ).then_inc(gathered[u], 16)
                    if scatters and u < 2:
                        pool.wait_ge(slots_loaded, (i - PLAIN_BODIES) * 32 + 32)
                        pool.sem_inc(turns, 1)
                        pool.indirect_dma_start(
                            out=dram["sorted_record"],
                            out_offset=bass.IndirectOffsetOnAxis(ap=slot[:, u:u + 1], axis=0),
                            in_=record[:, u, :], in_offset=None,
                        ).then_inc(scattered, 16)

            with pool.Fori(0, PLAIN_BODIES if first else NG // U) as i:
                body(i, False)
            if first:
                with pool.Fori(PLAIN_BODIES, NG // U) as i:
                    body(i, True)
                pool.wait_ge(scattered, (NG // U - PLAIN_BODIES) * 32)

        @block.tensor
        def _(pe):
            def edge_network(g, u, count):
                pe.wait_ge(attr_loaded[u], count * 16)
                for m in range(2):
                    pe.wait_ge(hidden_ready, g * 2 + m + 1)
                    for j in range(2):
                        mm = nc.tensor.matmul(ps_h[:, m, j, :], attr[:, u, 2 * m + j, :], w1[:],
                                              start=j == 0, stop=j == 1, skip_group_check=True)
                    mm.then_inc(hidden_ps, 1)

            def window(target, hot, u, hu):
                for j in range(T):
                    mm = nc.tensor.matmul(target[:, 0, 0:C], hot[:, j, :].bitcast(F32), rows[:, u, j, :],
                                          start=j == 0, stop=j == T - 1)
                if first:
                    for j in range(T):
                        for half in range(2):
                            mm = nc.tensor.matmul(target[:, 1, 0:C], hot[:, j, :], hidden[:, hu, half, j, :],
                                                  start=j + half == 0, stop=j + half == T)
                return mm

            if first:
                pe.sem_inc(hidden_ps, 2 * U)
                pe.wait_ge(consts, 32)
                pe.wait_ge(ones_set, 1)
                edge_network(0, 0, 1)
            further = pe.alloc_register(f"further_windows_{parts}")
            pe.reg_mov(further, 0)
            with pe.Fori(0, NG // U) as i:
                for u in range(U):
                    g = i * U + u
                    low = pe.value_load(windows[0:1, bass.ds(g * 2, 1)], min_val=0, max_val=NB - 1)
                    high = pe.value_load(windows[0:1, bass.ds(g * 2 + 1, 1)], min_val=0, max_val=NB - 1)
                    if first:
                        edge_network(g + 1, (u + 1) % U, i + 1 + (u + 1) // U)
                        pe.wait_ge(hidden_ready, g * 2 + 4)
                    pe.wait_ge(gathered[u], i * 16 * T + 16 * T)
                    pe.wait_ge(onehot_ready, g + 1)
                    pe.wait_ge(ps_free, g + 1)
                    window(ps[:, u % 2], onehot[:, u % 2], u, u % 2).then_inc(summed, 1)
                    with pe.If(low < high):
                        with pe.Fori(low, high) as b:
                            pe.reg_add(further, further, 1)
                            pe.wait_ge(onehot_x_ready, pe.snap(further, min_val=1, max_val=NG * NB))
                            window(ps_x, onehot_x, u, u % 2).then_inc(summed_x, 1)

        @block.scalar
        def _(act):
            if first:
                act.preload_act_table(ACT.Relu)

                def relu(g, hu):
                    act.wait_ge(group_done, g + 3)
                    for m in range(2):
                        act.wait_ge(hidden_ps, g * 2 + m + 1 + 2 * U)
                        nc.scalar.activation(hidden[:, hu, 0, 2 * m:2 * m + 2, :], ps_h[:, m, :, :],
                                             ACT.Relu).then_inc(high_ready, 1)

                with act.Fori(0, NG // U) as i:
                    for u in range(U):
                        relu(i * U + u, u % 2)
                relu(NG, 0)

        @block.vector
        def _(v):
            v.sem_inc(group_done, U)
            v.sem_inc(ps_free, 2)
            if first:
                v.sem_inc(hidden_ready, 2)
                v.memset(attr[EC:EC + 1, :, :, :], 1.0).then_inc(ones_set, 1)
            else:
                v.wait_ge(consts, 16)
                v.memset(iw[:, NT:], 0.0).then_inc(ones_set, 1)
                v.wait_ge(ones_set, 1)
            further = v.alloc_register(f"further_windows_{parts}")
            v.reg_mov(further, 0)

            def one_hots(target, g, b):
                for j in range(T):
                    column = bass.ds(g * T + j, 1)
                    block_nodes = iota[:, bass.ds(b * P, P)]
                    if first:
                        ins = v.tensor_scalar(target[:, j, :], block_nodes, dstf[:, column], None, ALU.is_equal)
                    else:
                        ins = v.tensor_scalar(target[:, j, :], block_nodes, dstf[:, column], iw[:, column],
                                              ALU.is_equal, ALU.mult)
                return ins

            def low_parts(g, hu):
                for m in range(2):
                    v.wait_ge(high_ready, g * 2 + m + 1)
                    v.scalar_tensor_tensor(out=hidden[:, hu, 1, 2 * m:2 * m + 2, :], in0=ps_h[:, m, :, :], scalar=0.0,
                                           in1=hidden[:, hu, 0, 2 * m:2 * m + 2, :].bitcast(F32), op0=ALU.max,
                                           op1=ALU.subtract).then_inc(hidden_ready, 1)

            def add(source, b):
                sums = acc[:, bass.ds(b, 1), :].rearrange("p b (k c) -> p (b k) c", k=2)[:, 0:parts, :]
                return v.tensor_tensor(sums, sums, source[:, 0:parts, 0:C], ALU.add)

            low_block = v.alloc_register(f"low_block_{parts}")
            window = v.alloc_register(f"window_{parts}")
            v.reg_mov(window, 0)
            v.reg_mov(low_block, v.value_load(windows[0:1, 0:1], min_val=0, max_val=NB - 1))
            one_hots(onehot[:, 0], 0, v.snap(low_block, min_val=0, max_val=NB - 1)).then_inc(onehot_ready, 1)
            if first:
                low_parts(0, 0)
            if first:
                v.wait_ge(src_loaded, 16)
                v.tensor_single_scalar(mask[:].bitcast(I32), mask[:].bitcast(I32), BUCKET_SHIFT,
                                       op=ALU.arith_shift_right).then_inc(place_step, 1)
                v.wait_ge(place_step, 1)
                v.tensor_copy(place[:], mask[:].bitcast(I32)).then_inc(place_step, 1)

            def rank(k, step):
                v.wait_ge(place_step, k * U + step + 2)
                if step == 0:
                    v.tensor_scalar(mask[:], place[:], t["kcol"][:, bass.ds(k, 1)], None, ALU.is_equal
                                    ).then_inc(place_step, 1)
                elif step == 1:
                    v.tensor_tensor_scan(scan[:, 0:NT // 2], mask[:, 0:NT // 2], mask[:, 0:NT // 2],
                                         t["offset"][:, bass.ds(k, 1)], ALU.add, ALU.bypass).then_inc(place_step, 1)
                elif step == 2:
                    v.tensor_tensor_scan(scan[:, NT // 2:], mask[:, NT // 2:], mask[:, NT // 2:],
                                         scan[:, NT // 2 - 1:NT // 2], ALU.add, ALU.bypass).then_inc(place_step, 1)
                else:
                    v.memset(tick[:], 0.0)
                    v.copy_predicated(place[:], mask[:].bitcast(I32), scan[:]).then_inc(place_step, 1)

            def body(i, ranks):
                for u in range(U):
                    g = i * U + u
                    low = v.snap(low_block, min_val=0, max_val=NB - 1)
                    high = v.value_load(windows[0:1, bass.ds(g * 2 + 1, 1)], min_val=0, max_val=NB - 1)
                    low_next = v.value_load(windows[0:1, bass.ds(g * 2 + 2, 1)], min_val=0, max_val=NB - 1)
                    one_hots(onehot[:, (u + 1) % 2], g + 1, low_next).then_inc(onehot_ready, 1)
                    with v.If(low < high):
                        v.reg_add(window, low_block, 1)
                        one_hots(onehot_x, g, v.snap(window, min_val=1, max_val=NB - 1)).then_inc(onehot_x_ready, 1)
                    if first:
                        low_parts(g + 1, (u + 1) % 2)
                    if ranks:
                        rank(i, u)
                    v.wait_ge(summed, g + 1)
                    v.wait_ge(ps_free, g + 2)
                    add(ps[:, u % 2], low).then_inc(ps_free, 1)
                    with v.If(low < high):
                        with v.Fori(low + 1, high + 1) as b:
                            v.reg_add(further, further, 1)
                            done = v.snap(further, min_val=1, max_val=NG * NB)
                            v.wait_ge(summed_x, done)
                            add(ps_x, b).then_inc(added_x, 1)
                            v.wait_ge(added_x, done)
                            v.sem_inc(turns_v, 1)
                            with v.If(b < high):
                                v.reg_add(window, window, 1)
                                one_hots(onehot_x, g, v.snap(window, min_val=1, max_val=NB - 1)
                                         ).then_inc(onehot_x_ready, 1)
                    v.sem_inc(group_done, 1)
                    v.reg_mov(low_block, low_next)

            with v.Fori(0, NB if first else NG // U) as i:
                body(i, first)
            if first:
                v.wait_ge(place_step, NB * U + 2)
                v.tensor_scalar(place[:], place[:], -float(NB), None, ALU.add).then_inc(place_step, 1)
                v.wait_ge(place_step, NB * U + 3)
                v.tensor_copy(scan[:].bitcast(I32), place[:]).then_inc(places_ready, 1)
                with v.Fori(NB, NG // U) as i:
                    body(i, False)


def record_scatter(n, dram, first_tile, per_step, steps):
    index = n.sb("index", [P, 2, per_step], I32)
    record = n.sb("record", [P, 2, per_step, 4])
    loaded = [n.sem("records_loaded0"), n.sem("records_loaded1")]
    scattered = [n.sem("scattered0"), n.sem("scattered1")]
    turns = n.sem("scatter_turns")

    def load(sp, q, k):
        tile = q * per_step + first_tile
        sp.dma_start(index[:, k, :], dram["edge_slot"][:, bass.ds(tile, per_step)]).then_inc(loaded[k], 16)
        sp.dma_start(record[:, k, :, :].rearrange("p t w -> p (t w)"),
                     dram["edge_record"][:, bass.ds(tile * 4, 4 * per_step)]).then_inc(loaded[k], 16)

    def load_first(sp):
        for k in range(2):
            load(sp, k, k)

    def load_rest(sp):
        with sp.Fori(1, steps // 2) as i:
            for k in range(2):
                sp.wait_ge(scattered[k], i * (16 * per_step))
                load(sp, i * 2 + k, k)
        if steps % 2:
            sp.wait_ge(scattered[0], steps // 2 * 16 * per_step)
            load(sp, steps - 1, 0)

    def scatter_all(pool):
        def scatter(i, k):
            pool.wait_ge(loaded[k], i * 32 + 32)
            pool.sem_inc(turns, 1)
            for j in range(per_step):
                pool.indirect_dma_start(
                    out=dram["sorted_record"], out_offset=bass.IndirectOffsetOnAxis(ap=index[:, k, j:j + 1], axis=0),
                    in_=record[:, k, j, :], in_offset=None,
                ).then_inc(scattered[k], 16)

        with pool.Fori(0, steps // 2) as i:
            for k in range(2):
                scatter(i, k)
        if steps % 2:
            scatter(steps // 2, 0)
        for k in range(2):
            pool.wait_ge(scattered[k], (steps + 1 - k) // 2 * 16 * per_step)

    return load_first, load_rest, scatter_all


def node_network(nc, a, dram, t):
    acc, ident = t["acc"], t["ident"]
    with ExitStack() as s:
        n = Names(nc, "net", s)
        w_ee = n.sb("w_ee", [P, CC, C])
        w1 = n.sb("w1", [P, CC, H])
        w2 = n.sb("w2", [P, HC, H])
        w3 = n.sb("w3", [P, HC, C])
        bias = n.sb("bias", [P, 2, H])
        bias3 = n.sb("bias3", [P, C])
        bn_g, bn_b = n.sb("bn_g", [P, C]), n.sb("bn_b", [P, C])
        gain = n.sb("gain", [P, 2, HC])
        shift = n.sb("shift", [P, 2, HC])
        sums = n.sb("sums", [P, 2 * C])
        hid_t = n.sb("hid_t", [P, CC, P])
        in_t = n.sb("in_t", [P, CC, P])
        z = n.sb("z", [P, H])
        act_t = n.sb("act_t", [P, 2, HC, P])
        stats = n.sb("stats", [P, 2, 6])
        mv = n.sb("mv", [P, 2])
        std, rstd, eps = n.sb("std", [P, 1]), n.sb("rstd", [P, 1]), n.sb("eps", [P, 1])
        x_in = n.sb("x_in", [P, C])
        y = n.sb("y", [P, C])
        x1 = n.sb("x1", [P, C])
        ps_t = n.ps("ps_t", [P, 1, 512])
        ps_z = n.ps("ps_z", [P, 2, 512])
        ps_a = n.ps("ps_a", [P, 2, 512])
        ps_in = n.ps("ps_in", [P, 512])
        ps_y = n.ps("ps_y", [P, 512])
        ps_x = n.ps("ps_x", [P, 512])

        loaded, loaded_later = n.sem("loaded"), n.sem("loaded_later")
        x_loaded = n.sem("x_loaded")
        sums_ready, hid_turned, hid_copied = n.sem("sums_ready"), n.sem("hid_turned"), n.sem("hid_copied")
        in_summed, in_copied = n.sem("in_summed"), n.sem("in_copied")
        eps_set = n.sem("eps_set")
        z_summed, z_read = n.sem("z_summed"), n.sem("z_read")
        z_ready, z_turned, act_ready = n.sem("z_ready"), n.sem("z_turned"), n.sem("act_ready")
        var_ready, std_ready = n.sem("var_ready"), n.sem("std_ready")
        y_summed, y_read = n.sem("y_summed"), n.sem("y_read")
        x1_ready, x1_turned, x1_stored = n.sem("x1_ready"), n.sem("x1_turned"), n.sem("x1_stored")
        dve = n.sem("dve")
        turns_v = n.sem("turns_v")
        load_first, load_rest, scatter_records = record_scatter(n, dram, TILES_SUM, NET_STEP, NET_STEPS)
        block = s.enter_context(nc.Block())
        LOADS, LATER_LOADS = 8, 5

        @block.sync
        def _(sp):
            load_first(sp)
            sp.dma_start(w_ee[:], a["ee_w2"].rearrange("(c p) n -> p c n", p=P)).then_inc(loaded, 16)
            sp.dma_start(w1[:], a["w1"].rearrange("(c p) n -> p c n", p=P)).then_inc(loaded, 16)
            sp.dma_start(bias[:, 0, :], row(a["b1"])).then_inc(loaded, 16)
            sp.dma_start(bias[:, 1, :], row(a["b2"])).then_inc(loaded, 16)
            for k, (g, be) in enumerate((("g1", "be1"), ("g2", "be2"))):
                sp.dma_start(gain[:, k, :], a[g]).then_inc(loaded, 16)
                sp.dma_start(shift[:, k, :], a[be]).then_inc(loaded, 16)
            sp.dma_start(w2[:], a["w2"].rearrange("(c p) n -> p c n", p=P)).then_inc(loaded_later, 16)
            sp.dma_start(w3[:], a["w3"].rearrange("(c p) n -> p c n", p=P)).then_inc(loaded_later, 16)
            sp.dma_start(bias3[:], row(a["b3"])).then_inc(loaded_later, 16)
            sp.dma_start(bn_g[:], row(a["bn_g"])).then_inc(loaded_later, 16)
            sp.dma_start(bn_b[:], row(a["bn_b"])).then_inc(loaded_later, 16)
            load_rest(sp)

        @block.gpsimd
        def _(pool):
            scatter_records(pool)

        @block.tensor
        def _(pe):
            def network_input(b):
                pe.wait_ge(sums_ready, b + 1)
                for c in range(CC):
                    mm = nc.tensor.transpose(ps_t[:, 0, c * P:(c + 1) * P], sums[:, C + c * P:C + (c + 1) * P], ident[:])
                mm.then_inc(hid_turned, 1)
                pe.wait_ge(hid_copied, b + 1)
                for c in range(CC):
                    target = ps_in[:, c * P:(c + 1) * P]
                    nc.tensor.matmul(target, sums[:, c * P:(c + 1) * P], ident[:], start=c == 0, stop=False,
                                     skip_group_check=True)
                    for k in range(CC):
                        mm = nc.tensor.matmul(target, w_ee[:, k, c * P:(c + 1) * P], hid_t[:, k, :], start=False,
                                              stop=k == CC - 1, skip_group_check=True)
                mm.then_inc(in_summed, 1)

            def hidden_layer(b, layer):
                pe.wait_ge(z_read, b * 2 + layer + 1)
                if layer == 0:
                    pe.wait_ge(in_copied, b + 1)
                    chunks, w = [in_t[:, c, :] for c in range(CC)], w1
                else:
                    chunks, w = [act_t[:, 0, c, :] for c in range(HC)], w2
                for m in range(2):
                    for c, x in enumerate(chunks):
                        if layer == 1 and m == 0:
                            pe.wait_ge(act_ready, b * 2 * HC + HC // 2 + c + 2)
                        mm = nc.tensor.matmul(ps_z[:, m, :], x, w[:, c, m * 512:(m + 1) * 512], start=c == 0,
                                              stop=c == len(chunks) - 1)
                    mm.then_inc(z_summed, 1)

            def turn_hidden(b, layer):
                pe.wait_ge(z_ready, b * 2 + layer + 1)
                for m in range(2):
                    pe.wait_ge(act_ready, (b * 2 + layer) * HC + m * (HC // 2) + 1)
                    for c in range(HC // 2):
                        k = m * (HC // 2) + c
                        mm = nc.tensor.transpose(ps_a[:, m, c * P:(c + 1) * P], z[:, k * P:(k + 1) * P], ident[:])
                    mm.then_inc(z_turned, 1)

            def output_layer(b):
                pe.wait_ge(y_read, b + 1)
                for c in range(HC):
                    pe.wait_ge(act_ready, b * 2 * HC + HC + HC // 2 + c + 2)
                    mm = nc.tensor.matmul(ps_y[:, 0:C], act_t[:, 1, c, :], w3[:, c, :], start=c == 0, stop=c == HC - 1)
                mm.then_inc(y_summed, 1)

            def turn_x1(b):
                pe.wait_ge(x1_ready, b + 1)
                pe.wait_ge(x1_stored, b + 1)
                for c in range(CC):
                    mm = nc.tensor.transpose(ps_x[:, c * P:(c + 1) * P], x1[:, c * P:(c + 1) * P], ident[:])
                mm.then_inc(x1_turned, 1)

            def body(b, first=False, last=False):
                turn_hidden(b, 0)
                hidden_layer(b, 1)
                if not first:
                    turn_x1(b - 1)
                if not last:
                    network_input(b + 1)
                turn_hidden(b, 1)
                if not last:
                    hidden_layer(b + 1, 0)
                output_layer(b)

            pe.wait_ge(loaded, 16 * LOADS)
            network_input(0)
            hidden_layer(0, 0)
            pe.wait_ge(loaded_later, 16 * LATER_LOADS)
            body(0, first=True)
            with pe.Fori(1, NB - 1) as b:
                body(b)
            body(NB - 1, last=True)
            turn_x1(NB - 1)

        @block.scalar
        def _(act):
            act.preload_act_table(ACT.Sqrt)
            act.sem_inc(act_ready, HC // 2 + 1)
            act.sem_inc(x1_stored, 1)
            act.wait_ge(loaded, 16 * LOADS)

            def copy_sums(b):
                nc.scalar.activation(sums[:], acc[:, bass.ds(b, 1), :].rearrange("p b c -> p (b c)"),
                                     ACT.Copy).then_inc(sums_ready, 1)

            def copy_input(b):
                act.wait_ge(hid_turned, b + 1)
                nc.scalar.activation(hid_t[:].rearrange("p c n -> p (c n)"), ps_t[:, 0, 0:C], ACT.Copy
                                     ).then_inc(hid_copied, 1)
                act.wait_ge(in_summed, b + 1)
                nc.scalar.activation(in_t[:].rearrange("p c n -> p (c n)"), ps_in[:, 0:C], ACT.Copy
                                     ).then_inc(in_copied, 1)

            def activate(b, layer):
                for c in range(HC):
                    if c % (HC // 2) == 0:
                        act.wait_ge(z_turned, (b * 2 + layer) * 2 + c // (HC // 2) + 1)
                    nc.scalar.activation(act_t[:, layer, c, :],
                                         ps_a[:, c // (HC // 2), (c % (HC // 2)) * P:(c % (HC // 2) + 1) * P], ACT.Relu,
                                         bias=shift[:, layer, c:c + 1], scale=gain[:, layer, c:c + 1]
                                         ).then_inc(act_ready, 1)

            def load_x(b):
                act.dma_start(x_in[:], a["x"].rearrange("(b p) c -> p b c", p=P)[:, bass.ds(b, 1), :]
                              .rearrange("p b c -> p (b c)")).then_inc(x_loaded, 16)

            def root(number):
                act.wait_ge(var_ready, number + 1)
                nc.scalar.activation(std[:], mv[:, 1:2], ACT.Sqrt, bias=eps[:, 0:1]).then_inc(std_ready, 1)

            def store_x1(b):
                act.wait_ge(x1_turned, b + 1)
                nc.scalar.activation(acc[:, bass.ds(b, 1), C:2 * C].rearrange("p b c -> p (b c)"), ps_x[:, 0:C],
                                     ACT.Copy).then_inc(x1_stored, 1)

            def body(b, first=False, last=False):
                activate(b, 0)
                if not last:
                    act.wait_ge(in_summed, b + 1)
                    copy_sums(b + 1)
                if not first:
                    root(b * 4 - 1)
                    root(b * 4)
                    store_x1(b - 1)
                    load_x(b)
                if not last:
                    copy_input(b + 1)
                root(b * 4 + 1)
                activate(b, 1)
                if not last:
                    root(b * 4 + 2)

            load_x(0)
            copy_sums(0)
            copy_input(0)
            act.wait_ge(eps_set, 1)
            root(0)
            body(0, first=True)
            with act.Fori(1, NB - 1) as b:
                body(b)
            body(NB - 1, last=True)
            root(NB * 4 - 2)
            root(NB * 4 - 1)
            store_x1(NB - 1)

        @block.vector
        def _(v):
            chain = Chain(v, dve)
            v.sem_inc(z_read, 1)
            v.sem_inc(y_read, 1)
            v.memset(eps[:], LN_EPS).then_inc(eps_set, 1)
            v.wait_ge(loaded, 16 * LOADS)

            def normed(out_, in_, number):
                halves = -(-in_.shape[1] // 512)
                w = in_.shape[1] // halves
                for m in range(halves):
                    ins = v.bn_stats(stats[:, m, :], in_[:, m * w:(m + 1) * w])
                chain.then(ins)
                v.sem_inc(turns_v, 1)
                chain.then(v.bn_aggr(mv[:], stats[:, 0:halves, :].rearrange("p m s -> p (m s)")))
                v.sem_inc(var_ready, 1)
                v.wait_ge(std_ready, number + 1)
                chain.then(v.reciprocal(rstd[:], std[:]))
                return v.tensor_scalar(out_, in_, mv[:, 0:1], rstd[:, 0:1], ALU.subtract, ALU.mult)

            def hidden(b, layer):
                number = b * 2 + layer
                for m in range(2):
                    v.wait_ge(z_summed, number * 2 + m + 1)
                    ins = v.tensor_tensor(z[:, m * 512:(m + 1) * 512], ps_z[:, m, :],
                                          bias[:, layer, m * 512:(m + 1) * 512], ALU.add)
                ins.then_inc(z_read, 1)
                v.wait_ge(z_read, number + 2)
                normed(z[:], z[:], b * 4 + 1 if layer else b * 4 - 2 if not isinstance(b, int) or b else 0
                       ).then_inc(z_ready, 1)

            def output(b, last):
                v.wait_ge(y_summed, b + 1)
                v.tensor_tensor(y[:], ps_y[:, 0:C], bias3[:], ALU.add).then_inc(y_read, 1)
                v.wait_ge(y_read, b + 2)
                v.wait_ge(x_loaded, b * 16 + 16)
                chain.then(v.tensor_tensor(y[:], y[:], x_in[:], ALU.add))
                at = b * 4 + 3 - last
                chain.then(normed(y[:], y[:], at))
                chain.then(v.tensor_tensor(y[:], y[:], bn_g[:], ALU.mult))
                chain.then(v.tensor_tensor(y[:], y[:], bn_b[:], ALU.add))
                chain.then(v.scalar_tensor_tensor(out=y[:], in0=y[:], scalar=0.0, in1=x_in[:], op0=ALU.max, op1=ALU.add))
                normed(x1[:], y[:], at + 1).then_inc(x1_ready, 1)
                v.wait_ge(x1_ready, b + 1)
                v.tensor_copy(acc[:, bass.ds(b, 1), 0:C].rearrange("p b c -> p (b c)"), x1[:])

            def body(b, last=False):
                hidden(b, 1)
                if not last:
                    hidden(b + 1, 0)
                output(b, last)

            hidden(0, 0)
            v.wait_ge(loaded_later, 16 * LATER_LOADS)
            body(0)
            with chain.loop(v, 1, NB - 1, 17) as b:
                body(b)
            body(NB - 1, last=True)


def make_tables(nc, a, dram, t):
    acc = t["acc"]
    with ExitStack() as s:
        n = Names(nc, "tab", s)
        w_io = n.sb("w_io", [P, CC, 2 * C])
        bias = n.sb("bias", [P, 2 * C])
        gamma, beta = n.sb("gamma", [P, CC]), n.sb("beta", [P, CC])
        stats = n.sb("stats", [P, CC, NB, 6])
        mv = n.sb("mv", [P, CC, 2])
        scale, shift = n.sb("scale", [P, CC]), n.sb("shift", [P, CC])
        B = 4
        assert NB % B == 1 and NB % 6 == 1
        h_t = n.sb("h_t", [P, B, CC, P])
        feat = n.sb("feat", [P, B, 2 * C])
        ps = n.ps("ps", [P, B, 2 * C])
        loaded, x1_saved, dve, stats_done = n.sem("loaded"), n.sem("x1_saved"), n.sem("dve"), n.sem("stats_done")
        h_ready, summed, feat_ready = n.sem("h_ready"), n.sem("summed"), n.sem("feat_ready")
        var_ready, std_ready = n.sem("var_ready"), n.sem("std_ready")
        stored = [n.sem(f"stored{k}") for k in range(B)]
        load_first, load_rest, scatter_records = record_scatter(n, dram, TILES_SUM + TILES_NET, TAB_STEP, TAB_STEPS)
        block = s.enter_context(nc.Block())
        LD = 6

        def blocks(eng, body):
            for k in range(B):
                body(k, k, 0)
            with eng.Fori(1, NB // B) as i:
                for k in range(B):
                    body(i * B + k, k, i)
            body(NB - 1, 0, NB // B)

        @block.sync
        def _(sp):
            sp.dma_start(w_io[:, :, 0:C], a["W_in"].rearrange("(c p) n -> p c n", p=P)).then_inc(loaded, 16)
            sp.dma_start(w_io[:, :, C:2 * C], a["W_out"].rearrange("(c p) n -> p c n", p=P)).then_inc(loaded, 16)
            sp.dma_start(bias[:, 0:C], row(a["b_in"])).then_inc(loaded, 16)
            sp.dma_start(bias[:, C:2 * C], row(a["b_out"])).then_inc(loaded, 16)
            sp.dma_start(gamma[:], a["gamma"]).then_inc(loaded, 16)
            sp.dma_start(beta[:], a["beta"]).then_inc(loaded, 16)
            sp.dma_start(dram["x1"].rearrange("p (b c) -> p b c", c=C), acc[:, :, 0:C]).then_inc(x1_saved, 16)

            def store(b, k, i):
                sp.wait_ge(h_ready, b + 1)
                sp.dma_start(dram["hT"][:, bass.ds(b * C, C)], h_t[:, k].rearrange("p c n -> p (c n)")
                             ).then_inc(stored[k], 16)
                sp.wait_ge(feat_ready, b + 1)
                for part, name in enumerate(("feat_in", "feat_out")):
                    sp.dma_start(dram[name].rearrange("(b p) c -> p b c", p=P)[:, bass.ds(b, 1), :]
                                 .rearrange("p b c -> p (b c)"), feat[:, k, part * C:(part + 1) * C]
                                 ).then_inc(stored[k], 16)

            blocks(sp, store)
            for k in range(B):
                sp.wait_ge(stored[k], (NB // B + (k == 0)) * 48)
            sp.wait_ge(x1_saved, 16)

        @block.gpsimd
        def _(pool):
            nc.gpsimd.iota(t["iota"][:], pattern=[[1, NP]], base=0, channel_multiplier=0,
                           allow_small_or_imprecise_dtypes=True)
            scatter_records(pool)

        @block.tensor
        def _(pe):
            pe.wait_ge(loaded, 16 * LD)

            def multiply(b, k, i):
                pe.wait_ge(h_ready, b + 1)
                for c in range(CC):
                    mm = nc.tensor.matmul(ps[:, k, :], h_t[:, k, c, :], w_io[:, c, :], start=c == 0, stop=c == CC - 1)
                mm.then_inc(summed, 1)

            blocks(pe, multiply)

        @block.scalar
        def _(act):
            load_first(act)
            act.wait_ge(var_ready, 1)
            nc.scalar.activation(shift[:], scale[:], ACT.Sqrt).then_inc(std_ready, 1)
            load_rest(act)

        @block.vector
        def _(v):
            chain = Chain(v, dve)
            with v.Fori(0, NB // 6) as i:
                for k in range(6):
                    b = i * 6 + k
                    for c in range(CC):
                        v.bn_stats(stats[:, c, bass.ds(b, 1), :].rearrange("p b s -> p (b s)"),
                                   acc[:, bass.ds(b, 1), C + c * P:C + (c + 1) * P].rearrange("p b c -> p (b c)")
                                   ).then_inc(stats_done, 1)
            for c in range(CC):
                v.bn_stats(stats[:, c, NB - 1, :], acc[:, NB - 1, C + c * P:C + c * P + LAST]).then_inc(stats_done, 1)
            v.wait_ge(stats_done, CC * NB)
            v.wait_ge(loaded, 16 * LD)
            for c in range(CC):
                ins = v.bn_aggr(mv[:, c, :], stats[:, c, :, :].rearrange("p b s -> p (b s)"))
            chain.then(ins)
            chain.then(v.tensor_scalar(scale[:], mv[:, :, 1], LN_EPS, None, ALU.add))
            v.sem_inc(var_ready, 1)
            v.wait_ge(std_ready, 1)
            chain.then(v.reciprocal(scale[:], shift[:]))
            chain.then(v.tensor_tensor(scale[:], scale[:], gamma[:], ALU.mult))
            chain.then(v.tensor_tensor(shift[:], scale[:], mv[:, :, 0], ALU.mult))
            chain.then(v.tensor_tensor(shift[:], beta[:], shift[:], ALU.subtract))

            def make_h(b, k, i):
                if not isinstance(i, int) or i:
                    v.wait_ge(stored[k], i * 48)
                for c in range(CC):
                    ins = v.tensor_scalar(h_t[:, k, c, :],
                                          acc[:, bass.ds(b, 1), C + c * P:C + (c + 1) * P].rearrange("p b c -> p (b c)"),
                                          scale[:, c:c + 1], shift[:, c:c + 1], ALU.mult, ALU.add)
                ins.then_inc(h_ready, 1)

            def table(b, k, i):
                if not isinstance(b, int) or b < NB - 1:
                    make_h(b + 1, (k + 1) % B, i + (k + 1) // B)
                v.wait_ge(summed, b + 1)
                v.tensor_tensor(feat[:, k, :], ps[:, k, :], bias[:], ALU.add).then_inc(feat_ready, 1)

            make_h(0, 0, 0)
            blocks(v, table)
            v.wait_ge(x1_saved, 16)
            v.wait_ge(feat_ready, NB)
            v.memset(acc[:].rearrange("p b c -> p (b c)"), 0.0)


def sum_over_src_and_gates(nc, a, dram, t, out):
    acc, bucket, ident, iota = t["acc"], t["sorted_bucket"], t["ident"], t["iota"]
    KC = 2 * CC
    with ExitStack() as s:
        n = Names(nc, "sum3", s)
        record = n.sb("record", [P, U, T, 4])
        rows = n.sb("rows", [P, U, T, C])
        onehot = n.sb("onehot", [P, 2, T, P])
        w_x = n.sb("w_x", [P, KC, 2 * C])
        w_h = n.sb("w_h", [P, CC, 2 * C])
        bias = n.sb("bias", [P, 2 * C])
        x1 = n.sb("x1", [P, C])
        h_t = n.sb("h_t", [P, CC, P])
        sums = n.sb("sums", [P, 2 * C])
        sums_t = n.sb("sums_t", [P, KC, P])
        pre = n.sb("pre", [P, 2 * C])
        gate = n.sb("gate", [P, 2 * C])
        y = n.sb("y", [P, C])
        stats, mv, eps = n.sb("stats", [P, 6]), n.sb("mv", [P, 2]), n.sb("eps", [P, 1])
        std, rstd = n.sb("std", [P, 1]), n.sb("rstd", [P, 1])
        result = n.sb("result", [P, C])
        ps = n.ps("ps", [P, 2, 2, 512])
        ps_t = n.ps("ps_t", [P, 512])
        ps_h = n.ps("ps_h", [P, 512])
        ps_g = n.ps("ps_g", [P, 512])
        loaded = [n.sem(f"loaded{u}") for u in range(U)]
        gathered = [n.sem(f"gathered{u}") for u in range(U)]
        turns, turns_v, turns_sp = n.sem("turns"), n.sem("turns_v"), n.sem("turns_sp")
        onehot_ready, summed, added = n.sem("onehot_ready"), n.sem("summed"), n.sem("added")
        group_done = n.sem("group_done")
        eps_set, weights = n.sem("eps_set"), n.sem("weights")
        in_loaded, stored = n.sem("in_loaded"), n.sem("stored")
        sums_ready, turned, sums_t_ready = n.sem("sums_ready"), n.sem("turned"), n.sem("sums_t_ready")
        multiplied, pre_ready, gates_ready = n.sem("multiplied"), n.sem("pre_ready"), n.sem("gates_ready")
        mixed, var_ready, std_ready = n.sem("mixed"), n.sem("var_ready"), n.sem("std_ready")
        done, dve = n.sem("done"), n.sem("dve")
        block = s.enter_context(nc.Block())
        records = dram["sorted_record"].rearrange("(g h p j) w -> p g h (j w)", h=2, p=P, j=T // 2)

        def due_blocks(eng, gates):
            next_block = eng.alloc_register("next_block")
            eng.reg_mov(next_block, 0)

            def due(g, limit, q):
                with eng.If(eng.snap(next_block, min_val=0, max_val=NB - 1) < limit):
                    gates[q](eng.snap(next_block, min_val=0, max_val=NB - 2), g)
                    if q == len(gates) - 1:
                        eng.reg_add(next_block, next_block, 1)

            def rest():
                with eng.Fori(eng.snap(next_block, min_val=0, max_val=NB - 1), NB) as b:
                    for part in gates:
                        part(b, SG)

            return due, rest

        def first_bucket(eng, g):
            return eng.value_load(bucket[0:1, bass.ds(g * 2, 1)], min_val=0, max_val=NB - 1)

        @block.sync
        def _(sp):

            def load(g, u, source, times):
                if not isinstance(times, int) or times:
                    sp.wait_ge(gathered[u], times * (16 * T))
                    sp.sem_inc(turns_sp, 1)
                    sp.wait_ge(onehot_ready, g - U + 1)
                sp.dma_start(record[:, u].rearrange("p (h j) w -> p h (j w)", h=2),
                             records[:, bass.ds(source, 1), :, :].rearrange("p g h w -> p (g h) w")
                             ).then_inc(loaded[u], 16)

            for u in range(U):
                load(u, u, u, 0)
            sp.dma_start(w_x[:], a["W_x2i"].rearrange("(c p) n -> p c n", p=P)).then_inc(weights, 16)
            sp.dma_start(w_h[:], a["W_h2h"].rearrange("(c p) n -> p c n", p=P)).then_inc(weights, 16)
            sp.dma_start(bias[:], row(a["b_x2i"])).then_inc(weights, 16)
            with sp.Fori(1, SG // U) as i:
                for u in range(U):
                    load(i * U + u, u, i * U + u, i)
            load(SG, 0, 0, SG // U)
            sp.wait_ge(loaded[0], (SG // U + 1) * 16)

        @block.gpsimd
        def _(pool):
            with pool.Fori(0, SG // U) as i:
                for u in range(U):
                    pool.wait_ge(loaded[u], i * 16 + 16)
                    pool.wait_ge(group_done, i * U + u + 1)
                    pool.sem_inc(turns, 1)
                    for j in range(T):
                        pool.indirect_dma_start(
                            out=rows[:, u, j, :], out_offset=None, in_=dram["feat_out"],
                            in_offset=bass.IndirectOffsetOnAxis(ap=record[:, u, j, 0:1].bitcast(I32), axis=0),
                        ).then_inc(gathered[u], 16)

        @block.tensor
        def _(pe):
            def turn(b, groups):
                pe.wait_ge(weights, 48)
                pe.wait_ge(in_loaded, b * 32 + 32)
                pe.wait_ge(mixed, b + 1)
                for c in range(CC):
                    nc.tensor.transpose(ps_h[:, c * P:(c + 1) * P], h_t[:, c, :], ident[:])
                for c in range(CC):
                    nc.tensor.matmul(ps_g[:], h_t[:, c, :], w_h[:, c, :], start=c == 0, stop=False)
                pe.wait_ge(sums_ready, b + 1)
                for c in range(KC):
                    mm = nc.tensor.transpose(ps_t[:, c * P:(c + 1) * P], sums[:, c * P:(c + 1) * P], ident[:])
                mm.then_inc(turned, 1)

            def multiply(b, groups):
                pe.wait_ge(sums_t_ready, b + 1)
                for c in range(KC):
                    mm = nc.tensor.matmul(ps_g[:], sums_t[:, c, :], w_x[:, c, :], start=False, stop=c == KC - 1)
                mm.then_inc(multiplied, 1)

            due, rest = due_blocks(pe, (turn, multiply))
            with pe.Fori(0, SG // U) as i:
                for u in range(U):
                    g = i * U + u
                    limit = first_bucket(pe, g)
                    due(g, limit, 0)
                    pe.wait_ge(gathered[u], i * 16 * T + 16 * T)
                    pe.wait_ge(onehot_ready, g + 1)
                    pe.wait_ge(added, g * 2 + 2)
                    for j in range(T):
                        mm = nc.tensor.matmul(ps[:, u % 2, j // 2, 0:C], onehot[:, u % 2, j, :], rows[:, u, j, :],
                                              start=j % 2 == 0, stop=j % 2 == 1)
                        if j % 2:
                            mm.then_inc(summed, 1)
                    due(g, limit, 1)
            rest()

        @block.scalar
        def _(act):
            act.wait_ge(eps_set, 1)

            def activate(b, groups):
                act.wait_ge(mixed, b + 1)
                act.dma_start(x1[:], dram["x1"][:, bass.ds(b * C, C)]).then_inc(in_loaded, 16)
                act.dma_start(h_t[:].rearrange("p c n -> p (c n)"), dram["hT"][:, bass.ds(b * C, C)]
                              ).then_inc(in_loaded, 16)
                act.wait_ge(added, groups * 2 + 4)
                nc.scalar.activation(sums[:], acc[:, bass.ds(b, 1), :].rearrange("p b c -> p (b c)"), ACT.Copy
                                     ).then_inc(sums_ready, 1)
                act.wait_ge(turned, b + 1)
                nc.scalar.activation(sums_t[:].rearrange("p c n -> p (c n)"), ps_t[:], ACT.Copy
                                     ).then_inc(sums_t_ready, 1)
                act.wait_ge(pre_ready, b + 1)
                nc.scalar.activation(gate[:, 0:C], pre[:, 0:C], ACT.Sigmoid)
                nc.scalar.activation(gate[:, C:2 * C], pre[:, C:2 * C], ACT.Tanh).then_inc(gates_ready, 1)
                act.wait_ge(var_ready, b + 1)
                nc.scalar.activation(std[:], mv[:, 1:2], ACT.Sqrt, bias=eps[:, 0:1]).then_inc(std_ready, 1)
                act.wait_ge(done, b + 1)
                act.dma_start(out.rearrange("(b p) c -> p b c", p=P)[:, bass.ds(b, 1), :]
                              .rearrange("p b c -> p (b c)"), result[:]).then_inc(stored, 16)
                act.wait_ge(stored, b * 16 + 16)

            due, rest = due_blocks(act, (activate,))
            with act.Fori(0, SG) as g:
                due(g, first_bucket(act, g), 0)
            rest()

        @block.vector
        def _(v):
            v.sem_inc(group_done, U)
            v.sem_inc(added, 4)
            v.sem_inc(mixed, 1)
            v.memset(eps[:], LN_EPS).then_inc(eps_set, 1)
            chain = Chain(v, dve)
            MIX_STEPS = 7

            def one_hots(g, u, count):
                v.wait_ge(loaded[u], count * 16)
                for j in range(T):
                    if j % 2 == 0:
                        b = v.value_load(bucket[0:1, bass.ds(g * 2 + j // 2, 1)], min_val=0, max_val=NB - 1)
                        v.reg_mov(next_bucket[j // 2], b)
                    ins = v.tensor_scalar(onehot[:, u % 2, j, :], iota[:, bass.ds(b * P, P)], record[:, u, j, 1:2],
                                          record[:, u, j, 2:3], ALU.is_equal, ALU.mult)
                ins.then_inc(onehot_ready, 1)

            def mix(b, groups):
                chain.at(b * MIX_STEPS)
                v.wait_ge(weights, 48)
                v.wait_ge(multiplied, b + 1)
                v.tensor_tensor(pre[:], ps_g[:], bias[:], ALU.add).then_inc(pre_ready, 1)
                v.wait_ge(gates_ready, b + 1)
                new = gate[:, C:2 * C]
                chain.then(v.tensor_tensor(y[:], ps_h[:, 0:C], new, ALU.subtract))
                chain.then(v.tensor_tensor(y[:], y[:], gate[:, 0:C], ALU.mult))
                chain.then(v.tensor_tensor(y[:], y[:], new, ALU.add))
                chain.then(v.tensor_tensor(y[:], y[:], x1[:], ALU.add))
                v.sem_inc(mixed, 1)
                chain.then(v.bn_stats(stats[:], y[:]))
                v.sem_inc(turns_v, 1)
                chain.then(v.bn_aggr(mv[:], stats[:]))
                v.sem_inc(var_ready, 1)
                v.wait_ge(std_ready, b + 1)
                chain.then(v.reciprocal(rstd[:], std[:]))
                v.tensor_scalar(result[:], y[:], mv[:, 0:1], rstd[:, 0:1], ALU.subtract, ALU.mult).then_inc(done, 1)
                assert chain.steps == MIX_STEPS

            last_bucket = v.alloc_register("last_bucket")
            this_bucket = [v.alloc_register(f"this_bucket{h}") for h in range(2)]
            next_bucket = [v.alloc_register(f"next_bucket{h}") for h in range(2)]
            one_hots(0, 0, 1)
            v.reg_mov(this_bucket[0], 0)
            due, rest = due_blocks(v, (mix,))
            with v.Fori(0, SG // U) as i:
                for u in range(U):
                    g = i * U + u
                    v.reg_mov(last_bucket, this_bucket[0])
                    for h in range(2):
                        v.reg_mov(this_bucket[h], next_bucket[h])
                    one_hots(g + 1, (u + 1) % U, i + 1 + (u + 1) // U)
                    due(g, v.snap(last_bucket, min_val=0, max_val=NB - 1), 0)
                    for h in range(2):
                        b = v.snap(this_bucket[h], min_val=0, max_val=NB - 1)
                        v.wait_ge(summed, g * 2 + h + 1)
                        v.wait_ge(added, g * 2 + h + 4)
                        sums_b = acc[:, bass.ds(b, 1), C:2 * C].rearrange("p b c -> p (b c)")
                        v.tensor_tensor(sums_b, sums_b, ps[:, u % 2, h, 0:C], ALU.add).then_inc(added, 1)
                    v.sem_inc(group_done, 1)
            rest()


def kernel(**inputs):
    import numpy as np
    import concourse.bacc as bacc
    from concourse.bass_utils import run_bass_kernel_spmd as run

    arrays = layout(np, inputs)
    nc = bacc.Bacc("TRN2", target_bir_lowering=False, num_devices=1)
    a = {k: nc.dram_tensor(f"in_{k}", v.shape, mybir.dt.from_np(v.dtype), kind="ExternalInput").ap()
         for k, v in arrays.items()}
    out = nc.dram_tensor("out_0", (NP, C), F32, kind="ExternalOutput").ap()
    gnn_kernel(nc, a, out)
    r = run(nc, [{f"in_{k}": v for k, v in arrays.items()}], core_ids=[0])
    return r.results[0]["out_0"][:NODES]


def layout(np, inputs):
    def pad(v, n, fill):
        return np.concatenate([v, np.full((n - v.shape[0],) + v.shape[1:], fill, v.dtype)])

    def by_partition(v):
        return np.ascontiguousarray(v.reshape(NG, P, T).transpose(1, 0, 2).reshape(P, NT))

    given = {k: np.asarray(v) for k, v in inputs.items()}
    arrays = {
        "x": pad(given["x"], NP, 0),
        "src": by_partition(pad(given["src"], EP, NODES)),
        "dst": by_partition(pad(given["dst"], EP, NODES)),
        "iw": by_partition(pad(given["edge_weight"], EP, 0)),
        "ow": by_partition(pad(given["edge_weight_n2"], EP, 0)),
        "edge_attr": np.ascontiguousarray(
            pad(given["edge_attr_64"], (NG + 1) * GE, 0).reshape(NG + 1, P, T, EC).transpose(3, 0, 2, 1)
            .reshape(EC, (NG + 1) * GE)),
        "eps": given["L0_gnn_eps"].reshape(1),
    }
    for k in ("ee_w1", "ee_b1", "ee_w2", "ee_b2", "w1", "b1", "g1", "be1", "w2", "b2", "g2", "be2", "w3", "b3",
              "bn_g", "bn_b"):
        arrays[k] = given["L0_gnn_" + k]
    for k in ("gamma", "beta", "W_in", "b_in", "W_out", "b_out", "W_x2i", "b_x2i", "W_h2h"):
        arrays[k] = given["L1_gnn_" + k]
    for k in ("g1", "be1", "g2", "be2", "gamma", "beta"):
        arrays[k] = np.ascontiguousarray(arrays[k].reshape(-1, P).T)
    return arrays
```
